# Optimizing a Trainium2 kernel written in Bass

```python
import numpy as np
import jax
import jax.numpy as jnp

def _softmax(x, axis=-1):
    return jax.nn.softmax(x, axis=axis)

def _gelu(x):
    return jax.nn.gelu(x, approximate=True)

def _silu(x):
    return jax.nn.silu(x)

def _sigmoid(x):
    return jax.nn.sigmoid(x)

def _layernorm(x, axis=-1, eps=1e-05):
    m = jnp.mean(x, axis=axis, keepdims=True)
    v = jnp.var(x, axis=axis, keepdims=True)
    return (x - m) / jnp.sqrt(v + eps)

def _scatter_add(tgt, idx, src, axis=0):
    return tgt.at[idx].add(src)

def _segment_sum(src, seg, n):
    return jax.ops.segment_sum(src, seg, n)
kernel_name = 'mk_seq_preln_d4_jaxref_r8_83fd7d'

def setup_inputs(seed: int=0):
    np.random.seed(seed)
    _w = jnp.asarray

    def _L0_attn_setup():
        import jax, jax.numpy as jnp
        import numpy as np
        D_MODEL = 128
        N_HEADS = 16
        HEAD_DIM = D_MODEL // N_HEADS
        WINDOW = 128
        LOCAL_BLOCK = 32
        LATENT_TOKENS = 64
        LATENT_D = 32
        LATENT_HEADS = 4
        LATENT_HD = LATENT_D // LATENT_HEADS
        NEG = -1000000000.0

        def _local_attention(q, k, v):
            B, H, S, hd = q.shape
            bs = min(S, max(WINDOW, LOCAL_BLOCK))
            nb = S // bs
            w = WINDOW
            L = bs + w - 1
            k_pad = jnp.pad(k, ((0, 0), (0, 0), (w - 1, 0), (0, 0)))
            v_pad = jnp.pad(v, ((0, 0), (0, 0), (w - 1, 0), (0, 0)))
            starts = jnp.arange(nb) * bs
            idx = starts[:, None] + jnp.arange(L)[None, :]
            kb = k_pad[:, :, idx]
            vb = v_pad[:, :, idx]
            qb = q.reshape(B, H, nb, bs, hd)
            q_pos = starts[:, None] + jnp.arange(bs)[None, :]
            k_gpos = starts[:, None] + jnp.arange(L)[None, :] - (w - 1)
            dist = q_pos[:, :, None] - k_gpos[:, None, :]
            allowed = (dist > 0) & (dist <= w) & (k_gpos[:, None, :] >= 0)
            scale = 1.0 / np.sqrt(hd)
            scores = jnp.einsum('bhnqd,bhnkd->bhnqk', qb, kb) * scale
            scores = jnp.where(allowed, scores, NEG)
            attn = jax.nn.softmax(scores, axis=-1)
            attn = jnp.where(allowed.any(-1)[None, None, :, :, None], attn, 0.0)
            out = jnp.einsum('bhnqk,bhnkd->bhnqd', attn, vb)
            return out.reshape(B, H, S, hd)
        key = jax.random.key(seed)
        ks = jax.random.split(key, 14)
        B, S = (2, 512)
        s = 0.02
        f32 = jnp.float32
        return {'x': jax.random.normal(ks[0], (B, S, D_MODEL), f32), 'qkv_w': jax.random.normal(ks[1], (D_MODEL, 3 * D_MODEL), f32) * s, 'qkv_b': jnp.zeros((3 * D_MODEL,), f32), 'rq_w': jax.random.normal(ks[2], (D_MODEL, LATENT_D), f32) * s, 'rq_b': jnp.zeros((LATENT_D,), f32), 'rkv_w': jax.random.normal(ks[3], (D_MODEL, 2 * LATENT_D), f32) * s, 'rkv_b': jnp.zeros((2 * LATENT_D,), f32), 'rout_w': jax.random.normal(ks[4], (LATENT_D, D_MODEL), f32) * s, 'rout_b': jnp.zeros((D_MODEL,), f32), 'out_w': jax.random.normal(ks[5], (D_MODEL, D_MODEL), f32) * s, 'out_b': jnp.zeros((D_MODEL,), f32), 'gl_w': jax.random.normal(ks[6], (HEAD_DIM, 1), f32) * s, 'gr_w': jax.random.normal(ks[7], (HEAD_DIM, 1), f32) * s}
    _L0_attn_in = _L0_attn_setup()

    def _L0_ffn_setup():
        import jax, jax.numpy as jnp
        import numpy as np
        BLOCK = 16
        _GRID = jnp.array([0.0, 0.5, 1.0, 1.5, 2.0, 3.0, 4.0, 6.0], dtype=jnp.float32)
        _MID = jnp.array([0.25, 0.75, 1.25, 1.75, 2.5, 3.5, 5.0], dtype=jnp.float32)

        def fp4_quant_dequant(x):
            shape = x.shape
            xb = x.reshape(shape[:-1] + (shape[-1] // BLOCK, BLOCK))
            scale = jnp.max(jnp.abs(xb), axis=-1, keepdims=True) / 6.0
            scale = jnp.maximum(scale, jnp.float32(1e-12))
            xn = xb / scale
            idx = jnp.searchsorted(_MID, jnp.abs(xn))
            q = _GRID[idx] * jnp.sign(xn) * scale
            return q.reshape(shape)

        def fp4_linear(x, w):
            xq = fp4_quant_dequant(x)
            wq = fp4_quant_dequant(w)
            return jnp.einsum('bsk,nk->bsn', xq, wq)
        key = jax.random.key(seed)
        k1, k2, k3, k4 = jax.random.split(key, 4)
        H, I = (128, 352)
        x = jax.random.normal(k1, (4, 512, H), dtype=jnp.float32)
        w_gate = jax.random.normal(k2, (I, H), dtype=jnp.float32) * 0.02
        w_up = jax.random.normal(k3, (I, H), dtype=jnp.float32) * 0.02
        w_down = jax.random.normal(k4, (H, I), dtype=jnp.float32) * 0.02
        return {'x': x, 'w_gate': w_gate, 'w_up': w_up, 'w_down': w_down}
    _L0_ffn_in = _L0_ffn_setup()

    def _L1_attn_setup():
        import jax, jax.numpy as jnp
        import numpy as np
        DIM = 128
        HEADS = 16
        HEAD_DIM = DIM // HEADS

        def _xavier(key, shape):
            fan_out, fan_in = shape
            limit = float(np.sqrt(6.0 / (fan_in + fan_out)))
            return jax.random.uniform(key, shape, jnp.float32, -limit, limit)
        key = jax.random.key(seed)
        kx, kv, kk, kq = jax.random.split(key, 4)
        x = jax.random.normal(kx, (4, 256, DIM), jnp.float32)
        Wv = _xavier(kv, (DIM, DIM))
        Wk = _xavier(kk, (DIM, DIM))
        Wq = _xavier(kq, (DIM, DIM))
        return {'x': x, 'Wq': Wq, 'Wk': Wk, 'Wv': Wv}
    _L1_attn_in = _L1_attn_setup()

    def _L1_ffn_setup():
        import jax, jax.numpy as jnp
        import numpy as np
        B, T, D, E, H, K = (2, 256, 128, 8, 512, 2)
        key = jax.random.key(seed)
        ks = jax.random.split(key, 8)
        s = 0.02
        return {'x': jax.random.normal(ks[0], (B, T, D), jnp.float32), 'rw1': jax.random.normal(ks[1], (D, D), jnp.float32) * s, 'rb1': jnp.zeros((D,), jnp.float32), 'rw2': jax.random.normal(ks[2], (D, E), jnp.float32) * s, 'rb2': jnp.zeros((E,), jnp.float32), 'we1': jax.random.normal(ks[3], (E, D, H), jnp.float32) * s, 'be1': jnp.zeros((E, H), jnp.float32), 'we2': jax.random.normal(ks[4], (E, H, D), jnp.float32) * s, 'be2': jnp.zeros((E, D), jnp.float32)}
    _L1_ffn_in = _L1_ffn_setup()

    def _L2_attn_setup():
        import jax, jax.numpy as jnp
        import numpy as np
        N_HEADS = 16
        EPS = 1e-06
        key = jax.random.key(seed)
        ks = jax.random.split(key, 5)
        B, N, D, H = (4, 256, 128, N_HEADS)
        x = jax.random.normal(ks[0], (B, N, D), dtype=jnp.float32)
        Wq = jax.random.normal(ks[1], (D, D), dtype=jnp.float32) * D ** (-0.5)
        Wk = jax.random.normal(ks[2], (D, D), dtype=jnp.float32) * D ** (-0.5)
        Wv = jax.random.normal(ks[3], (D, D), dtype=jnp.float32) * D ** (-0.5)
        Wo = jax.random.normal(ks[4], (D, D), dtype=jnp.float32) * D ** (-0.5)
        q_scale = jnp.ones((H,), dtype=jnp.float32)
        k_scale = jnp.ones((H,), dtype=jnp.float32)
        return {'x': x, 'Wq': Wq, 'Wk': Wk, 'Wv': Wv, 'Wo': Wo, 'q_scale': q_scale, 'k_scale': k_scale}
    _L2_attn_in = _L2_attn_setup()

    def _L2_ffn_setup():
        import jax, jax.numpy as jnp
        import numpy as np
        DIM = 128
        DEPTH = 2
        HEADS = 8
        DIM_HEAD = 64
        WINDOW = 64
        INNER = HEADS * DIM_HEAD
        HID = int(DIM * 4 * 2 / 3)
        B, N = (2, 1024)
        QK_SCALE = 8.0

        def shift_token(t):
            t1, t2 = jnp.split(t, 2, axis=-1)
            t2 = jnp.pad(t2, ((0, 0), (1, 0), (0, 0)))[:, :-1]
            return jnp.concatenate([t1, t2], axis=-1)

        def l2norm(t):
            return t / jnp.clip(jnp.linalg.norm(t, axis=-1, keepdims=True), 1e-12)

        def rotate_half(x):
            x1, x2 = jnp.split(x, 2, axis=-1)
            return jnp.concatenate([-x2, x1], axis=-1)

        def rotary_xpos(q, k):
            n = q.shape[-2]
            half_idx = jnp.arange(0, DIM_HEAD, 2, dtype=jnp.float32)
            inv_freq = 1.0 / 10000.0 ** (half_idx / DIM_HEAD)
            t = jnp.arange(n, dtype=jnp.float32)
            freqs = t[:, None] * inv_freq[None, :]
            freqs = jnp.concatenate([freqs, freqs], axis=-1)
            base = (half_idx + 0.4 * DIM_HEAD) / (1.4 * DIM_HEAD)
            power = (t - n // 2) / float(WINDOW // 2)
            scale = base[None, :] ** power[:, None]
            scale = jnp.concatenate([scale, scale], axis=-1)
            cos, sin = (jnp.cos(freqs), jnp.sin(freqs))
            q = q * cos * scale + rotate_half(q) * sin * scale
            k = k * cos / scale + rotate_half(k) * sin / scale
            return (q, k)

        def local_attention(q, k, v):
            b, h, n, d = q.shape
            w = n // WINDOW
            bq = q.reshape(b, h, w, WINDOW, d) * QK_SCALE
            bk = k.reshape(b, h, w, WINDOW, d)
            bv = v.reshape(b, h, w, WINDOW, d)

            def look_around(t):
                p = jnp.pad(t, ((0, 0), (0, 0), (1, 0), (0, 0), (0, 0)))
                return jnp.concatenate([p[:, :, :w], p[:, :, 1:]], axis=3)
            bk, bv = (look_around(bk), look_around(bv))
            bt = jnp.arange(n).reshape(w, WINDOW)
            btp = jnp.pad(bt, ((1, 0), (0, 0)), constant_values=-1)
            btk = jnp.concatenate([btp[:w], btp[1:]], axis=1)
            sim = jnp.einsum('bhwid,bhwjd->bhwij', bq, bk)
            i = bt[:, :, None]
            j = btk[:, None, :]
            mask = (i < j) | (i > j + WINDOW) | (j == -1)
            sim = jnp.where(mask, -jnp.finfo(sim.dtype).max, sim)
            attn = jax.nn.softmax(sim, axis=-1)
            out = jnp.einsum('bhwij,bhwjd->bhwid', attn, bv)
            return out.reshape(b, h, n, d)

        def _layer(x, wqkv, qs, ksc, wo, lg, lb, w1, b1, w2, b2):
            b, n, _ = x.shape
            h = shift_token(x)
            qkv = h @ wqkv
            q, k, v = jnp.split(qkv, 3, axis=-1)
            to_heads = lambda t: t.reshape(b, n, HEADS, DIM_HEAD).transpose(0, 2, 1, 3)
            q, k, v = (to_heads(q), to_heads(k), to_heads(v))
            q = l2norm(q) * qs
            k = l2norm(k) * ksc
            q, k = rotary_xpos(q, k)
            o = local_attention(q, k, v)
            o = o.transpose(0, 2, 1, 3).reshape(b, n, INNER)
            x = x + o @ wo
            h = shift_token(x)
            mu = h.mean(-1, keepdims=True)
            var = h.var(-1, keepdims=True)
            h = (h - mu) / jnp.sqrt(var + 1e-05) * lg + lb
            h = h @ w1 + b1
            a, g = jnp.split(h, 2, axis=-1)
            h = a * jax.nn.gelu(g, approximate=False)
            x = x + h @ w2 + b2
            return x
        key = jax.random.key(seed)
        ks = jax.random.split(key, 6)
        return {'x': jax.random.normal(ks[0], (B, N, DIM), jnp.float32), 'wqkv': jax.random.normal(ks[1], (DEPTH, DIM, 3 * INNER), jnp.float32) * 0.02, 'q_scale': jnp.ones((DEPTH, DIM_HEAD), jnp.float32), 'k_scale': jnp.ones((DEPTH, DIM_HEAD), jnp.float32), 'wo': jax.random.normal(ks[2], (DEPTH, INNER, DIM), jnp.float32) * 0.02, 'ln_g': jnp.ones((DEPTH, DIM), jnp.float32), 'ln_b': jnp.zeros((DEPTH, DIM), jnp.float32), 'w1': jax.random.normal(ks[3], (DEPTH, DIM, 2 * HID), jnp.float32) * 0.02, 'b1': jnp.zeros((DEPTH, 2 * HID), jnp.float32), 'w2': jax.random.normal(ks[4], (DEPTH, HID, DIM), jnp.float32) * 0.02, 'b2': jnp.zeros((DEPTH, DIM), jnp.float32)}
    _L2_ffn_in = _L2_ffn_setup()

    def _L3_attn_setup():
        import jax, jax.numpy as jnp
        import numpy as np
        from jax import lax
        B_SZ, SEQ = (8, 256)
        D_MODEL, D_STATE, EXPAND, HEADDIM = (128, 128, 2, 64)
        D_INNER = EXPAND * D_MODEL
        NHEADS = D_INNER // HEADDIM
        NGROUPS, D_CONV, CHUNK = (1, 4, 128)
        CONV_DIM = D_INNER + 2 * NGROUPS * D_STATE
        D_IN_PROJ = 2 * D_INNER + 2 * NGROUPS * D_STATE + NHEADS
        VAR_NUM, EPS = (3, 1e-05)

        def _segsum(a):
            L = a.shape[-1]
            cs = jnp.cumsum(a, -1)
            ss = cs[..., :, None] - cs[..., None, :]
            mask = jnp.tril(jnp.ones((L, L), bool))
            return jnp.where(mask, ss, -jnp.inf)

        def _ssd(x, dt, A, Bm, Cm):
            b, l, h, p = x.shape
            n = Bm.shape[-1]
            c = l // CHUNK
            xc = x.reshape(b, c, CHUNK, h, p)
            dtc = dt.reshape(b, c, CHUNK, h)
            Bc = Bm.reshape(b, c, CHUNK, n)
            Cc = Cm.reshape(b, c, CHUNK, n)
            ac = (dt * A).reshape(b, c, CHUNK, h).transpose(0, 3, 1, 2)
            acs = jnp.cumsum(ac, -1)
            Lmat = jnp.exp(_segsum(ac))
            xdt = xc * dtc[..., None]
            CB = jnp.einsum('bcln,bcsn->bcls', Cc, Bc)
            Y_diag = jnp.einsum('bcls,bhcls,bcshp->bclhp', CB, Lmat, xdt)
            decay_states = jnp.exp(acs[..., -1:] - acs)
            states = jnp.einsum('bcln,bhcl,bclhp->bchpn', Bc, decay_states, xdt)
            chunk_decay = jnp.exp(acs[..., -1])

            def step(carry, inp):
                st, dec = inp
                return (carry * dec[..., None, None] + st, carry)
            _, states_in = lax.scan(step, jnp.zeros((b, h, p, n), x.dtype), (jnp.moveaxis(states, 1, 0), jnp.moveaxis(chunk_decay, 2, 0)))
            states_in = jnp.moveaxis(states_in, 0, 1)
            Y_off = jnp.einsum('bcln,bchpn,bhcl->bclhp', Cc, states_in, jnp.exp(acs))
            return (Y_diag + Y_off).reshape(b, l, h, p)

        def _reference_tuple_inner(embed_data, in_proj_w, conv_w, conv_b, dt_bias, A_log, D, norm_w, out_proj_w, dec_w, dec_b):
            b, l, _ = embed_data.shape
            zxbcdt = embed_data @ in_proj_w.T
            z = zxbcdt[..., :D_INNER]
            xBC = zxbcdt[..., D_INNER:D_INNER + CONV_DIM]
            dt = jax.nn.softplus(zxbcdt[..., D_INNER + CONV_DIM:] + dt_bias)
            xt = lax.conv_general_dilated(xBC.transpose(0, 2, 1), conv_w[:, None, :], (1,), [(D_CONV - 1, 0)], feature_group_count=CONV_DIM, dimension_numbers=('NCH', 'OIH', 'NCH'))
            xBC = jax.nn.silu(xt.transpose(0, 2, 1) + conv_b)
            x = xBC[..., :D_INNER].reshape(b, l, NHEADS, HEADDIM)
            Bm = xBC[..., D_INNER:D_INNER + D_STATE]
            Cm = xBC[..., D_INNER + D_STATE:]
            A = -jnp.exp(A_log)
            y = _ssd(x, dt, A, Bm, Cm) + D[None, None, :, None] * x
            y = y.reshape(b, l, D_INNER) * jax.nn.silu(z)
            y = y * lax.rsqrt(jnp.mean(y * y, -1, keepdims=True) + EPS) * norm_w
            hidden = y @ out_proj_w.T
            pred = hidden @ dec_w.T + dec_b
            return (pred, hidden)
        key = jax.random.key(seed)
        ks = jax.random.split(key, 10)
        return {'embed_data': jax.random.normal(ks[0], (B_SZ, SEQ, D_MODEL), jnp.float32), 'in_proj_w': jax.random.normal(ks[1], (D_IN_PROJ, D_MODEL), jnp.float32) * 0.02, 'conv_w': jax.random.normal(ks[2], (CONV_DIM, D_CONV), jnp.float32) * 0.2, 'conv_b': jnp.zeros((CONV_DIM,), jnp.float32), 'dt_bias': jnp.log(jnp.expm1(jax.random.uniform(ks[3], (NHEADS,), jnp.float32, 0.001, 0.1))), 'A_log': jnp.log(jax.random.uniform(ks[4], (NHEADS,), jnp.float32, 1.0, 16.0)), 'D': jnp.ones((NHEADS,), jnp.float32), 'norm_w': jnp.ones((D_INNER,), jnp.float32), 'out_proj_w': jax.random.normal(ks[5], (D_MODEL, D_INNER), jnp.float32) * 0.02, 'dec_w': jax.random.normal(ks[6], (VAR_NUM, D_MODEL), jnp.float32) * 0.02, 'dec_b': jnp.zeros((VAR_NUM,), jnp.float32)}
    _L3_attn_in = _L3_attn_setup()

    def _L3_ffn_setup():
        import jax, jax.numpy as jnp
        import numpy as np
        B, S, H = (4, 256, 128)
        E, K, INTER = (16, 2, 64)
        ALPHA, LIMIT = (1.702, 7.0)
        key = jax.random.key(seed)
        ks = jax.random.split(key, 6)
        return {'hidden_states': jax.random.normal(ks[0], (B, S, H), jnp.float32), 'router_weight': jax.random.normal(ks[1], (H, E), jnp.float32) * 0.02, 'gate_up_proj': jax.random.normal(ks[2], (E, H, 2 * INTER), jnp.float32) * 0.02, 'gate_up_proj_bias': jax.random.normal(ks[3], (E, 2 * INTER), jnp.float32) * 0.02, 'down_proj': jax.random.normal(ks[4], (E, INTER, H), jnp.float32) * 0.02, 'down_proj_bias': jax.random.normal(ks[5], (E, H), jnp.float32) * 0.02}
    _L3_ffn_in = _L3_ffn_setup()
    _d = {'L0_attn_x': _L0_attn_in['x'], 'L0_attn_qkv_w': _L0_attn_in['qkv_w'], 'L0_attn_qkv_b': _L0_attn_in['qkv_b'], 'L0_attn_rq_w': _L0_attn_in['rq_w'], 'L0_attn_rq_b': _L0_attn_in['rq_b'], 'L0_attn_rkv_w': _L0_attn_in['rkv_w'], 'L0_attn_rkv_b': _L0_attn_in['rkv_b'], 'L0_attn_rout_w': _L0_attn_in['rout_w'], 'L0_attn_rout_b': _L0_attn_in['rout_b'], 'L0_attn_out_w': _L0_attn_in['out_w'], 'L0_attn_out_b': _L0_attn_in['out_b'], 'L0_attn_gl_w': _L0_attn_in['gl_w'], 'L0_attn_gr_w': _L0_attn_in['gr_w'], 'L0_ffn_w_gate': _L0_ffn_in['w_gate'], 'L0_ffn_w_up': _L0_ffn_in['w_up'], 'L0_ffn_w_down': _L0_ffn_in['w_down'], 'L1_attn_Wq': _L1_attn_in['Wq'], 'L1_attn_Wk': _L1_attn_in['Wk'], 'L1_attn_Wv': _L1_attn_in['Wv'], 'L1_ffn_rw1': _L1_ffn_in['rw1'], 'L1_ffn_rb1': _L1_ffn_in['rb1'], 'L1_ffn_rw2': _L1_ffn_in['rw2'], 'L1_ffn_rb2': _L1_ffn_in['rb2'], 'L1_ffn_we1': _L1_ffn_in['we1'], 'L1_ffn_be1': _L1_ffn_in['be1'], 'L1_ffn_we2': _L1_ffn_in['we2'], 'L1_ffn_be2': _L1_ffn_in['be2'], 'L2_attn_Wq': _L2_attn_in['Wq'], 'L2_attn_Wk': _L2_attn_in['Wk'], 'L2_attn_Wv': _L2_attn_in['Wv'], 'L2_attn_Wo': _L2_attn_in['Wo'], 'L2_attn_q_scale': _L2_attn_in['q_scale'], 'L2_attn_k_scale': _L2_attn_in['k_scale'], 'L2_ffn_wqkv': _L2_ffn_in['wqkv'], 'L2_ffn_q_scale': _L2_ffn_in['q_scale'], 'L2_ffn_k_scale': _L2_ffn_in['k_scale'], 'L2_ffn_wo': _L2_ffn_in['wo'], 'L2_ffn_ln_g': _L2_ffn_in['ln_g'], 'L2_ffn_ln_b': _L2_ffn_in['ln_b'], 'L2_ffn_w1': _L2_ffn_in['w1'], 'L2_ffn_b1': _L2_ffn_in['b1'], 'L2_ffn_w2': _L2_ffn_in['w2'], 'L2_ffn_b2': _L2_ffn_in['b2'], 'L3_attn_in_proj_w': _L3_attn_in['in_proj_w'], 'L3_attn_conv_w': _L3_attn_in['conv_w'], 'L3_attn_conv_b': _L3_attn_in['conv_b'], 'L3_attn_dt_bias': _L3_attn_in['dt_bias'], 'L3_attn_A_log': _L3_attn_in['A_log'], 'L3_attn_D': _L3_attn_in['D'], 'L3_attn_norm_w': _L3_attn_in['norm_w'], 'L3_attn_out_proj_w': _L3_attn_in['out_proj_w'], 'L3_attn_dec_w': _L3_attn_in['dec_w'], 'L3_attn_dec_b': _L3_attn_in['dec_b'], 'L3_ffn_router_weight': _L3_ffn_in['router_weight'], 'L3_ffn_gate_up_proj': _L3_ffn_in['gate_up_proj'], 'L3_ffn_gate_up_proj_bias': _L3_ffn_in['gate_up_proj_bias'], 'L3_ffn_down_proj': _L3_ffn_in['down_proj'], 'L3_ffn_down_proj_bias': _L3_ffn_in['down_proj_bias']}
    _x0 = _d['L0_attn_x']
    _d['L0_attn_x'] = jax.random.normal(jax.random.fold_in(jax.random.key(seed), 1), (1, 2048, 128), dtype=_x0.dtype)
    del _x0
    return _d

def reference(L0_attn_x, L0_attn_qkv_w, L0_attn_qkv_b, L0_attn_rq_w, L0_attn_rq_b, L0_attn_rkv_w, L0_attn_rkv_b, L0_attn_rout_w, L0_attn_rout_b, L0_attn_out_w, L0_attn_out_b, L0_attn_gl_w, L0_attn_gr_w, L0_ffn_w_gate, L0_ffn_w_up, L0_ffn_w_down, L1_attn_Wq, L1_attn_Wk, L1_attn_Wv, L1_ffn_rw1, L1_ffn_rb1, L1_ffn_rw2, L1_ffn_rb2, L1_ffn_we1, L1_ffn_be1, L1_ffn_we2, L1_ffn_be2, L2_attn_Wq, L2_attn_Wk, L2_attn_Wv, L2_attn_Wo, L2_attn_q_scale, L2_attn_k_scale, L2_ffn_wqkv, L2_ffn_q_scale, L2_ffn_k_scale, L2_ffn_wo, L2_ffn_ln_g, L2_ffn_ln_b, L2_ffn_w1, L2_ffn_b1, L2_ffn_w2, L2_ffn_b2, L3_attn_in_proj_w, L3_attn_conv_w, L3_attn_conv_b, L3_attn_dt_bias, L3_attn_A_log, L3_attn_D, L3_attn_norm_w, L3_attn_out_proj_w, L3_attn_dec_w, L3_attn_dec_b, L3_ffn_router_weight, L3_ffn_gate_up_proj, L3_ffn_gate_up_proj_bias, L3_ffn_down_proj, L3_ffn_down_proj_bias):

    def _L0_attn_ref(x, qkv_w, qkv_b, rq_w, rq_b, rkv_w, rkv_b, rout_w, rout_b, out_w, out_b, gl_w, gr_w):
        import jax, jax.numpy as jnp
        import numpy as np
        D_MODEL = 128
        N_HEADS = 16
        HEAD_DIM = D_MODEL // N_HEADS
        WINDOW = 128
        LOCAL_BLOCK = 32
        LATENT_TOKENS = 64
        LATENT_D = 32
        LATENT_HEADS = 4
        LATENT_HD = LATENT_D // LATENT_HEADS
        NEG = -1000000000.0

        def _local_attention(q, k, v):
            B, H, S, hd = q.shape
            bs = min(S, max(WINDOW, LOCAL_BLOCK))
            nb = S // bs
            w = WINDOW
            L = bs + w - 1
            k_pad = jnp.pad(k, ((0, 0), (0, 0), (w - 1, 0), (0, 0)))
            v_pad = jnp.pad(v, ((0, 0), (0, 0), (w - 1, 0), (0, 0)))
            starts = jnp.arange(nb) * bs
            idx = starts[:, None] + jnp.arange(L)[None, :]
            kb = k_pad[:, :, idx]
            vb = v_pad[:, :, idx]
            qb = q.reshape(B, H, nb, bs, hd)
            q_pos = starts[:, None] + jnp.arange(bs)[None, :]
            k_gpos = starts[:, None] + jnp.arange(L)[None, :] - (w - 1)
            dist = q_pos[:, :, None] - k_gpos[:, None, :]
            allowed = (dist > 0) & (dist <= w) & (k_gpos[:, None, :] >= 0)
            scale = 1.0 / np.sqrt(hd)
            scores = jnp.einsum('bhnqd,bhnkd->bhnqk', qb, kb) * scale
            scores = jnp.where(allowed, scores, NEG)
            attn = jax.nn.softmax(scores, axis=-1)
            attn = jnp.where(allowed.any(-1)[None, None, :, :, None], attn, 0.0)
            out = jnp.einsum('bhnqk,bhnkd->bhnqd', attn, vb)
            return out.reshape(B, H, S, hd)
        B, S, D = x.shape
        qkv = x @ qkv_w + qkv_b
        q, k, v = jnp.split(qkv, 3, axis=-1)

        def heads(t):
            return t.reshape(B, S, N_HEADS, HEAD_DIM).transpose(0, 2, 1, 3)
        local = _local_attention(heads(q), heads(k), heads(v))
        chunk = -(-S // min(LATENT_TOKENS, S))
        nlat = S // chunk
        pooled = x.reshape(B, nlat, chunk, D).mean(axis=2)
        chunk_ids = jnp.arange(S) // chunk
        rq = (x @ rq_w + rq_b).reshape(B, S, LATENT_HEADS, LATENT_HD).transpose(0, 2, 1, 3)
        rkv = pooled @ rkv_w + rkv_b
        rk, rv = jnp.split(rkv, 2, axis=-1)
        rk = rk.reshape(B, nlat, LATENT_HEADS, LATENT_HD).transpose(0, 2, 1, 3)
        rv = rv.reshape(B, nlat, LATENT_HEADS, LATENT_HD).transpose(0, 2, 1, 3)
        lscale = 1.0 / np.sqrt(LATENT_HD)
        lscores = jnp.einsum('bhsd,bhld->bhsl', rq, rk) * lscale
        lat_allowed = jnp.arange(nlat)[None, :] < chunk_ids[:, None]
        lscores = jnp.where(lat_allowed[None, None], lscores, NEG)
        lattn = jax.nn.softmax(lscores, axis=-1)
        lattn = jnp.where(lat_allowed.any(-1)[None, None, :, None], lattn, 0.0)
        lat_out = jnp.einsum('bhsl,bhld->bhsd', lattn, rv)
        lat_out = lat_out.transpose(0, 2, 1, 3).reshape(B, S, LATENT_D)
        remote = lat_out @ rout_w + rout_b
        remote_h = remote.reshape(B, S, N_HEADS, HEAD_DIM).transpose(0, 2, 1, 3)
        gate = jax.nn.sigmoid(local @ gl_w + remote_h @ gr_w)
        mixed = gate * local + (1.0 - gate) * remote_h
        mixed = mixed.transpose(0, 2, 1, 3).reshape(B, S, D)
        return mixed @ out_w + out_b

    def _L0_ffn_ref(x, w_gate, w_up, w_down):
        import jax, jax.numpy as jnp
        import numpy as np
        BLOCK = 16
        _GRID = jnp.array([0.0, 0.5, 1.0, 1.5, 2.0, 3.0, 4.0, 6.0], dtype=jnp.float32)
        _MID = jnp.array([0.25, 0.75, 1.25, 1.75, 2.5, 3.5, 5.0], dtype=jnp.float32)

        def fp4_quant_dequant(x):
            shape = x.shape
            xb = x.reshape(shape[:-1] + (shape[-1] // BLOCK, BLOCK))
            scale = jnp.max(jnp.abs(xb), axis=-1, keepdims=True) / 6.0
            scale = jnp.maximum(scale, jnp.float32(1e-12))
            xn = xb / scale
            idx = jnp.searchsorted(_MID, jnp.abs(xn))
            q = _GRID[idx] * jnp.sign(xn) * scale
            return q.reshape(shape)

        def fp4_linear(x, w):
            xq = fp4_quant_dequant(x)
            wq = fp4_quant_dequant(w)
            return jnp.einsum('bsk,nk->bsn', xq, wq)
        gate = fp4_linear(x, w_gate)
        y = fp4_linear(x, w_up)
        h = jax.nn.silu(gate) * y
        return fp4_linear(h, w_down)

    def _L1_attn_ref(x, Wq, Wk, Wv):
        import jax, jax.numpy as jnp
        import numpy as np
        DIM = 128
        HEADS = 16
        HEAD_DIM = DIM // HEADS

        def _xavier(key, shape):
            fan_out, fan_in = shape
            limit = float(np.sqrt(6.0 / (fan_in + fan_out)))
            return jax.random.uniform(key, shape, jnp.float32, -limit, limit)
        B, S, D = x.shape
        H, Hd = (HEADS, HEAD_DIM)
        q = (x @ Wq.T).reshape(B, S, H, Hd)
        k = (x @ Wk.T).reshape(B, S, H, Hd)
        v = (x @ Wv.T).reshape(B, S, H, Hd)
        energy = jnp.einsum('bqhd,bkhd->bhqk', q, k)
        attn = jax.nn.softmax(energy / jnp.sqrt(jnp.float32(D)), axis=-1)
        out = jnp.einsum('bhqk,bkhd->bqhd', attn, v).reshape(B, S, D)
        return out

    def _L1_ffn_ref(x, rw1, rb1, rw2, rb2, we1, be1, we2, be2):
        import jax, jax.numpy as jnp
        import numpy as np
        B, T, D, E, H, K = (2, 256, 128, 8, 512, 2)
        b, t, d = x.shape
        xt = x.reshape(b * t, d)
        n = xt.shape[0]
        logits = jax.nn.silu(xt @ rw1 + rb1) @ rw2 + rb2
        _, idx = jax.lax.top_k(logits, K)
        mask = jnp.zeros((n, E), bool).at[jnp.arange(n)[:, None], idx].set(True)
        w = jax.nn.softmax(jnp.where(mask, logits, -jnp.inf), axis=1)
        h = jax.nn.silu(jnp.einsum('nd,edh->enh', xt, we1) + be1[:, None, :])
        eo = jnp.einsum('enh,ehd->end', h, we2) + be2[:, None, :]
        y = xt + jnp.einsum('ne,end->nd', w, eo)
        return y.reshape(b, t, d)

    def _L2_attn_ref(x, Wq, Wk, Wv, Wo, q_scale, k_scale):
        import jax, jax.numpy as jnp
        import numpy as np
        N_HEADS = 16
        EPS = 1e-06
        B, N, D = x.shape
        H = N_HEADS
        hd = D // H
        q = jax.nn.silu(x @ Wq.T)
        k = jax.nn.silu(x @ Wk.T)
        v = jax.nn.silu(x @ Wv.T)
        q = q.reshape(B, N, H, hd).transpose(0, 2, 1, 3)
        k = k.reshape(B, N, H, hd).transpose(0, 2, 1, 3)
        v = v.reshape(B, N, H, hd).transpose(0, 2, 1, 3)
        r_q = jnp.linalg.norm(q, axis=-1, keepdims=True)
        r_k = jnp.linalg.norm(k, axis=-1, keepdims=True)
        q_dir = q / (r_q + EPS)
        k_dir = k / (r_k + EPS)
        scores = jnp.einsum('bhnd,bhmd->bhnm', q_dir, k_dir)
        sq = q_scale[None, :, None, None]
        sk = k_scale[None, :, None, None]
        scores = scores * (r_q * sq) * (jnp.swapaxes(r_k, -2, -1) * sk)
        mask = jnp.tril(jnp.ones((N, N), dtype=bool))
        scores = jnp.where(mask, scores, -jnp.inf)
        probs = jax.nn.softmax(scores, axis=-1)
        out = jnp.einsum('bhnm,bhmd->bhnd', probs, v)
        out = out.transpose(0, 2, 1, 3).reshape(B, N, D)
        return out @ Wo.T

    def _L2_ffn_ref(x, wqkv, q_scale, k_scale, wo, ln_g, ln_b, w1, b1, w2, b2):
        import jax, jax.numpy as jnp
        import numpy as np
        DIM = 128
        DEPTH = 2
        HEADS = 8
        DIM_HEAD = 64
        WINDOW = 64
        INNER = HEADS * DIM_HEAD
        HID = int(DIM * 4 * 2 / 3)
        B, N = (2, 1024)
        QK_SCALE = 8.0

        def shift_token(t):
            t1, t2 = jnp.split(t, 2, axis=-1)
            t2 = jnp.pad(t2, ((0, 0), (1, 0), (0, 0)))[:, :-1]
            return jnp.concatenate([t1, t2], axis=-1)

        def l2norm(t):
            return t / jnp.clip(jnp.linalg.norm(t, axis=-1, keepdims=True), 1e-12)

        def rotate_half(x):
            x1, x2 = jnp.split(x, 2, axis=-1)
            return jnp.concatenate([-x2, x1], axis=-1)

        def rotary_xpos(q, k):
            n = q.shape[-2]
            half_idx = jnp.arange(0, DIM_HEAD, 2, dtype=jnp.float32)
            inv_freq = 1.0 / 10000.0 ** (half_idx / DIM_HEAD)
            t = jnp.arange(n, dtype=jnp.float32)
            freqs = t[:, None] * inv_freq[None, :]
            freqs = jnp.concatenate([freqs, freqs], axis=-1)
            base = (half_idx + 0.4 * DIM_HEAD) / (1.4 * DIM_HEAD)
            power = (t - n // 2) / float(WINDOW // 2)
            scale = base[None, :] ** power[:, None]
            scale = jnp.concatenate([scale, scale], axis=-1)
            cos, sin = (jnp.cos(freqs), jnp.sin(freqs))
            q = q * cos * scale + rotate_half(q) * sin * scale
            k = k * cos / scale + rotate_half(k) * sin / scale
            return (q, k)

        def local_attention(q, k, v):
            b, h, n, d = q.shape
            w = n // WINDOW
            bq = q.reshape(b, h, w, WINDOW, d) * QK_SCALE
            bk = k.reshape(b, h, w, WINDOW, d)
            bv = v.reshape(b, h, w, WINDOW, d)

            def look_around(t):
                p = jnp.pad(t, ((0, 0), (0, 0), (1, 0), (0, 0), (0, 0)))
                return jnp.concatenate([p[:, :, :w], p[:, :, 1:]], axis=3)
            bk, bv = (look_around(bk), look_around(bv))
            bt = jnp.arange(n).reshape(w, WINDOW)
            btp = jnp.pad(bt, ((1, 0), (0, 0)), constant_values=-1)
            btk = jnp.concatenate([btp[:w], btp[1:]], axis=1)
            sim = jnp.einsum('bhwid,bhwjd->bhwij', bq, bk)
            i = bt[:, :, None]
            j = btk[:, None, :]
            mask = (i < j) | (i > j + WINDOW) | (j == -1)
            sim = jnp.where(mask, -jnp.finfo(sim.dtype).max, sim)
            attn = jax.nn.softmax(sim, axis=-1)
            out = jnp.einsum('bhwij,bhwjd->bhwid', attn, bv)
            return out.reshape(b, h, n, d)

        def _layer(x, wqkv, qs, ksc, wo, lg, lb, w1, b1, w2, b2):
            b, n, _ = x.shape
            h = shift_token(x)
            qkv = h @ wqkv
            q, k, v = jnp.split(qkv, 3, axis=-1)
            to_heads = lambda t: t.reshape(b, n, HEADS, DIM_HEAD).transpose(0, 2, 1, 3)
            q, k, v = (to_heads(q), to_heads(k), to_heads(v))
            q = l2norm(q) * qs
            k = l2norm(k) * ksc
            q, k = rotary_xpos(q, k)
            o = local_attention(q, k, v)
            o = o.transpose(0, 2, 1, 3).reshape(b, n, INNER)
            x = x + o @ wo
            h = shift_token(x)
            mu = h.mean(-1, keepdims=True)
            var = h.var(-1, keepdims=True)
            h = (h - mu) / jnp.sqrt(var + 1e-05) * lg + lb
            h = h @ w1 + b1
            a, g = jnp.split(h, 2, axis=-1)
            h = a * jax.nn.gelu(g, approximate=False)
            x = x + h @ w2 + b2
            return x
        for l in range(DEPTH):
            x = _layer(x, wqkv[l], q_scale[l], k_scale[l], wo[l], ln_g[l], ln_b[l], w1[l], b1[l], w2[l], b2[l])
        return x

    def _L3_attn_ref(embed_data, in_proj_w, conv_w, conv_b, dt_bias, A_log, D, norm_w, out_proj_w, dec_w, dec_b):
        import jax, jax.numpy as jnp
        import numpy as np
        from jax import lax
        B_SZ, SEQ = (8, 256)
        D_MODEL, D_STATE, EXPAND, HEADDIM = (128, 128, 2, 64)
        D_INNER = EXPAND * D_MODEL
        NHEADS = D_INNER // HEADDIM
        NGROUPS, D_CONV, CHUNK = (1, 4, 128)
        CONV_DIM = D_INNER + 2 * NGROUPS * D_STATE
        D_IN_PROJ = 2 * D_INNER + 2 * NGROUPS * D_STATE + NHEADS
        VAR_NUM, EPS = (3, 1e-05)

        def _segsum(a):
            L = a.shape[-1]
            cs = jnp.cumsum(a, -1)
            ss = cs[..., :, None] - cs[..., None, :]
            mask = jnp.tril(jnp.ones((L, L), bool))
            return jnp.where(mask, ss, -jnp.inf)

        def _ssd(x, dt, A, Bm, Cm):
            b, l, h, p = x.shape
            n = Bm.shape[-1]
            c = l // CHUNK
            xc = x.reshape(b, c, CHUNK, h, p)
            dtc = dt.reshape(b, c, CHUNK, h)
            Bc = Bm.reshape(b, c, CHUNK, n)
            Cc = Cm.reshape(b, c, CHUNK, n)
            ac = (dt * A).reshape(b, c, CHUNK, h).transpose(0, 3, 1, 2)
            acs = jnp.cumsum(ac, -1)
            Lmat = jnp.exp(_segsum(ac))
            xdt = xc * dtc[..., None]
            CB = jnp.einsum('bcln,bcsn->bcls', Cc, Bc)
            Y_diag = jnp.einsum('bcls,bhcls,bcshp->bclhp', CB, Lmat, xdt)
            decay_states = jnp.exp(acs[..., -1:] - acs)
            states = jnp.einsum('bcln,bhcl,bclhp->bchpn', Bc, decay_states, xdt)
            chunk_decay = jnp.exp(acs[..., -1])

            def step(carry, inp):
                st, dec = inp
                return (carry * dec[..., None, None] + st, carry)
            _, states_in = lax.scan(step, jnp.zeros((b, h, p, n), x.dtype), (jnp.moveaxis(states, 1, 0), jnp.moveaxis(chunk_decay, 2, 0)))
            states_in = jnp.moveaxis(states_in, 0, 1)
            Y_off = jnp.einsum('bcln,bchpn,bhcl->bclhp', Cc, states_in, jnp.exp(acs))
            return (Y_diag + Y_off).reshape(b, l, h, p)

        def _reference_tuple_inner(embed_data, in_proj_w, conv_w, conv_b, dt_bias, A_log, D, norm_w, out_proj_w, dec_w, dec_b):
            b, l, _ = embed_data.shape
            zxbcdt = embed_data @ in_proj_w.T
            z = zxbcdt[..., :D_INNER]
            xBC = zxbcdt[..., D_INNER:D_INNER + CONV_DIM]
            dt = jax.nn.softplus(zxbcdt[..., D_INNER + CONV_DIM:] + dt_bias)
            xt = lax.conv_general_dilated(xBC.transpose(0, 2, 1), conv_w[:, None, :], (1,), [(D_CONV - 1, 0)], feature_group_count=CONV_DIM, dimension_numbers=('NCH', 'OIH', 'NCH'))
            xBC = jax.nn.silu(xt.transpose(0, 2, 1) + conv_b)
            x = xBC[..., :D_INNER].reshape(b, l, NHEADS, HEADDIM)
            Bm = xBC[..., D_INNER:D_INNER + D_STATE]
            Cm = xBC[..., D_INNER + D_STATE:]
            A = -jnp.exp(A_log)
            y = _ssd(x, dt, A, Bm, Cm) + D[None, None, :, None] * x
            y = y.reshape(b, l, D_INNER) * jax.nn.silu(z)
            y = y * lax.rsqrt(jnp.mean(y * y, -1, keepdims=True) + EPS) * norm_w
            hidden = y @ out_proj_w.T
            pred = hidden @ dec_w.T + dec_b
            return (pred, hidden)
        return _reference_tuple_inner(embed_data, in_proj_w, conv_w, conv_b, dt_bias, A_log, D, norm_w, out_proj_w, dec_w, dec_b)[1]

    def _L3_ffn_ref(hidden_states, router_weight, gate_up_proj, gate_up_proj_bias, down_proj, down_proj_bias):
        import jax, jax.numpy as jnp
        import numpy as np
        B, S, H = (4, 256, 128)
        E, K, INTER = (16, 2, 64)
        ALPHA, LIMIT = (1.702, 7.0)
        b, s, h = hidden_states.shape
        x = hidden_states.reshape(-1, h)
        logits = x @ router_weight
        topk_w, topk_i = jax.lax.top_k(logits, K)
        topk_w = jax.nn.softmax(topk_w, axis=-1)
        one_hot = (topk_i[..., None] == jnp.arange(E)[None, None, :]).astype(topk_w.dtype)
        scores = jnp.einsum('tk,tke->te', topk_w, one_hot)
        gu = jnp.einsum('th,ehf->tef', x, gate_up_proj) + gate_up_proj_bias
        gate = gu[..., ::2]
        up = gu[..., 1::2]
        gate = jnp.minimum(gate, LIMIT)
        up = jnp.clip(up, -LIMIT, LIMIT)
        glu = gate * jax.nn.sigmoid(gate * ALPHA)
        act = (up + 1.0) * glu
        out = jnp.einsum('tei,eih,te->th', act, down_proj, scores)
        out = out + jnp.einsum('te,eh->th', scores, down_proj_bias)
        return out.reshape(b, s, h)
    x = L0_attn_x
    x = x + _L0_attn_ref(_layernorm(x, axis=-1), L0_attn_qkv_w, L0_attn_qkv_b, L0_attn_rq_w, L0_attn_rq_b, L0_attn_rkv_w, L0_attn_rkv_b, L0_attn_rout_w, L0_attn_rout_b, L0_attn_out_w, L0_attn_out_b, L0_attn_gl_w, L0_attn_gr_w)
    x = x + _L0_ffn_ref(_layernorm(x, axis=-1), L0_ffn_w_gate, L0_ffn_w_up, L0_ffn_w_down)
    x = x + _L1_attn_ref(_layernorm(x, axis=-1), L1_attn_Wq, L1_attn_Wk, L1_attn_Wv)
    x = x + _L1_ffn_ref(_layernorm(x, axis=-1), L1_ffn_rw1, L1_ffn_rb1, L1_ffn_rw2, L1_ffn_rb2, L1_ffn_we1, L1_ffn_be1, L1_ffn_we2, L1_ffn_be2)
    x = x + _L2_attn_ref(_layernorm(x, axis=-1), L2_attn_Wq, L2_attn_Wk, L2_attn_Wv, L2_attn_Wo, L2_attn_q_scale, L2_attn_k_scale)
    x = x + _L2_ffn_ref(_layernorm(x, axis=-1), L2_ffn_wqkv, L2_ffn_q_scale, L2_ffn_k_scale, L2_ffn_wo, L2_ffn_ln_g, L2_ffn_ln_b, L2_ffn_w1, L2_ffn_b1, L2_ffn_w2, L2_ffn_b2)
    x = x + _L3_attn_ref(_layernorm(x, axis=-1), L3_attn_in_proj_w, L3_attn_conv_w, L3_attn_conv_b, L3_attn_dt_bias, L3_attn_A_log, L3_attn_D, L3_attn_norm_w, L3_attn_out_proj_w, L3_attn_dec_w, L3_attn_dec_b)
    x = x + _L3_ffn_ref(_layernorm(x, axis=-1), L3_ffn_router_weight, L3_ffn_gate_up_proj, L3_ffn_gate_up_proj_bias, L3_ffn_down_proj, L3_ffn_down_proj_bias)
    return x

_drawn_inputs = setup_inputs


def setup_inputs(seed=0):
    import zlib

    import numpy as np

    out = dict(_drawn_inputs(seed))
    spreads = {'L0_attn_qkv_b': (0.0, 0.501),
     'L0_attn_rq_b': (0.0, 0.8),
     'L0_attn_rkv_b': (0.0, 0.8),
     'L0_attn_rout_b': (0.0, 0.509),
     'L0_attn_out_b': (0.0, 0.1),
     'L1_ffn_rb1': (0.0, 0.8),
     'L1_ffn_rb2': (0.0, 0.1),
     'L1_ffn_be1': (0.0, 0.8),
     'L1_ffn_be2': (0.0, 0.1),
     'L2_attn_q_scale': (1.0, 0.6),
     'L2_attn_k_scale': (1.0, 0.6),
     'L2_ffn_q_scale': (1.0, 0.6),
     'L2_ffn_k_scale': (1.0, 0.6),
     'L2_ffn_ln_g': (1.0, 0.6),
     'L2_ffn_ln_b': (0.0, 0.8),
     'L2_ffn_b1': (0.0, 0.8),
     'L2_ffn_b2': (0.0, 0.1),
     'L3_attn_conv_b': (0.0, 0.1),
     'L3_attn_D': (1.0, 0.6),
     'L3_attn_norm_w': (1.0, 0.6),
     'L3_attn_dec_b': (0.0, 0.1)}
    factors = {'L0_attn_qkv_w': 8.0,
     'L0_attn_rq_w': 8.0,
     'L0_attn_rkv_w': 8.0,
     'L0_attn_rout_w': 8.0,
     'L0_attn_gl_w': 8.0,
     'L0_attn_gr_w': 8.0,
     'L0_ffn_w_gate': 5.475,
     'L0_ffn_w_up': 5.218,
     'L0_ffn_w_down': 5.235,
     'L1_ffn_rw1': 8.0,
     'L1_ffn_rw2': 8.0,
     'L1_ffn_we1': 3.091,
     'L1_ffn_we2': 2.836,
     'L2_ffn_wqkv': 4.805,
     'L2_ffn_wo': 4.723,
     'L2_ffn_w1': 8.0,
     'L2_ffn_w2': 8.0,
     'L3_attn_dt_bias': 8.0,
     'L3_attn_A_log': 8.0,
     'L3_ffn_router_weight': 8.0,
     'L3_ffn_gate_up_proj': 8.0,
     'L3_ffn_gate_up_proj_bias': 8.0,
     'L3_ffn_down_proj': 8.0,
     'L3_ffn_down_proj_bias': 8.0}
    for name, (base, spread) in spreads.items():
        noise = np.random.default_rng([zlib.crc32(name.encode()), seed]).standard_normal(out[name].shape)
        drawn = base * np.exp(spread * noise) if base else spread * noise
        out[name] = jnp.asarray(drawn.astype(out[name].dtype))
    for name, factor in factors.items():
        out[name] = (out[name] * factor).astype(out[name].dtype)
    return out
```

```python
from contextlib import ExitStack

import numpy as np

import concourse.bass as bass
from concourse import mybir

F32 = mybir.dt.float32
BF16 = mybir.dt.bfloat16
ALU = mybir.AluOpType
ACT = mybir.ActivationFunctionType
AX = mybir.AxisListType

P = 128
S = 2048
NT = S // P
CH = 512
NC = S // CH
H = 16
HD = P // H
NEG = -1.0e30
M_FLOOR = -1.0e29
TERMS = 9
QK_ROWS = TERMS * HD
QKM_ROWS = QK_ROWS + 3


class Stage:

    def __init__(self, nc, name):
        self.nc, self.name, self.ctx, self.sems = nc, name, ExitStack(), []

    def sb(self, name, shape, dt=F32):
        return self.ctx.enter_context(self.nc.sbuf_tensor(f"{self.name}_{name}", shape, dt))

    def ps(self, name, cols=CH, dt=F32):
        return self.ctx.enter_context(self.nc.psum_tensor(f"{self.name}_{name}", [P, cols], dt))

    def sem(self, name):
        s = self.nc.alloc_semaphore(name=f"{self.name}_{name}")
        self.sems.append(s)
        return s

    def block(self):
        return self.nc.Block()

    def close(self):
        self.nc.clear_and_free_semaphores(self.sems)
        self.nc.all_engine_barrier()
        self.ctx.close()


class Head:

    def __init__(self, k, i=None, stride=0):
        self.k, self.i, self.stride = k, i, stride

    def __add__(self, n):
        return Head(self.k + n, self.i, self.stride)

    def __sub__(self, n):
        return self + -n

    def count(self, per_head, more=0):
        fixed = self.k * per_head + more
        return fixed if self.i is None else self.i * (self.stride * per_head) + fixed

    def turn(self, per_head, more=0):
        fixed = self.k // 2 * per_head + more
        return fixed if self.i is None else self.i * per_head + fixed


def wait(eng, sem, value):
    if isinstance(value, int) and value <= 0:
        return
    eng.wait_ge(sem, value)


def held_since(n, bufs, per_head):
    if n >= bufs:
        return n - bufs + 1
    last = max(m for m in range(per_head) if m % bufs == n % bufs)
    return last + 1 - per_head


def build_constants(nc, g):
    st = Stage(nc, "const")
    made = st.sem("made")
    count = [0]
    with st.block() as block:
        @block.gpsimd
        def _(pool):
            def chain(ins):
                ins.then_inc(made, 1)
                count[0] += 1
                pool.wait_ge(made, count[0])

            def fill(t, v):
                chain(nc.gpsimd.memset(t, v))

            def keep(t, op, base, cm, step, value, n=P):
                chain(nc.gpsimd.affine_select(out=t, in_=t, compare_op=op, fill=value, base=base,
                                              pattern=[[step, n]], channel_multiplier=cm))

            fill(g.ident[:], 0.0)
            keep(g.ident[:], ALU.not_equal, 0, 1, -1, 1.0)
            fill(g.identb[:], 0.0)
            keep(g.identb[:], ALU.not_equal, 0, 1, -1, 1.0)
            fill(g.ones[:], 1.0)
            fill(g.expand[:], 1.0)
            keep(g.expand[:], ALU.is_ge, 0, -HD, 1, 0.0)
            keep(g.expand[:], ALU.is_ge, HD - 1, HD, -1, 0.0)
            fill(g.blockdiag[:], 1.0)
            v = g.blockdiag[:].rearrange("p (h d) -> p h d", d=HD)
            for base, cm, step in ((0, 1, -HD), (HD - 1, -1, HD)):
                chain(nc.gpsimd.affine_select(out=v, in_=v, compare_op=ALU.is_ge, fill=0.0, base=base,
                                              pattern=[[step, H], [0, HD]], channel_multiplier=cm))
            for t in (g.cur_q, g.cur_k, g.prev_q, g.prev_k, g.caus_q, g.caus_k):
                fill(t[:], 0.0)
            keep(g.cur_q[:], ALU.is_gt, 0, 1, -1, NEG)
            keep(g.cur_k[:], ALU.is_gt, 0, -1, 1, NEG)
            keep(g.prev_q[:], ALU.is_ge, 0, -1, 1, NEG)
            keep(g.prev_q[:], ALU.is_ge, -1, 0, 1, NEG)
            keep(g.prev_k[:], ALU.is_ge, 0, 1, -1, NEG)
            keep(g.prev_k[:], ALU.is_ge, -1, 1, 0, NEG)
            keep(g.caus_q[:], ALU.is_ge, 0, 1, -1, NEG)
            keep(g.caus_k[:], ALU.is_ge, 0, -1, 1, NEG)
    st.close()


def load_tokens(nc, g, x):
    st = Stage(nc, "loadx")
    loaded = st.sem("loaded")
    with st.block() as block:
        @block.sync
        def _(sp):
            sp.dma_start(g.X[:], x[0].rearrange("(t p) d -> p t d", p=P)).then_inc(loaded, 16)
            sp.wait_ge(loaded, 16)
    st.close()


def store_tokens(nc, g, out):
    st = Stage(nc, "storex")
    stored = g.out_stored
    with st.block() as block:
        @block.sync
        def _(sp):
            sp.dma_start(out[0].rearrange("(t p) d -> p t d", p=P), g.X[:]).then_inc(stored, 16)
            sp.wait_ge(stored, 16)
    st.close()


def layernorm_transpose(nc, g, name, keep_rows=None, normalise=True, src=None, affine=None):
    st = Stage(nc, name)
    X = g.X if src is None else src
    stats = st.sb("stats", [P, NT, 6])
    mv = st.sb("mv", [P, NT, 2])
    std = st.sb("std", [P, NT])
    rstd = st.sb("rstd", [P, NT])
    xn = keep_rows if keep_rows is not None else (st.sb("xn", [P, NT, P]) if normalise else X)
    psT = [st.ps(f"psT{i}") for i in range(2)]
    stats_ready, moments_ready, std_ready, rstd_ready = (
        st.sem("stats_ready"), st.sem("moments_ready"), st.sem("std_ready"), st.sem("rstd_ready"))
    xn_ready, transposed, copied = st.sem("xn_ready"), st.sem("transposed"), st.sem("copied")
    gain = st.sb("gain", [P, 2])
    loaded = st.sem("loaded")
    with st.block() as block:
        @block.sync
        def _(sp):
            if affine is not None:
                for i in range(2):
                    sp.dma_start(gain[:, i:i + 1], affine[i]).then_inc(loaded, 16)

        @block.vector
        def _(dve):
            if not normalise:
                return
            for t in range(NT):
                nc.vector.bn_stats(stats[:, t, :], X[:, t, :]).then_inc(stats_ready, 1)
            for t in range(NT):
                dve.wait_ge(stats_ready, t + 1)
                nc.vector.bn_aggr(mv[:, t, :], stats[:, t, :]).then_inc(moments_ready, 1)
            dve.wait_ge(std_ready, 1)
            nc.vector.reciprocal(rstd[:], std[:]).then_inc(rstd_ready, 1)
            dve.wait_ge(rstd_ready, 1)
            for t in range(NT):
                nc.vector.tensor_scalar(xn[:, t, :], X[:, t, :], mv[:, t, 0:1], rstd[:, t:t + 1],
                                        ALU.subtract, ALU.mult).then_inc(xn_ready, 1)

        @block.scalar
        def _(act):
            if normalise:
                act.wait_ge(moments_ready, NT)
                nc.scalar.activation(std[:], mv[:, :, 1], ACT.Sqrt, bias=1e-5).then_inc(std_ready, 1)
            for c in range(NC):
                act.wait_ge(transposed, 4 * (c + 1))
                if affine is None:
                    ins = nc.scalar.activation(g.XnT[:, c * CH:(c + 1) * CH], psT[c % 2][:], ACT.Copy)
                else:
                    act.wait_ge(loaded, 32)
                    ins = nc.scalar.activation(g.XnT[:, c * CH:(c + 1) * CH], psT[c % 2][:], ACT.Identity,
                                               scale=gain[:, 0:1], bias=gain[:, 1:2])
                ins.then_inc(copied, 1)

        @block.tensor
        def _(pe):
            for t in range(NT):
                if normalise:
                    pe.wait_ge(xn_ready, t + 1)
                if t % 4 == 0 and t >= 8:
                    pe.wait_ge(copied, t // 4 - 1)
                nc.tensor.transpose(psT[t // 4 % 2][:, t % 4 * P:(t % 4 + 1) * P], xn[:, t, :],
                                    g.ident[:]).then_inc(transposed, 1)
    st.close()


def score_pieces(blocks, per_bank, same_chunk):
    out = []
    for i, (r, c) in enumerate(blocks):
        if out and i % per_bank and out[-1][0] == r and out[-1][1] + out[-1][2] == c and not (
                same_chunk and c % 4 == 0):
            out[-1][2] += 1
        else:
            out.append([r, c, 1, i])
    return out


def attention_plan(kind):
    def keys(qb):
        return {"full": range(NT), "causal": range(qb + 1), "window": range(max(qb - 1, 0), qb + 1)}[kind]
    by_query = [(qb, kb) for qb in range(NT) for kb in keys(qb)]
    by_key = [(kb, qb) for kb in range(NT) for qb in range(NT) if kb in keys(qb)]
    a = [score_pieces(by_query[i:i + 4], 4, False) for i in range(0, len(by_query), 4)]
    b = [score_pieces(by_key[i:i + 8], 4, True) for i in range(0, len(by_key), 8)]
    return a, b


def attention_core(nc, g, name, kind, scale):
    a_plan, b_plan = attention_plan(kind)
    NA, NB = len(a_plan), len(b_plan)
    st = Stage(nc, name)
    qh = [st.sb(f"qh{i}", [P, S], BF16) for i in range(2)]
    kh = [st.sb(f"kh{i}", [P, S], BF16) for i in range(2)]
    vh = [st.sb(f"vh{i}", [P, NT, 32]) for i in range(2)]
    prob = [st.sb(f"prob{i}", [P, 2 * CH]) for i in range(4)]
    oh = [st.sb(f"oh{i}", [P, CH]) for i in range(2)]
    npart = 5
    mpart = st.sb("mpart", [P, NT, npart])
    mrow = st.sb("mrow", [P, NT])
    negm = st.sb("negm", [P, NT])
    mrest = st.sb("mrest", [P, NT])
    mb = st.sb("mb", [P, P // NT, NT], BF16)
    mT = st.sb("mT", [3 * NT, P], BF16)
    psA = [st.ps(f"psA{i}") for i in range(2)]
    psB = [st.ps(f"psB{i}", 2 * CH) for i in range(2)]
    psV = [st.ps(f"psV{i}") for i in range(2)]
    psM = psA[0][:].bitcast(BF16)[:, 0:P]

    preset = st.sem("preset")
    qk_loaded = [st.sem(f"qk_loaded{i}") for i in range(2)]
    vh_ready = st.sem("vh_ready")
    a_scored = st.sem("a_scored")
    a_reduced = st.sem("a_reduced")
    m_step = st.sem("m_step")
    mT_written = st.sem("mT_written")
    mT_ready = st.sem("mT_ready")
    m_loaded = st.sem("m_loaded")
    b_scored = st.sem("b_scored")
    b_exped = st.sem("b_exped")
    pv_done = st.sem("pv_done")
    o_copied = st.sem("o_copied")
    o_stored = [st.sem(f"o_stored{i}") for i in range(2)]

    def mask_of(kb, qb, by_query):
        if kind == "causal" and kb == qb:
            return g.caus_q if by_query else g.caus_k
        if kind == "window":
            if kb == qb:
                return g.cur_q if by_query else g.cur_k
            return g.prev_q if by_query else g.prev_k
        return None

    part = {}
    seen = [0] * NT
    for n, pieces in enumerate(a_plan):
        for qb, kb, nb, at in pieces:
            part[n, at] = seen[qb]
            seen[qb] += 1
    assert max(seen) <= npart
    last_of_chunk = {}
    for u, pieces in enumerate(b_plan):
        for kb, qb, nb, at in pieces:
            last_of_chunk[qb // 4] = (u, at)
    first_of_chunk = {}
    for u, pieces in reversed(list(enumerate(b_plan))):
        for kb, qb, nb, at in reversed(pieces):
            first_of_chunk[qb // 4] = (u, at)

    with st.block() as block:
        @block.sync
        def _(sp):
            def load_qk(h, p):
                wait(sp, pv_done, (h - 1).count(NB))
                for i in range(3):
                    lo = 3 * HD * i
                    sp.dma_start(kh[p][lo:lo + 3 * HD, :], g.kparts[:, bass.ds(h.count(HD), HD), :]).then_inc(qk_loaded[p], 16)
                    sp.dma_start(qh[p][lo:lo + 3 * HD, :], g.qparts[i:i + 1, bass.ds(h.count(HD), HD), :]
                                 .broadcast_to([3, HD, S])).then_inc(qk_loaded[p], 16)

            def load_m(h, p):
                wait(sp, mT_ready, (h + 1).count(1))
                for i in range(3):
                    sp.dma_start(qh[p][QK_ROWS + i:QK_ROWS + i + 1, :].rearrange("o (t j) -> o t j", j=P),
                                 mT[i * NT:(i + 1) * NT, :]).then_inc(m_loaded, 16)

            def store_o(h, p):
                wait(sp, o_copied, (h + 1).count(1))
                for c in range(NC):
                    sp.dma_start(g.o_dram[bass.ds(h.count(HD), HD), c * CH:(c + 1) * CH],
                                 oh[p][32 * c:32 * c + HD, :]).then_inc(o_stored[p], 16)
                    sp.dma_start(g.den_dram[bass.ds(h.count(1), 1), c * CH:(c + 1) * CH],
                                 oh[p][32 * c + HD:32 * c + HD + 1, :]).then_inc(o_stored[p], 16)

            def step(h, p, first=False, more=2):
                if more >= 1:
                    load_m(h + 1, 1 - p)
                if not first:
                    store_o(h - 1, 1 - p)
                if more == 2:
                    load_qk(h + 2, p)

            sp.wait_ge(preset, 8)
            load_qk(Head(0), 0)
            load_qk(Head(1), 1)
            load_m(Head(0), 0)
            step(Head(0), 0, first=True)
            with nc.sync.Fori(0, (H - 4) // 2) as i:
                step(Head(1, i, 2), 1)
                step(Head(2, i, 2), 0)
            step(Head(H - 3), 1)
            step(Head(H - 2), 0, more=1)
            step(Head(H - 1), 1, more=0)
            store_o(Head(H - 1), 1)
            for p in range(2):
                sp.wait_ge(o_stored[p], 64 * H)

        @block.gpsimd
        def _(pool):
            for p in range(2):
                nc.gpsimd.memset(kh[p][:], 1.0).then_inc(preset, 1)
                nc.gpsimd.memset(vh[p][:], 0.0).then_inc(preset, 1)
            pool.wait_ge(preset, 4)
            for p in range(2):
                nc.gpsimd.memset(vh[p][:, :, HD:HD + 1], 1.0).then_inc(preset, 1)
            nc.gpsimd.memset(mpart[:], -3.0e38).then_inc(preset, 1)
            nc.gpsimd.memset(mb[:], 0.0).then_inc(preset, 1)

            def lay_v(h, p):
                wait(pool, pv_done, (h - 1).count(NB))
                nc.gpsimd.tensor_copy(vh[p][:, :, 0:HD], g.V[:, :, bass.ds(h.count(HD), HD)]).then_inc(vh_ready, 1)

            pool.wait_ge(preset, 8)
            lay_v(Head(0), 0)
            lay_v(Head(1), 1)
            with nc.gpsimd.Fori(0, (H - 2) // 2) as i:
                lay_v(Head(2, i, 2), 0)
                lay_v(Head(3, i, 2), 1)

        @block.tensor
        def _(pe):
            def a_unit(h, p, n):
                if n == 0:
                    wait(pe, qk_loaded[p], h.turn(96, 96))
                    wait(pe, mT_ready, h.count(1))
                wait(pe, a_reduced, h.count(NA, held_since(n, 2, NA)))
                for qb, kb, nb, at in a_plan[n]:
                    ins = nc.tensor.matmul(psA[n % 2][:, at * P:(at + nb) * P], qh[p][0:QK_ROWS, qb * P:(qb + 1) * P],
                                           kh[p][0:QK_ROWS, kb * P:(kb + nb) * P], start=True,
                                           stop=not any(mask_of(kb + i, qb, True) for i in range(nb)),
                                           skip_group_check=True)
                    for i in range(nb):
                        m = mask_of(kb + i, qb, True)
                        if m is not None:
                            ins = nc.tensor.matmul(psA[n % 2][:, (at + i) * P:(at + i + 1) * P], g.identb[:], m[:],
                                                   start=False, stop=True, skip_group_check=True)
                ins.then_inc(a_scored, 1)

            def transpose_m(h):
                wait(pe, m_step, (h + 1).count(6))
                nc.tensor.transpose(psM, mb[:].rearrange("p a b -> p (a b)"), g.identb[:]).then_inc(mT_written, 1)

            def b_unit(h, p, u):
                if u == 0:
                    wait(pe, m_loaded, (h + 1).count(48))
                wait(pe, b_exped, h.count(NB, held_since(u, 2, NB)))
                for kb, qb, nb, at in b_plan[u]:
                    ins = nc.tensor.matmul(psB[u % 2][:, at * P:(at + nb) * P], kh[p][0:QKM_ROWS, kb * P:(kb + 1) * P],
                                           qh[p][0:QKM_ROWS, qb * P:(qb + nb) * P], start=True,
                                           stop=not any(mask_of(kb, qb + i, False) for i in range(nb)),
                                           skip_group_check=True)
                    for i in range(nb):
                        m = mask_of(kb, qb + i, False)
                        if m is not None:
                            ins = nc.tensor.matmul(psB[u % 2][:, (at + i) * P:(at + i + 1) * P], g.identb[:], m[:],
                                                   start=False, stop=True, skip_group_check=True)
                ins.then_inc(b_scored, 1)

            def pv(h, p, u):
                if u == 0:
                    wait(pe, vh_ready, (h + 1).count(1))
                    wait(pe, o_copied, (h - 1).count(1))
                wait(pe, b_exped, h.count(NB, u + 1))
                for kb, qb, nb, at in b_plan[u]:
                    c, q = qb // 4, qb % 4
                    ins = nc.tensor.matmul(psV[p][32 * c:32 * c + 32, q * P:(q + nb) * P], vh[p][:, kb, :],
                                           prob[u % 4][:, at * P:(at + nb) * P], start=(u, at) == first_of_chunk[c],
                                           stop=(u, at) == last_of_chunk[c], skip_group_check=True)
                ins.then_inc(pv_done, 1)

            def step(h, p, more=True):
                done = 0
                for u in range(NB):
                    quota = NA if u >= NB - 3 else NA * (u + 1) // (NB - 3)
                    while more and done < quota:
                        a_unit(h + 1, 1 - p, done)
                        done += 1
                    b_unit(h, p, u)
                    if u % 2 == 0 and u:
                        pv(h, p, u - 2)
                        pv(h, p, u - 1)
                    if more and u == NB - 2:
                        transpose_m(h + 1)
                for u in range((NB - 1) // 2 * 2, NB):
                    pv(h, p, u)

            pe.wait_ge(preset, 8)
            for n in range(NA):
                a_unit(Head(0), 0, n)
            transpose_m(Head(0))
            step(Head(0), 0)
            step(Head(1), 1)
            with nc.tensor.Fori(0, (H - 4) // 2) as i:
                step(Head(2, i, 2), 0)
                step(Head(3, i, 2), 1)
            step(Head(H - 2), 0)
            step(Head(H - 1), 1, more=False)

        @block.scalar
        def _(act):
            def copy_o(h, p):
                wait(act, pv_done, (h + 1).count(NB))
                wait(act, o_stored[p], h.turn(128))
                nc.scalar.activation(oh[p][:], psV[p][:], ACT.Copy).then_inc(o_copied, 1)

            def step(h, p, first=False):
                for u in range(NB):
                    wait(act, b_scored, h.count(NB, u + 1))
                    wait(act, pv_done, h.count(NB, held_since(u, 4, NB)))
                    n = sum(x[2] for x in b_plan[u]) * P
                    nc.scalar.activation(prob[u % 4][:, 0:n], psB[u % 2][:, 0:n], ACT.Exp, scale=scale).then_inc(b_exped, 1)
                    if u == 1 and not first:
                        copy_o(h - 1, 1 - p)

            step(Head(0), 0, first=True)
            step(Head(1), 1)
            step(Head(2), 0)
            with nc.scalar.Fori(0, (H - 4) // 2) as i:
                step(Head(3, i, 2), 1)
                step(Head(4, i, 2), 0)
            step(Head(H - 1), 1)
            copy_o(Head(H - 1), 1)

        @block.vector
        def _(dve):
            def maxima(h):
                for n in range(NA):
                    wait(dve, a_scored, h.count(NA, n + 1))
                    for qb, kb, nb, at in a_plan[n]:
                        k = part[n, at]
                        ins = nc.vector.tensor_reduce(mpart[:, qb, k:k + 1], psA[n % 2][:, at * P:(at + nb) * P],
                                                      AX.X, ALU.max)
                    ins.then_inc(a_reduced, 1)
                wait(dve, a_reduced, (h + 1).count(NA))
                step = [0]

                def chain(ins):
                    ins.then_inc(m_step, 1)
                    step[0] += 1
                    wait(dve, m_step, h.count(6, step[0]))

                chain(nc.vector.tensor_reduce(mrow[:], mpart[:], AX.X, ALU.max))
                chain(nc.vector.tensor_scalar(negm[:], mrow[:], -1.0, -M_FLOOR, ALU.mult, ALU.min))
                wait(dve, mT_written, h.count(1))
                chain(nc.vector.tensor_copy(mb[:, 0, :], negm[:]))
                chain(nc.vector.tensor_tensor(mrest[:], negm[:], mb[:, 0, :], ALU.subtract))
                chain(nc.vector.tensor_copy(mb[:, 1, :], mrest[:]))
                chain(nc.vector.tensor_tensor(mb[:, 2, :], mrest[:], mb[:, 1, :], ALU.subtract))
                wait(dve, mT_written, (h + 1).count(1))
                wait(dve, m_loaded, h.count(48))
                nc.vector.tensor_copy(mT[:], psM[0:3 * NT, :]).then_inc(mT_ready, 1)

            dve.wait_ge(preset, 8)
            maxima(Head(0))
            with nc.vector.Fori(0, H - 1) as i:
                maxima(Head(1, i, 1))
    st.close()


def attention_front(nc, g, name, wqT, wkT, wvT, bq=None, bk=None, bv=None, func=None, head_scales=None):
    st = Stage(nc, name)
    func = func or ACT.Identity
    w = st.sb("w", [P, 3, P])
    bqk = st.sb("bqk", [P, 2])
    bvr = st.sb("bvr", [P, P])
    qk = [st.sb(n, [P, S]) for n in ("qT", "kT")]
    parts = [[st.sb(f"part{n}{i}", [P, S], BF16) for i in range(3)] for n in ("q", "k")]
    rest = [st.sb(f"rest{n}", [P, S]) for n in ("q", "k")]
    psQ = [st.ps(f"psQ{i}") for i in range(4)]
    w_loaded, projected, qk_ready, v_projected, v_ready = (
        st.sem("w_loaded"), st.sem("projected"), st.sem("qk_ready"), st.sem("v_projected"), st.sem("v_ready"))
    part_step = [st.sem("q_part_step"), st.sem("k_part_step")]
    stored = st.sem("stored")
    zeroed = st.sem("zeroed")
    squared, norm2_ready, norm_ready, scaled, scale_step = (
        st.sem("squared"), st.sem("norm2_ready"), st.sem("norm_ready"), st.sem("scaled"), st.sem("scale_step"))
    has_bias = bq is not None
    nload = 3 + (3 if has_bias else 0) + (2 if head_scales else 0)
    nscale = 5
    if head_scales:
        hs = st.sb("hs", [P, 2])
        nrm = st.sb("nrm", [P, 2, S])
        dn = st.sb("dn", [P, S])

    def split(eng, e, which):
        sem, f, (p1, p2, p3), r = part_step[which], qk[which], parts[which], rest[which]
        if head_scales:
            eng.wait_ge(scaled, nscale * 2)
        else:
            eng.wait_ge(qk_ready, 2 * NC)
        e.tensor_copy(p1[:], f[:]).then_inc(sem, 1)
        eng.wait_ge(sem, 1)
        e.tensor_tensor(r[:], f[:], p1[:], ALU.subtract).then_inc(sem, 1)
        eng.wait_ge(sem, 2)
        e.tensor_copy(p2[:], r[:]).then_inc(sem, 1)
        eng.wait_ge(sem, 3)
        e.tensor_tensor(p3[:], r[:], p2[:], ALU.subtract).then_inc(sem, 1)

    with st.block() as block:
        @block.sync
        def _(sp):
            for i, a in enumerate((wqT, wkT, wvT)):
                sp.dma_start(w[:, i, :], a).then_inc(w_loaded, 16)
            if has_bias:
                sp.dma_start(bqk[:, 0:1], bq).then_inc(w_loaded, 16)
                sp.dma_start(bqk[:, 1:2], bk).then_inc(w_loaded, 16)
                sp.dma_start(bvr[:], bv).then_inc(w_loaded, 16)
            if head_scales:
                sp.dma_start(hs[:, 0:1], head_scales[0]).then_inc(w_loaded, 16)
                sp.dma_start(hs[:, 1:2], head_scales[1]).then_inc(w_loaded, 16)
            for i, after in enumerate((1, 3, 4)):
                for which, dram in ((0, g.qparts), (1, g.kparts)):
                    sp.wait_ge(part_step[which], after)
                    sp.dma_start(dram[i], parts[which][i][:]).then_inc(stored, 16)
            sp.wait_ge(stored, 96)

        @block.tensor
        def _(pe):
            pe.wait_ge(w_loaded, 16 * nload)
            for n in range(2 * NC):
                c, which = n // 2, n % 2
                if n >= 4:
                    pe.wait_ge(qk_ready, n - 3)
                nc.tensor.matmul(psQ[n % 4][:], w[:, which, :], g.XnT[:, c * CH:(c + 1) * CH],
                                 start=True, stop=True).then_inc(projected, 1)
            for t in range(NT):
                if t % 4 == 0:
                    pe.wait_ge(qk_ready, t // 4 + 5)
                nc.tensor.matmul(psQ[t // 4][:, t % 4 * P:(t % 4 + 1) * P], g.XnT[:, t * P:(t + 1) * P], w[:, 2, :],
                                 start=True, stop=True, skip_group_check=True).then_inc(v_projected, 1)
            if head_scales:
                for n in range(2 * NC):
                    c, which = n // 2, n % 2
                    pe.wait_ge(squared, which + 1)
                    if n >= 4:
                        pe.wait_ge(norm_ready, n - 3)
                    else:
                        pe.wait_ge(v_ready, n + 1)
                    nc.tensor.matmul(psQ[n % 4][:], g.blockdiag[:], rest[which][:, c * CH:(c + 1) * CH],
                                     start=True, stop=True).then_inc(norm2_ready, 1)

        @block.scalar
        def _(act):
            act.wait_ge(w_loaded, 16 * nload)
            act.wait_ge(zeroed, 1)
            for n in range(2 * NC):
                c, which = n // 2, n % 2
                act.wait_ge(projected, n + 1)
                nc.scalar.activation(qk[which][:, c * CH:(c + 1) * CH], psQ[n % 4][:], func,
                                     bias=bqk[:, which:which + 1]).then_inc(qk_ready, 1)
            for c in range(NC):
                act.wait_ge(v_projected, 4 * (c + 1))
                nc.scalar.activation(g.V[:, 4 * c:4 * c + 4, :].rearrange("p a b -> p (a b)"), psQ[c][:],
                                     func).then_inc(v_ready, 1)
            if head_scales:
                for n in range(2 * NC):
                    c, which = n // 2, n % 2
                    act.wait_ge(norm2_ready, n + 1)
                    nc.scalar.activation(nrm[:, which, c * CH:(c + 1) * CH], psQ[n % 4][:],
                                         ACT.Sqrt).then_inc(norm_ready, 1)

        @block.vector
        def _(dve):
            if not has_bias:
                nc.vector.memset(bqk[:], 0.0).then_inc(zeroed, 1)
            else:
                dve.wait_ge(w_loaded, 16 * nload)
                nc.vector.tensor_copy(bqk[:], bqk[:]).then_inc(zeroed, 1)
            if head_scales:
                dve.wait_ge(qk_ready, 2 * NC)
                for which in range(2):
                    nc.vector.tensor_tensor(rest[which][:], qk[which][:], qk[which][:], ALU.mult).then_inc(squared, 1)
                dve.wait_ge(norm_ready, 2 * NC)
                dve.wait_ge(norm2_ready, 2 * NC)
                n = [0]

                def chain(ins):
                    ins.then_inc(scaled, 1)
                    n[0] += 1
                    dve.wait_ge(scaled, n[0])
                for which in range(2):
                    f, r = qk[which], nrm[:, which, :]
                    chain(nc.vector.tensor_scalar(dn[:], r, 1e-6, None, ALU.add))
                    chain(nc.vector.reciprocal(dn[:], dn[:]))
                    chain(nc.vector.tensor_tensor(f[:], f[:], dn[:], ALU.mult))
                    chain(nc.vector.tensor_scalar(r, r, hs[:, which:which + 1], None, ALU.mult))
                    chain(nc.vector.tensor_tensor(f[:], f[:], r, ALU.mult))
            split(dve, nc.vector, 0)

        @block.gpsimd
        def _(pool):
            split(pool, nc.gpsimd, 1)
            if has_bias:
                pool.wait_ge(w_loaded, 16 * nload)
                pool.wait_ge(v_ready, NC)
                nc.gpsimd.tensor_tensor(g.V[:], g.V[:], bvr[:].unsqueeze(1).broadcast_to([P, NT, P]), ALU.add).then_inc(scale_step, 1)
    st.close()


def attention_normalise(nc, g, name):
    st = Stage(nc, name)
    den = st.sb("den", [H, S])
    psD = [st.ps(f"psD{i}") for i in range(4)]
    loaded, clamped, recip_ready, spread, ctx_ready = (
        st.sem("loaded"), st.sem("clamped"), st.sem("recip_ready"), st.sem("spread"), st.sem("ctx_ready"))
    with st.block() as block:
        @block.sync
        def _(sp):
            sp.dma_start(den[:], g.den_dram).then_inc(loaded, 16)
            sp.dma_start(g.CT[:], g.o_dram).then_inc(loaded, 16)

        @block.tensor
        def _(pe):
            pe.wait_ge(recip_ready, 1)
            for c in range(NC):
                nc.tensor.matmul(psD[c][:], g.expand[:], den[:, c * CH:(c + 1) * CH],
                                 start=True, stop=True).then_inc(spread, 1)

        @block.vector
        def _(dve):
            dve.wait_ge(loaded, 32)
            nc.vector.tensor_scalar(den[:], den[:], 1e-30, None, ALU.max).then_inc(clamped, 1)
            dve.wait_ge(clamped, 1)
            nc.vector.reciprocal(den[:], den[:]).then_inc(recip_ready, 1)
            for c in range(NC):
                dve.wait_ge(spread, c + 1)
                nc.vector.tensor_tensor(g.CT[:, c * CH:(c + 1) * CH], g.CT[:, c * CH:(c + 1) * CH], psD[c][:],
                                        ALU.mult).then_inc(ctx_ready, 1)
    st.close()


def project_add(nc, g, name, srcT, wT, bias_row=None, ntiles=1):
    st = Stage(nc, name)
    w = st.sb("w", [P, P])
    b = st.sb("b", [P, P])
    psO = [st.ps(f"psO{i}") for i in range(4)]
    loaded, projected, added, bias_added = st.sem("loaded"), st.sem("projected"), st.sem("added"), st.sem("bias_added")
    nload = (wT is not None) + (bias_row is not None)
    with st.block() as block:
        @block.sync
        def _(sp):
            if wT is not None:
                sp.dma_start(w[:], wT).then_inc(loaded, 16)
            if bias_row is not None:
                sp.dma_start(b[:], bias_row).then_inc(loaded, 16)

        @block.tensor
        def _(pe):
            if nload:
                pe.wait_ge(loaded, 16 * nload)
            for t in range(NT):
                o = psO[t // 4][:, t % 4 * P:(t % 4 + 1) * P]
                if wT is None:
                    ins = nc.tensor.transpose(o, srcT[:, t * P:(t + 1) * P], g.ident[:])
                else:
                    ins = nc.tensor.matmul(o, srcT[:, t * P:(t + 1) * P], w[:], start=True, stop=True,
                                           skip_group_check=True)
                ins.then_inc(projected, 1)

        @block.vector
        def _(dve):
            if bias_row is not None:
                dve.wait_ge(loaded, 16 * nload)
                nc.vector.tensor_tensor(g.X[:], g.X[:], b[:].unsqueeze(1).broadcast_to([P, NT, P]), ALU.add).then_inc(bias_added, 1)
                dve.wait_ge(bias_added, 1)
            for c in range(NC):
                dve.wait_ge(projected, 4 * (c + 1))
                x = g.X[:, 4 * c:4 * c + 4, :].rearrange("p a b -> p (a b)")
                nc.vector.tensor_tensor(x, x, psO[c][:], ALU.add).then_inc(added, 1)
    st.close()


NLAT = 64
LH = 4
LD = LH * HD
LCH = S // NLAT


def latent_mix(nc, g, a):
    st = Stage(nc, "latent")
    rq_w, rkv_w, rout_w = st.sb("rq_w", [P, LD]), st.sb("rkv_w", [P, 2 * LD]), st.sb("rout_w", [LD, P])
    rq_b, rk_b, rv_b, rout_b = st.sb("rq_b", [LD, 1]), st.sb("rk_b", [LD, 1]), st.sb("rv_b", [P, LD]), st.sb("rout_b", [P, 1])
    gcol = st.sb("gcol", [P, 2])
    gmat = st.sb("gmat", [P, 2, P])
    pooled = st.sb("pooled", [P, 2, NLAT])
    rqT = st.sb("rqT", [LD, S])
    rkT = st.sb("rkT", [LD, NLAT])
    rkd = st.sb("rkd", [LD, LH, NLAT])
    rvs = st.sb("rvs", [P, LD])
    rvmask = st.sb("rvmask", [P, 2, LD])
    rvd = st.sb("rvd", [P, 2, LD])
    lmask = st.sb("lmask", [P, 2 * NLAT])
    sc = st.sb("sc", [P, NT, LH, NLAT])
    mx, den = st.sb("mx", [P, NT * LH]), st.sb("den", [P, NT * LH])
    scT = st.sb("scT", [P, 2, S])
    latT = st.sb("latT", [LD, S])
    remT = st.sb("remT", [P, S])
    gate = st.sb("gate", [P, S])
    diff = st.sb("diff", [P, S])
    psA = [st.ps(f"psA{i}") for i in range(4)]
    psB = [st.ps(f"psB{i}") for i in range(4)]
    loaded, masks = st.sem("loaded"), st.sem("masks_built")
    pooled_ready, gmat_ready = st.sem("pooled_ready"), st.sem("gmat_ready")
    kv_projected, kv_ready, rq_projected, rq_ready = (
        st.sem("kv_projected"), st.sem("kv_ready"), st.sem("rq_projected"), st.sem("rq_ready"))
    diag_ready, scored, masked, soft = st.sem("diag_ready"), st.sem("scored"), st.sem("masked"), st.sem("soft_step")
    exped, transposed, t_copied, lat_done, lat_copied = (
        st.sem("exped"), st.sem("transposed"), st.sem("t_copied"), st.sem("lat_done"), st.sem("lat_copied"))
    rem_done, rem_ready, gate_done, gate_ready, mixed = (
        st.sem("rem_done"), st.sem("rem_ready"), st.sem("gate_done"), st.sem("gate_ready"), st.sem("mixed"))
    NL = 10
    with st.block() as block:
        @block.sync
        def _(sp):
            for dst, src in ((rq_w[:], a["L0_attn_rq_w"]), (rkv_w[:], a["L0_attn_rkv_w"]), (rout_w[:], a["L0_attn_rout_w"]),
                             (rq_b[:], a["L0_attn_rq_b"].unsqueeze(1)), (rk_b[:], a["L0_attn_rkv_b"][0:LD].unsqueeze(1)),
                             (rv_b[:], a["L0_attn_rkv_b"][LD:2 * LD].unsqueeze(0).broadcast_to([P, LD])),
                             (rout_b[:], a["L0_attn_rout_b"].unsqueeze(1)),
                             (gcol[:, 0:1], a["L0_attn_gl_w"].unsqueeze(0).broadcast_to([H, HD, 1])),
                             (gcol[:, 1:2], a["L0_attn_gr_w"].unsqueeze(0).broadcast_to([H, HD, 1]))):
                sp.dma_start(dst, src).then_inc(loaded, 16)

        @block.gpsimd
        def _(pool):
            nc.gpsimd.memset(lmask[:], 0.0).then_inc(masks, 1)
            nc.gpsimd.memset(rvmask[:], 0.0).then_inc(masks, 1)
            pool.wait_ge(masks, 2)
            nc.gpsimd.affine_select(out=lmask[:], in_=lmask[:], compare_op=ALU.is_ge, fill=NEG, base=(NLAT - 1) * LCH,
                                    pattern=[[-LCH, 2 * NLAT]], channel_multiplier=1).then_inc(masks, 1)
            for c in range(2):
                for half in range(2):
                    lo = (2 * c + half) * HD
                    pool.wait_ge(masks, 3 + 2 * c + half)
                    nc.gpsimd.memset(rvmask[64 * half:64 * half + 64, c, lo:lo + HD], 1.0).then_inc(masks, 1)

        @block.vector
        def _(dve):
            tt, ts = nc.vector.tensor_tensor, nc.vector.tensor_scalar
            nc.vector.tensor_reduce(diff[:, 0:NLAT], g.XnT[:].rearrange("p (l j) -> p l j", j=LCH), AX.X,
                                    ALU.add).then_inc(pooled_ready, 1)
            dve.wait_ge(pooled_ready, 1)
            for i in range(2):
                ts(pooled[:, i, :], diff[:, 0:NLAT], 1.0 / LCH, None, ALU.mult).then_inc(pooled_ready, 1)
            dve.wait_ge(loaded, 16 * 9)
            for i in range(2):
                ts(gmat[:, i, :], g.blockdiag[:], gcol[:, i:i + 1], None, ALU.mult).then_inc(gmat_ready, 1)
            dve.wait_ge(kv_ready, 1)
            tt(rkd[:], rkT[:].unsqueeze(1).broadcast_to([LD, LH, NLAT]),
               g.blockdiag[0:LD, 0:LD:HD].unsqueeze(2).broadcast_to([LD, LH, NLAT]), ALU.mult).then_inc(diag_ready, 1)
            dve.wait_ge(masks, 7)
            dve.wait_ge(kv_projected, 2)
            tt(rvs[:], psA[1][:, 0:LD], rv_b[:], ALU.add).then_inc(diag_ready, 1)
            dve.wait_ge(diag_ready, 2)
            for c in range(2):
                tt(rvd[:, c, :], rvs[:], rvmask[:, c, :], ALU.mult).then_inc(diag_ready, 1)
            for t in range(NT):
                dve.wait_ge(scored, t + 1)
                nc.vector.scalar_tensor_tensor(
                    out=sc[:, t, :, :], in0=psB[t % 4][:, 0:LH * NLAT].rearrange("p (h l) -> p h l", h=LH),
                    scalar=float(1.0 / np.sqrt(HD)),
                    in1=lmask[:, NLAT - 4 * t:2 * NLAT - 4 * t].unsqueeze(1).broadcast_to([P, LH, NLAT]),
                    op0=ALU.mult, op1=ALU.add).then_inc(masked, 1)
            dve.wait_ge(masked, NT)
            s3 = sc[:].rearrange("p t h l -> p (t h) l")

            def wide(x):
                return x[:].unsqueeze(2).broadcast_to([P, NT * LH, NLAT])
            nc.vector.tensor_reduce(mx[:], s3, AX.X, ALU.max).then_inc(soft, 1)
            dve.wait_ge(soft, 1)
            ts(mx[:], mx[:], M_FLOOR, None, ALU.max).then_inc(soft, 1)
            dve.wait_ge(soft, 2)
            tt(s3, s3, wide(mx), ALU.subtract).then_inc(soft, 1)
            dve.wait_ge(exped, 1)
            nc.vector.tensor_reduce(den[:], s3, AX.X, ALU.add).then_inc(soft, 1)
            dve.wait_ge(soft, 4)
            ts(den[:], den[:], 1e-30, None, ALU.max).then_inc(soft, 1)
            dve.wait_ge(soft, 5)
            nc.vector.reciprocal(den[:], den[:]).then_inc(soft, 1)
            dve.wait_ge(soft, 6)
            tt(s3, s3, wide(den), ALU.mult).then_inc(soft, 1)
            dve.wait_ge(rem_ready, NC)
            tt(diff[:], g.CT[:], remT[:], ALU.subtract).then_inc(mixed, 1)
            dve.wait_ge(mixed, 1)
            dve.wait_ge(gate_ready, NC)
            tt(diff[:], diff[:], gate[:], ALU.mult).then_inc(mixed, 1)
            dve.wait_ge(mixed, 2)
            tt(g.CT[:], diff[:], remT[:], ALU.add).then_inc(mixed, 1)

        @block.scalar
        def _(act):
            act.wait_ge(loaded, 16 * 9)
            act.wait_ge(kv_projected, 1)
            nc.scalar.activation(rkT[:], psA[0][0:LD, 0:NLAT], ACT.Identity, bias=rk_b[:]).then_inc(kv_ready, 1)
            for c in range(NC):
                act.wait_ge(rq_projected, c + 1)
                nc.scalar.activation(rqT[:, c * CH:(c + 1) * CH], psB[c][0:LD, :], ACT.Identity,
                                     bias=rq_b[:]).then_inc(rq_ready, 1)
            act.wait_ge(soft, 3)
            nc.scalar.activation(sc[:], sc[:], ACT.Exp).then_inc(exped, 1)
            for n in range(2 * NC):
                act.wait_ge(transposed, 4 * (n + 1))
                c, half = n // 2, n % 2
                nc.scalar.activation(scT[:, half, c * CH:(c + 1) * CH], psA[n % 4][:], ACT.Copy).then_inc(t_copied, 1)
            for c in range(NC):
                act.wait_ge(lat_done, c + 1)
                nc.scalar.activation(latT[:, c * CH:(c + 1) * CH], psB[c][0:LD, :], ACT.Copy).then_inc(lat_copied, 1)
            for c in range(NC):
                act.wait_ge(rem_done, c + 1)
                nc.scalar.activation(remT[:, c * CH:(c + 1) * CH], psA[c][:], ACT.Identity, bias=rout_b[:]).then_inc(rem_ready, 1)
            for c in range(NC):
                act.wait_ge(gate_done, c + 1)
                nc.scalar.activation(gate[:, c * CH:(c + 1) * CH], psB[c][:], ACT.Sigmoid).then_inc(gate_ready, 1)

        @block.tensor
        def _(pe):
            mm = nc.tensor.matmul
            pe.wait_ge(loaded, 16 * 9)
            pe.wait_ge(pooled_ready, 3)
            mm(psA[0][0:LD, 0:NLAT], rkv_w[:, 0:LD], pooled[:, 0, :], start=True, stop=True).then_inc(kv_projected, 1)
            mm(psA[1][:, 0:LD], pooled[:].rearrange("p a l -> p (a l)"), rkv_w[:, LD:2 * LD], start=True,
               stop=True).then_inc(kv_projected, 1)
            for c in range(NC):
                mm(psB[c][0:LD, :], rq_w[:], g.XnT[:, c * CH:(c + 1) * CH], start=True, stop=True).then_inc(rq_projected, 1)
            pe.wait_ge(diag_ready, 4)
            pe.wait_ge(rq_ready, NC)
            for t in range(NT):
                if t >= 4:
                    pe.wait_ge(masked, t - 3)
                mm(psB[t % 4][:, 0:LH * NLAT], rqT[:, t * P:(t + 1) * P], rkd[:].rearrange("p h l -> p (h l)"),
                   start=True, stop=True).then_inc(scored, 1)
            pe.wait_ge(soft, 7)
            pe.wait_ge(kv_ready, 1)
            for n in range(2 * NC):
                c, half = n // 2, n % 2
                if n >= 4:
                    pe.wait_ge(t_copied, n - 3)
                for i in range(4):
                    src = sc[:, 4 * c + i, 2 * half:2 * half + 2, :].rearrange("p h l -> p (h l)")
                    nc.tensor.transpose(psA[n % 4][:, i * P:(i + 1) * P], src, g.ident[:]).then_inc(transposed, 1)
            for c in range(NC):
                pe.wait_ge(t_copied, 2 * c + 2)
                for half in range(2):
                    ins = mm(psB[c][0:LD, :], rvd[:, half, :], scT[:, half, c * CH:(c + 1) * CH],
                             start=half == 0, stop=half == 1)
                ins.then_inc(lat_done, 1)
            pe.wait_ge(t_copied, 2 * NC)
            for c in range(NC):
                pe.wait_ge(lat_copied, c + 1)
                mm(psA[c][:], rout_w[:], latT[:, c * CH:(c + 1) * CH], start=True, stop=True).then_inc(rem_done, 1)
            pe.wait_ge(gmat_ready, 2)
            pe.wait_ge(lat_copied, NC)
            for c in range(NC):
                pe.wait_ge(rem_ready, c + 1)
                mm(psB[c][:], gmat[:, 0, :], g.CT[:, c * CH:(c + 1) * CH], start=True, stop=False)
                mm(psB[c][:], gmat[:, 1, :], remT[:, c * CH:(c + 1) * CH], start=False, stop=True).then_inc(gate_done, 1)
    st.close()


def col(ap):
    return ap.unsqueeze(1)


def bcast_row(ap, n=P):
    return ap.unsqueeze(0).broadcast_to([P, n])


def l0_attn(nc, g, a):
    layernorm_transpose(nc, g, "l0a_ln")
    w, b = a["L0_attn_qkv_w"], a["L0_attn_qkv_b"]
    attention_front(nc, g, "l0a_front", w[:, 0:P], w[:, P:2 * P], w[:, 2 * P:3 * P],
                    col(b[0:P]), col(b[P:2 * P]), bcast_row(b[2 * P:3 * P]))
    attention_core(nc, g, "l0a_core", "window", float(1.0 / np.sqrt(HD)))
    attention_normalise(nc, g, "l0a_norm")
    latent_mix(nc, g, a)
    project_add(nc, g, "l0a_out", g.CT, a["L0_attn_out_w"], bias_row=bcast_row(a["L0_attn_out_b"]))


def l1_attn(nc, g, a):
    layernorm_transpose(nc, g, "l1a_ln")
    attention_front(nc, g, "l1a_front", a["L1_attn_WqT"], a["L1_attn_WkT"], a["L1_attn_WvT"])
    attention_core(nc, g, "l1a_core", "full", float(1.0 / np.sqrt(np.float32(P))))
    attention_normalise(nc, g, "l1a_norm")
    project_add(nc, g, "l1a_out", g.CT, None)


def l2_attn(nc, g, a):
    layernorm_transpose(nc, g, "l2a_ln")
    scales = [a[n].unsqueeze(1).unsqueeze(2).broadcast_to([H, HD, 1]) for n in ("L2_attn_q_scale", "L2_attn_k_scale")]
    attention_front(nc, g, "l2a_front", a["L2_attn_WqT"], a["L2_attn_WkT"], a["L2_attn_WvT"],
                    func=ACT.Silu, head_scales=scales)
    attention_core(nc, g, "l2a_core", "causal", 1.0)
    attention_normalise(nc, g, "l2a_norm")
    project_add(nc, g, "l2a_out", g.CT, a["L2_attn_WoT"])


def router(nc, g, name, E, rw, rb=None, hidden=None):
    st = Stage(nc, name)
    rw_s, rb_s = st.sb("rw", [P, E]), st.sb("rb", [P, E])
    w1, b1 = st.sb("w1", [P, P]), st.sb("b1", [P, 1])
    hT = st.sb("hT", [P, S])
    L = st.sb("L", [P, NT, E])
    gt, eq = st.sb("gt", [P, NT, E, E]), st.sb("eq", [P, NT, E, E])
    tri = st.sb("tri", [P, E, E])
    rank, mx, den = st.sb("rank", [P, NT, E]), st.sb("mx", [P, NT]), st.sb("den", [P, NT])
    psH = [st.ps(f"psH{i}") for i in range(4)]
    psL = st.ps("psL")
    loaded, tri_built, hid_done, hid_ready, scored, step, exped, transposed, copied = (
        st.sem("loaded"), st.sem("tri_built"), st.sem("hid_done"), st.sem("hid_ready"), st.sem("scored"),
        st.sem("step"), st.sem("exped"), st.sem("transposed"), st.sem("copied"))
    loads = [(rw_s[:], rw)]
    if rb is not None:
        loads.append((rb_s[:], rb))
    if hidden is not None:
        loads += [(w1[:], hidden[0]), (b1[:], hidden[1])]
    NL = 16 * len(loads)
    with st.block() as block:
        @block.sync
        def _(sp):
            for d, s in loads:
                sp.dma_start(d, s).then_inc(loaded, 16)

        @block.gpsimd
        def _(pool):
            nc.gpsimd.memset(tri[:], 1.0).then_inc(tri_built, 1)
            pool.wait_ge(tri_built, 1)
            nc.gpsimd.affine_select(out=tri[:], in_=tri[:], compare_op=ALU.is_gt, fill=0.0, base=0,
                                    pattern=[[1, E], [-1, E]], channel_multiplier=0).then_inc(tri_built, 1)

        @block.tensor
        def _(pe):
            pe.wait_ge(loaded, NL)
            if hidden is not None:
                for c in range(NC):
                    nc.tensor.matmul(psH[c][:], w1[:], g.XnT[:, c * CH:(c + 1) * CH], start=True, stop=True).then_inc(hid_done, 1)
            src = hT if hidden is not None else g.XnT
            for t in range(NT):
                if hidden is not None:
                    pe.wait_ge(hid_ready, t // 4 + 1)
                nc.tensor.matmul(psL[:, t * E:(t + 1) * E], src[:, t * P:(t + 1) * P], rw_s[:], start=True, stop=True,
                                 skip_group_check=True).then_inc(scored, 1)
            pe.wait_ge(step, 12)
            if hidden is not None:
                pe.wait_ge(hid_ready, NC)
            for t in range(NT):
                nc.tensor.transpose(psH[t // 4][0:E, t % 4 * P:(t % 4 + 1) * P], g.W[:, t, 0:E], g.ident[:]).then_inc(transposed, 1)

        @block.scalar
        def _(act):
            if hidden is not None:
                act.wait_ge(loaded, NL)
                for c in range(NC):
                    act.wait_ge(hid_done, c + 1)
                    nc.scalar.activation(hT[:, c * CH:(c + 1) * CH], psH[c][:], ACT.Silu, bias=b1[:]).then_inc(hid_ready, 1)
            act.wait_ge(step, 8)
            nc.scalar.activation(L[:], L[:], ACT.Exp).then_inc(exped, 1)
            for c in range(NC):
                act.wait_ge(transposed, 4 * (c + 1))
                nc.scalar.activation(g.WT[0:E, c * CH:(c + 1) * CH], psH[c][0:E, :], ACT.Copy).then_inc(copied, 1)

        @block.vector
        def _(dve):
            n = [0]

            def chain(ins):
                ins.then_inc(step, 1)
                n[0] += 1
                dve.wait_ge(step, n[0])
            tt = nc.vector.tensor_tensor
            dve.wait_ge(scored, NT)
            dve.wait_ge(loaded, NL)
            ps = psL[:, 0:NT * E].rearrange("p (t e) -> p t e", e=E)
            if rb is not None:
                chain(tt(L[:], ps, rb_s[:].unsqueeze(1).broadcast_to([P, NT, E]), ALU.add))
            else:
                chain(nc.vector.tensor_copy(L[:], ps))
            other = L[:].unsqueeze(2).broadcast_to([P, NT, E, E])
            this = L[:].unsqueeze(3).broadcast_to([P, NT, E, E])
            dve.wait_ge(tri_built, 2)
            chain(tt(gt[:], other, this, ALU.is_gt))
            chain(tt(eq[:], other, this, ALU.is_equal))
            chain(tt(eq[:], eq[:], tri[:].unsqueeze(1).broadcast_to([P, NT, E, E]), ALU.mult))
            chain(tt(gt[:], gt[:], eq[:], ALU.add))
            chain(nc.vector.tensor_reduce(rank[:], gt[:], AX.X, ALU.add))
            chain(nc.vector.tensor_reduce(mx[:], L[:], AX.X, ALU.max))
            chain(tt(L[:], L[:], mx[:].unsqueeze(2).broadcast_to([P, NT, E]), ALU.subtract))
            dve.wait_ge(exped, 1)
            chain(nc.vector.scalar_tensor_tensor(out=g.W[:, :, 0:E], in0=rank[:], scalar=1.5, in1=L[:],
                                                 op0=ALU.is_lt, op1=ALU.mult))
            chain(nc.vector.tensor_reduce(den[:], g.W[:, :, 0:E], AX.X, ALU.add))
            chain(nc.vector.reciprocal(den[:], den[:]))
            chain(tt(g.W[:, :, 0:E], g.W[:, :, 0:E], den[:].unsqueeze(2).broadcast_to([P, NT, E]), ALU.mult))
    st.close()


def l1_experts(nc, g, a):
    E, HID = 8, 512
    J = HID // P
    st = Stage(nc, "l1e")
    w1, w2 = st.sb("w1", [P, E, HID]), st.sb("w2", [P, E, J, P])
    b1, b2 = st.sb("b1", [P, E, J]), st.sb("b2", [E, P])
    h = [st.sb(f"h{i}", [P, J, CH]) for i in range(2)]
    wc = st.sb("wc", [P, 4, E])
    psH = [st.ps(f"psH{i}") for i in range(4)]
    psO = [st.ps(f"psO{i}") for i in range(2)]
    loaded, hid_done, hid_ready, out_done, out_added, wc_ready = (
        st.sem("loaded"), st.sem("hid_done"), st.sem("hid_ready"), st.sem("out_done"), st.sem("out_added"), st.sem("wc_ready"))
    UH, UO = E * J, E + 1

    with st.block() as block:
        @block.sync
        def _(sp):
            for d, s in ((w1[:], a["L1_ffn_we1"].rearrange("e d h -> d e h")),
                         (w2[:], a["L1_ffn_we2"].rearrange("e (j p) d -> p e j d", p=P)),
                         (b1[:], a["L1_ffn_be1"].rearrange("e (j p) -> p e j", p=P)),
                         (b2[:], a["L1_ffn_be2"])):
                sp.dma_start(d, s, allow_slow_non_contiguous=True).then_inc(loaded, 16)

        @block.tensor
        def _(pe):
            def hid(c, e, xs):
                for j in range(J):
                    n = e * J + j
                    wait(pe, hid_ready, c.count(UH, n - 3))
                    nc.tensor.matmul(psH[j][:], w1[:, e, j * P:(j + 1) * P], xs, start=True, stop=True).then_inc(hid_done, 1)

            def outp(c, e):
                wait(pe, hid_ready, c.count(UH, e * J + J))
                wait(pe, out_added, c.count(UO, e - 1))
                for t in range(4):
                    for j in range(J):
                        ins = nc.tensor.matmul(psO[e % 2][:, t * P:(t + 1) * P], h[e % 2][:, j, t * P:(t + 1) * P],
                                               w2[:, e, j, :], start=j == 0, stop=j == J - 1, skip_group_check=True)
                ins.then_inc(out_done, 1)

            def chunk(c, xs, c_static):
                hid(c, 0, xs)
                for e in range(E):
                    if e + 1 < E:
                        hid(c, e + 1, xs)
                    outp(c, e)

            pe.wait_ge(loaded, 64)
            for c in range(NC):
                chunk(Head(c), g.XnT[:, c * CH:(c + 1) * CH], c)
                wait(pe, out_added, c * UO + E - 1)
                for t in range(4):
                    q = c * 4 + t
                    ins = nc.tensor.matmul(psO[0][:, t * P:(t + 1) * P], g.WT[0:E, q * P:(q + 1) * P], b2[:],
                                           start=True, stop=True, skip_group_check=True)
                ins.then_inc(out_done, 1)
                wait(pe, out_added, (c + 1) * UO)

        @block.scalar
        def _(act):
            act.wait_ge(loaded, 64)
            for c in range(NC):
                for e in range(E):
                    for j in range(J):
                        wait(act, hid_done, c * UH + e * J + j + 1)
                        if j == 0:
                            wait(act, out_done, c * UO + e - 1 if e >= 2 else c * UO)
                        nc.scalar.activation(h[e % 2][:, j, :], psH[j][:], ACT.Silu, bias=b1[:, e, j:j + 1]).then_inc(hid_ready, 1)

        @block.vector
        def _(dve):
            for c in range(NC):
                for e in range(E):
                    wait(dve, out_done, c * UO + e + 1)
                    if e + c:
                        wait(dve, out_added, c * UO + e)
                    for t in range(4):
                        q = 4 * c + t
                        ins = nc.vector.scalar_tensor_tensor(
                            out=g.X[:, q, :], in0=psO[e % 2][:, t * P:(t + 1) * P], scalar=g.W[:, q, e:e + 1],
                            in1=g.X[:, q, :], op0=ALU.mult, op1=ALU.add)
                    ins.then_inc(out_added, 1)
                wait(dve, out_done, (c + 1) * UO)
                wait(dve, out_added, c * UO + E)
                x = g.X[:, 4 * c:4 * c + 4, :].rearrange("p t d -> p (t d)")
                nc.vector.tensor_tensor(x, x, psO[0][:], ALU.add).then_inc(out_added, 1)
    st.close()


def l1_ffn(nc, g, a):
    keep = Stage(nc, "l1f_keep")
    xn = keep.sb("xn", [P, NT, P])
    layernorm_transpose(nc, g, "l1f_ln", keep_rows=xn)
    added = keep.sem("added")
    with keep.block() as block:
        @block.vector
        def _(dve):
            nc.vector.tensor_tensor(g.X[:], g.X[:], xn[:], ALU.add).then_inc(added, 1)
    keep.close()
    router(nc, g, "l1r", 8, a["L1_ffn_rw2"], rb=bcast_row(a["L1_ffn_rb2"], 8),
           hidden=(a["L1_ffn_rw1"], col(a["L1_ffn_rb1"])))
    l1_experts(nc, g, a)


def l3_experts(nc, g, a):
    E, I = 16, 64
    PR = E // 2
    ALPHA, LIMIT = 1.702, 7.0
    st = Stage(nc, "l3e")
    gu, gub = st.sb("gu", [P, E, 2 * I]), st.sb("gub", [P, PR, 2])
    dn, dnb = st.sb("dn", [P, PR, P]), st.sb("dnb", [E, P])
    sel = st.sb("sel", [E, PR, P])
    gate = [st.sb(f"gate{i}", [P, CH]) for i in range(2)]
    up = [st.sb(f"up{i}", [P, CH]) for i in range(2)]
    sg = [st.sb(f"sg{i}", [P, CH]) for i in range(2)]
    hs = [st.sb(f"hs{i}", [P, CH]) for i in range(2)]
    psG = [st.ps(f"psG{i}") for i in range(2)]
    psU = [st.ps(f"psU{i}") for i in range(2)]
    psS = [st.ps(f"psS{i}") for i in range(2)]
    psO = [st.ps(f"psO{i}") for i in range(2)]
    loaded, sel_built, in_done, gate_ready, up_ready, sig_ready, up1_ready, glu_ready, act_ready, h_ready, down_done, o_ready = (
        [st.sem(n) for n in ("loaded", "sel_built", "in_done", "gate_ready", "up_ready", "sig_ready", "up1_ready",
                             "glu_ready", "act_ready", "h_ready", "down_done", "o_ready")])
    units = [(c, r) for c in range(NC) for r in range(PR)]
    with st.block() as block:
        @block.sync
        def _(sp):
            for d, s in ((gu[:], a["L3_ffn_gate_up_proj"].rearrange("e d f -> d e f")),
                         (dn[:], a["L3_ffn_down_proj"].rearrange("(r e) i h -> (e i) r h", e=2)),
                         (dnb[:], a["L3_ffn_down_proj_bias"])):
                sp.dma_start(d, s).then_inc(loaded, 16)
            for r in range(PR):
                sp.dma_start(gub[:, r, :], a["L3_ffn_gate_up_proj_bias"][2 * r:2 * r + 2, :]
                             .rearrange("e (i g) -> (e i) g", g=2), allow_slow_non_contiguous=True).then_inc(loaded, 16)

        @block.gpsimd
        def _(pool):
            nc.gpsimd.memset(sel[:], 1.0).then_inc(sel_built, 1)
            pool.wait_ge(sel_built, 1)
            v = sel[:].rearrange("e r m -> e (r m)")
            nc.gpsimd.affine_select(out=v, in_=v, compare_op=ALU.is_ge, fill=0.0, base=0,
                                    pattern=[[1, PR * P]], channel_multiplier=-I).then_inc(sel_built, 1)
            pool.wait_ge(sel_built, 2)
            nc.gpsimd.affine_select(out=v, in_=v, compare_op=ALU.is_ge, fill=0.0, base=I - 1,
                                    pattern=[[-1, PR * P]], channel_multiplier=I).then_inc(sel_built, 1)
            for n in range(len(units)):
                b = n % 2
                pool.wait_ge(up_ready, n + 1)
                if n >= 2:
                    pool.wait_ge(h_ready, n - 1)
                pool.wait_ge(sig_ready, n + 1)
                nc.gpsimd.tensor_tensor(sg[b][:], sg[b][:], gate[b][:], ALU.mult).then_inc(glu_ready, 1)
                pool.wait_ge(glu_ready, n + 1)
                nc.gpsimd.tensor_tensor(sg[b][:], sg[b][:], up[b][:], ALU.mult).then_inc(act_ready, 1)

        @block.tensor
        def _(pe):
            mm = nc.tensor.matmul

            def inputs(n):
                c, r = units[n]
                xs = g.XnT[:, c * CH:(c + 1) * CH]
                w = gu[:, 2 * r:2 * r + 2, :].rearrange("p e f -> p (e f)")
                if n >= 2:
                    pe.wait_ge(gate_ready, n - 1)
                    pe.wait_ge(up_ready, n - 1)
                    pe.wait_ge(h_ready, n - 1)
                mm(psG[n % 2][:], w[:, 0::2], xs, start=True, stop=True)
                mm(psU[n % 2][:], w[:, 1::2], xs, start=True, stop=True)
                mm(psS[n % 2][:], sel[:, r, :], g.WT[:, c * CH:(c + 1) * CH], start=True, stop=True).then_inc(in_done, 1)

            def down(n):
                c, r = units[n]
                if r == 0:
                    if c >= 2:
                        pe.wait_ge(o_ready, c - 1)
                    mm(psO[c % 2][:], dnb[:], g.WT[:, c * CH:(c + 1) * CH], start=True, stop=False)
                pe.wait_ge(h_ready, n + 1)
                mm(psO[c % 2][:], dn[:, r, :], hs[n % 2][:], start=False, stop=r == PR - 1).then_inc(down_done, 1)

            pe.wait_ge(loaded, 16 * (3 + PR))
            pe.wait_ge(sel_built, 3)
            for n in range(len(units) + 1):
                if n < len(units):
                    inputs(n)
                if n:
                    down(n - 1)

        @block.scalar
        def _(act):
            for n in range(len(units)):
                c, r = units[n]
                act.wait_ge(gate_ready, n + 1)
                if n >= 2:
                    act.wait_ge(h_ready, n - 1)
                nc.scalar.activation(sg[n % 2][:], gate[n % 2][:], ACT.Sigmoid, scale=ALPHA).then_inc(sig_ready, 1)
                if r == PR - 1:
                    act.wait_ge(down_done, n + 1)
                    nc.scalar.activation(g.CT[:, c * CH:(c + 1) * CH], psO[c % 2][:], ACT.Copy).then_inc(o_ready, 1)

        @block.vector
        def _(dve):
            ts = nc.vector.tensor_scalar
            dve.wait_ge(loaded, 16 * (3 + PR))

            def times_score(n):
                dve.wait_ge(act_ready, n + 1)
                if n >= 2:
                    dve.wait_ge(down_done, n - 1)
                nc.vector.tensor_tensor(hs[n % 2][:], psS[n % 2][:], sg[n % 2][:], ALU.mult).then_inc(h_ready, 1)

            for n in range(len(units)):
                c, r = units[n]
                b = n % 2
                dve.wait_ge(in_done, n + 1)
                if n >= 2:
                    dve.wait_ge(act_ready, n - 1)
                ts(gate[b][:], psG[b][:], gub[:, r, 0:1], LIMIT, ALU.add, ALU.min).then_inc(gate_ready, 1)
                ts(up[b][:], psU[b][:], gub[:, r, 1:2], LIMIT, ALU.add, ALU.min).then_inc(up1_ready, 1)
                dve.wait_ge(up1_ready, n + 1)
                ts(up[b][:], up[b][:], -LIMIT, 1.0, ALU.max, ALU.add).then_inc(up_ready, 1)
                if n:
                    times_score(n - 1)
            times_score(len(units) - 1)
    st.close()


def l3_ffn(nc, g, a):
    layernorm_transpose(nc, g, "l3f_ln")
    router(nc, g, "l3r", 16, a["L3_ffn_router_weight"])
    l3_experts(nc, g, a)
    project_add(nc, g, "l3f_out", g.CT, None)


QB = 16
FF = 352
FB = FF // QB


class Fp4:
    ACT_STEPS, DVE_STEPS = 2, 14

    def __init__(self, st, name, blocks):
        self.n = blocks
        self.mag, self.sgn, self.acc = (st.sb(name + s, [P, blocks, QB]) for s in ("mag", "sgn", "acc"))
        self.scale, self.inv = st.sb(name + "scale", [P, blocks]), st.sb(name + "inv", [P, blocks])
        self.act_step, self.dve_step = st.sem(name + "act_step"), st.sem(name + "dve_step")

    def on_act(self, nc, x):
        nc.scalar.activation(self.mag[:], x, ACT.Abs).then_inc(self.act_step, 1)
        nc.scalar.activation(self.sgn[:], x, ACT.Sign).then_inc(self.act_step, 1)

    def on_dve(self, nc, dve, x, turn=0):
        count = [turn * self.DVE_STEPS]

        def chain(ins):
            ins.then_inc(self.dve_step, 1)
            count[0] += 1
            dve.wait_ge(self.dve_step, count[0])
        mag, acc = self.mag[:], self.acc[:]
        stt, tt, ts = nc.vector.scalar_tensor_tensor, nc.vector.tensor_tensor, nc.vector.tensor_scalar
        wide = self.scale[:].unsqueeze(2).broadcast_to([P, self.n, QB])
        dve.wait_ge(self.act_step, 2 * turn + 1)
        chain(nc.vector.tensor_reduce(self.scale[:], mag, AX.X, ALU.max))
        chain(ts(self.scale[:], self.scale[:], float(np.float32(1) / np.float32(6)), 1e-12, ALU.mult, ALU.max))
        chain(nc.vector.reciprocal(self.inv[:], self.scale[:]))
        chain(tt(mag, mag, self.inv[:].unsqueeze(2).broadcast_to([P, self.n, QB]), ALU.mult))
        chain(ts(acc, mag, 5.0, 2.0, ALU.is_gt, ALU.mult))
        chain(stt(out=acc, in0=mag, scalar=3.5, in1=acc, op0=ALU.is_gt, op1=ALU.add))
        chain(stt(out=acc, in0=mag, scalar=2.5, in1=acc, op0=ALU.is_gt, op1=ALU.add))
        chain(ts(acc, acc, 2.0, None, ALU.mult))
        for mid in (1.75, 1.25, 0.75, 0.25):
            chain(stt(out=acc, in0=mag, scalar=mid, in1=acc, op0=ALU.is_gt, op1=ALU.add))
        dve.wait_ge(self.act_step, 2 * turn + 2)
        chain(stt(out=acc, in0=acc, scalar=0.5, in1=self.sgn[:], op0=ALU.mult, op1=ALU.mult))
        chain(tt(x, acc, wide, ALU.mult))


def l0_ffn(nc, g, a):
    big = Stage(nc, "l0f")
    KC = ((0, P), (P, P), (2 * P, FF - 2 * P))
    wT = big.sb("wT", [P, 2, FF])
    dT = big.sb("dT", [P, 3, P])
    xn = big.sb("xn", [P, NT, P])
    layernorm_transpose(nc, g, "l0f_ln", keep_rows=xn)

    st = Stage(nc, "l0w")
    nb = 6 * (P // QB) + FB
    wr = st.sb("wr", [P, nb, QB])
    q = Fp4(st, "w", nb)
    qx = Fp4(st, "x", NT * P // QB)
    psT = [st.ps(f"psT{i}") for i in range(5)]
    zeroed, loaded, transposed, copied = st.sem("zeroed"), st.sem("loaded"), st.sem("transposed"), st.sem("copied")
    flat = wr[:].rearrange("p n q -> p (n q)")
    xb = xn[:].rearrange("p t (n q) -> p (t n) q", q=QB)
    with st.block() as block:
        @block.gpsimd
        def _(pool):
            nc.gpsimd.memset(wr[:], 0.0).then_inc(zeroed, 1)

        @block.sync
        def _(sp):
            sp.wait_ge(zeroed, 1)
            for i, n in enumerate(("L0_ffn_w_gate", "L0_ffn_w_up")):
                for k, (lo, m) in enumerate(KC):
                    sp.dma_start(flat[0:m, (3 * i + k) * P:(3 * i + k + 1) * P], a[n][lo:lo + m, :]).then_inc(loaded, 16)
            sp.dma_start(flat[:, 6 * P:6 * P + FF], a["L0_ffn_w_down"]).then_inc(loaded, 16)

        @block.scalar
        def _(act):
            act.wait_ge(loaded, 16 * 7)
            q.on_act(nc, wr[:])
            qx.on_act(nc, xb)
            for n in range(3):
                act.wait_ge(transposed, n + 1)
                if n < 2:
                    nc.scalar.activation(wT[:, n, :], psT[n][:, 0:FF], ACT.Copy).then_inc(copied, 1)
                else:
                    for k, (lo, m) in enumerate(KC):
                        nc.scalar.activation(dT[0:m, k, :], psT[2][0:m, k * P:(k + 1) * P], ACT.Copy).then_inc(copied, 1)
            for c in range(NC):
                act.wait_ge(transposed, 4 + c)
                if c >= 2:
                    act.wait_ge(copied, 5)
                nc.scalar.activation(g.XnT[:, c * CH:(c + 1) * CH], psT[3 + c % 2][:], ACT.Copy).then_inc(copied, 1)

        @block.vector
        def _(dve):
            q.on_dve(nc, dve, wr[:])
            qx.on_dve(nc, dve, xb)

        @block.tensor
        def _(pe):
            pe.wait_ge(q.dve_step, q.DVE_STEPS)
            for n in range(2):
                for k, (lo, m) in enumerate(KC):
                    ins = nc.tensor.transpose(psT[n][:, lo:lo + m], flat[0:m, (3 * n + k) * P:(3 * n + k + 1) * P], g.ident[0:m, 0:m])
                ins.then_inc(transposed, 1)
            for k, (lo, m) in enumerate(KC):
                ins = nc.tensor.transpose(psT[2][0:m, k * P:(k + 1) * P], flat[:, 6 * P + lo:6 * P + lo + m], g.ident[:])
            ins.then_inc(transposed, 1)
            pe.wait_ge(qx.dve_step, qx.DVE_STEPS)
            for c in range(NC):
                if c >= 2:
                    pe.wait_ge(copied, 6 + c - 2)
                for t in range(4 * c, 4 * c + 4):
                    ins = nc.tensor.transpose(psT[3 + c % 2][:, t % 4 * P:(t % 4 + 1) * P], xn[:, t, :], g.ident[:])
                ins.then_inc(transposed, 1)
    st.close()

    st = Stage(nc, "l0h")
    hid = [st.sb(f"hid{i}", [P, 4, FF]) for i in range(2)]
    sg = [st.sb(f"sg{i}", [P, FF]) for i in range(2)]
    qg = [Fp4(st, f"h{i}", 4 * FB) for i in range(2)]
    hT = [st.sb(f"hT{i}", [P, 3, CH]) for i in range(2)]
    psG = [st.ps(f"psG{i}") for i in range(2)]
    psU = [st.ps(f"psU{i}") for i in range(2)]
    psH = [st.ps(f"psH{i}") for i in range(3)]
    psO = st.ps("psO")
    in_done, silu_ready, hid_ready, transposed, copied, out_done, out_added = [st.sem(n) for n in (
        "in_done", "silu_ready", "hid_ready", "transposed", "copied", "out_done", "out_added")]
    with st.block() as block:
        @block.tensor
        def _(pe):
            def inputs(t):
                if t >= 2:
                    pe.wait_ge(hid_ready, t - 1)
                for ps, i in ((psG, 0), (psU, 1)):
                    ins = nc.tensor.matmul(ps[t % 2][:, 0:FF], g.XnT[:, t * P:(t + 1) * P], wT[:, i, :], start=True, stop=True)
                ins.then_inc(in_done, 1)

            def down(c):
                b = c % 2
                pe.wait_ge(qg[b].dve_step, qg[b].DVE_STEPS * (c // 2 + 1))
                for k, (lo, m) in enumerate(KC):
                    pe.wait_ge(copied, 3 * c + k - 2) if 3 * c + k - 2 > 0 else None
                    for t in range(4):
                        ins = nc.tensor.transpose(psH[k][0:m, t * P:(t + 1) * P], hid[b][:, t, lo:lo + m], g.ident[:])
                    ins.then_inc(transposed, 1)
                if c:
                    pe.wait_ge(out_added, c)
                pe.wait_ge(copied, 3 * c + 3)
                for t in range(4):
                    for k, (lo, m) in enumerate(KC):
                        ins = nc.tensor.matmul(psO[:, t * P:(t + 1) * P], hT[b][0:m, k, t * P:(t + 1) * P], dT[0:m, k, :],
                                               start=k == 0, stop=k == 2, skip_group_check=True)
                ins.then_inc(out_done, 1)

            for c in range(NC):
                for t in range(4 * c, 4 * c + 4):
                    inputs(t)
                if c:
                    down(c - 1)
            down(NC - 1)

        def evacuate(act, c):
            for k, (lo, m) in enumerate(KC):
                act.wait_ge(transposed, 3 * c + k + 1)
                if c >= 2:
                    act.wait_ge(out_done, c - 1)
                nc.scalar.activation(hT[c % 2][0:m, k, :], psH[k][0:m, :], ACT.Copy).then_inc(copied, 1)

        @block.scalar
        def _(act):
            for c in range(NC):
                b = c % 2
                for t in range(4 * c, 4 * c + 4):
                    act.wait_ge(in_done, t + 1)
                    if t >= 2:
                        act.wait_ge(hid_ready, t - 1)
                    nc.scalar.activation(sg[t % 2][:], psG[t % 2][:, 0:FF], ACT.Silu).then_inc(silu_ready, 1)
                act.wait_ge(hid_ready, 4 * c + 4)
                if c >= 2:
                    act.wait_ge(qg[b].dve_step, qg[b].DVE_STEPS * (c // 2))
                qg[b].on_act(nc, hid[b][:].rearrange("p t (n q) -> p (t n) q", q=QB))
                if c:
                    evacuate(act, c - 1)
            evacuate(act, NC - 1)

        @block.vector
        def _(dve):

            def add_out(c):
                dve.wait_ge(out_done, c + 1)
                x = g.X[:, 4 * c:4 * c + 4, :].rearrange("p t d -> p (t d)")
                nc.vector.tensor_tensor(x, x, psO[:], ALU.add).then_inc(out_added, 1)

            for c in range(NC):
                b = c % 2
                for t in range(4 * c, 4 * c + 4):
                    dve.wait_ge(silu_ready, t + 1)
                    if c >= 2:
                        dve.wait_ge(transposed, 3 * (c - 1))
                    nc.vector.tensor_tensor(hid[b][:, t % 4, :], sg[t % 2][:], psU[t % 2][:, 0:FF], ALU.mult).then_inc(hid_ready, 1)
                qg[b].on_dve(nc, dve, hid[b][:].rearrange("p t (n q) -> p (t n) q", q=QB), c // 2)
                if c:
                    add_out(c - 1)
            add_out(NC - 1)
    st.close()
    big.close()


def l3_attn(nc, g, a):
    DI, DS, NH, HP, TAPS = 256, 128, 4, 64, 4
    KT = (DI + 2 * DS) // P
    layernorm_transpose(nc, g, "l3a_ln")
    big = Stage(nc, "l3a")
    F = big.sb("F", [P, KT, S])
    zs = big.sb("zs", [P, NT, DI])
    dt = big.sb("dt", [P, NT, NH])
    ac, acs, tot = big.sb("ac", [P, NT, NH]), big.sb("acs", [P, NT, NH]), big.sb("tot", [P, NT, NH])
    decay = big.sb("decay", [P, NT, NH])
    incl, strict = big.sb("incl", [P, P]), big.sb("strict", [P, P])

    st = Stage(nc, "l3p")
    w = st.sb("w", [P, 2 * DI + 2 * DS + NH])
    cw, cb = st.sb("cw", [P, KT, TAPS]), st.sb("cb", [P, KT])
    U = st.sb("U", [P, KT, TAPS - 1 + S])
    acc = [st.sb(f"acc{i}", [P, S]) for i in range(2)]
    dtb, al = st.sb("dtb", [P, NH]), st.sb("al", [P, NH])
    raw, e, u, d, z0 = [st.sb(n, [P, NT, NH]) for n in ("raw", "e", "u", "d", "z0")]
    psC = [st.ps(f"psC{i}") for i in range(4)]
    psZ = [st.ps(f"psZ{i}") for i in range(2)]
    psD = st.ps("psD")
    loaded, u_zeroed, ch_done, u_ready, z_done, z_ready, conv_step, conv_ready, dt_done, sp_step, sp_act, sums_done, built = [
        st.sem(n) for n in ("loaded", "u_zeroed", "ch_done", "u_ready", "z_done", "z_ready", "conv_step", "conv_ready",
                            "dt_done", "sp_step", "sp_act", "sums_done", "built")]
    with st.block() as block:
        @block.sync
        def _(sp):
            for dst, src in ((w[:], a["L3_attn_in_proj_wT"]),
                             (cw[:], a["L3_attn_conv_w"].rearrange("(k p) j -> p k j", p=P)),
                             (cb[:], a["L3_attn_conv_b"].rearrange("(k p) -> p k", p=P)),
                             (dtb[:], bcast_row(a["L3_attn_dt_bias"], NH)), (al[:], bcast_row(a["L3_attn_A_log"], NH))):
                sp.dma_start(dst, src, allow_slow_non_contiguous=True).then_inc(loaded, 16)

        @block.gpsimd
        def _(pool):
            nc.gpsimd.memset(U[:, :, 0:TAPS - 1], 0.0).then_inc(u_zeroed, 1)
            nc.gpsimd.memset(incl[:], 1.0).then_inc(built, 1)
            nc.gpsimd.memset(strict[:], 1.0).then_inc(built, 1)
            pool.wait_ge(built, 2)
            nc.gpsimd.affine_select(out=incl[:], in_=incl[:], compare_op=ALU.is_ge, fill=0.0, base=0,
                                    pattern=[[1, P]], channel_multiplier=-1).then_inc(built, 1)
            nc.gpsimd.affine_select(out=strict[:], in_=strict[:], compare_op=ALU.is_gt, fill=0.0, base=0,
                                    pattern=[[-1, P]], channel_multiplier=1).then_inc(built, 1)

        @block.tensor
        def _(pe):
            pe.wait_ge(loaded, 80)
            for t in range(NT):
                nc.tensor.matmul(psD[:, t * NH:(t + 1) * NH], g.XnT[:, t * P:(t + 1) * P], w[:, 2 * DI + 2 * DS:],
                                 start=True, stop=True, skip_group_check=True).then_inc(dt_done, 1)
            for n in range(KT * NC):
                k, c = n // NC, n % NC
                if n >= 4:
                    pe.wait_ge(u_ready, n - 3)
                nc.tensor.matmul(psC[n % 4][:], w[:, DI + k * P:DI + (k + 1) * P], g.XnT[:, c * CH:(c + 1) * CH],
                                 start=True, stop=True).then_inc(ch_done, 1)
            for t in range(NT):
                if t >= 2:
                    pe.wait_ge(z_ready, t - 1)
                nc.tensor.matmul(psZ[t % 2][:, 0:DI], g.XnT[:, t * P:(t + 1) * P], w[:, 0:DI],
                                 start=True, stop=True).then_inc(z_done, 1)
            pe.wait_ge(sp_step, 12)
            pe.wait_ge(built, 4)
            ac2 = ac[:].rearrange("p t h -> p (t h)")
            nc.tensor.matmul(psC[0][:, 0:NT * NH], incl[:], ac2, start=True, stop=True).then_inc(sums_done, 1)
            nc.tensor.matmul(psC[1][:, 0:NT * NH], g.ones[:], ac2, start=True, stop=True).then_inc(sums_done, 1)

        @block.scalar
        def _(act):
            act.wait_ge(loaded, 80)
            act.wait_ge(sp_step, 2)
            nc.scalar.activation(e[:], d[:], ACT.Exp).then_inc(sp_act, 1)
            nc.scalar.activation(al[:], al[:], ACT.Exp).then_inc(sp_act, 1)
            act.wait_ge(sp_step, 3)
            nc.scalar.activation(z0[:], u[:], ACT.Ln).then_inc(sp_act, 1)
            for n in range(KT * NC):
                k, c = n // NC, n % NC
                act.wait_ge(ch_done, n + 1)
                nc.scalar.activation(U[:, k, TAPS - 1 + c * CH:TAPS - 1 + (c + 1) * CH], psC[n % 4][:],
                                     ACT.Copy).then_inc(u_ready, 1)
            for t in range(NT):
                act.wait_ge(z_done, t + 1)
                nc.scalar.activation(zs[:, t, :], psZ[t % 2][:, 0:DI], ACT.Silu).then_inc(z_ready, 1)
            for k in range(KT):
                act.wait_ge(conv_step, TAPS * (k + 1))
                nc.scalar.activation(F[:, k, :], acc[k % 2][:], ACT.Silu, bias=cb[:, k:k + 1]).then_inc(conv_ready, 1)
            act.wait_ge(sp_step, 15)
            nc.scalar.activation(decay[:], decay[:], ACT.Exp).then_inc(sp_act, 1)
            nc.scalar.activation(acs[:], acs[:], ACT.Exp).then_inc(sp_act, 1)
            nc.scalar.activation(tot[:], tot[:], ACT.Exp).then_inc(sp_act, 1)

        @block.vector
        def _(dve):
            n = [0]

            def chain(ins):
                ins.then_inc(sp_step, 1)
                n[0] += 1
                dve.wait_ge(sp_step, n[0])
            tt, ts, stt = nc.vector.tensor_tensor, nc.vector.tensor_scalar, nc.vector.scalar_tensor_tensor
            dve.wait_ge(dt_done, NT)
            dve.wait_ge(loaded, 80)
            chain(tt(raw[:], psD[:, 0:NT * NH].rearrange("p (t h) -> p t h", h=NH),
                     dtb[:].unsqueeze(1).broadcast_to([P, NT, NH]), ALU.add))
            chain(stt(out=d[:], in0=raw[:], scalar=-1.0, in1=raw[:], op0=ALU.mult, op1=ALU.min))
            dve.wait_ge(sp_act, 1)
            chain(ts(u[:], e[:], 1.0, None, ALU.add))
            chain(ts(d[:], u[:], -1.0, None, ALU.add))
            dve.wait_ge(sp_act, 3)
            chain(ts(u[:], d[:], 0.0, None, ALU.is_equal))
            chain(tt(d[:], d[:], u[:], ALU.add))
            chain(nc.vector.reciprocal(d[:], d[:]))
            chain(tt(d[:], d[:], z0[:], ALU.mult))
            chain(tt(d[:], d[:], u[:], ALU.add))
            chain(tt(d[:], d[:], e[:], ALU.mult))
            chain(stt(out=dt[:], in0=raw[:], scalar=0.0, in1=d[:], op0=ALU.max, op1=ALU.add))
            chain(stt(out=ac[:], in0=dt[:], scalar=-1.0, in1=al[:].unsqueeze(1).broadcast_to([P, NT, NH]),
                      op0=ALU.mult, op1=ALU.mult))
            dve.wait_ge(u_zeroed, 1)
            m = 0
            for k in range(KT):
                dve.wait_ge(u_ready, NC * (k + 1))
                if k >= 2:
                    dve.wait_ge(conv_ready, k - 1)
                for j in range(TAPS):
                    if j == 0:
                        ins = ts(acc[k % 2][:], U[:, k, 0:S], cw[:, k, 0:1], None, ALU.mult)
                    else:
                        ins = stt(out=acc[k % 2][:], in0=U[:, k, j:j + S], scalar=cw[:, k, j:j + 1], in1=acc[k % 2][:],
                                  op0=ALU.mult, op1=ALU.add)
                    ins.then_inc(conv_step, 1)
                    m += 1
                    dve.wait_ge(conv_step, m)
            dve.wait_ge(sums_done, 2)
            chain(nc.vector.tensor_copy(acs[:], psC[0][:, 0:NT * NH].rearrange("p (t h) -> p t h", h=NH)))
            chain(nc.vector.tensor_copy(tot[:], psC[1][:, 0:NT * NH].rearrange("p (t h) -> p t h", h=NH)))
            chain(tt(decay[:], tot[:], acs[:], ALU.subtract))
    st.close()

    st = Stage(nc, "l3c")
    R = [st.sb(f"R{i}", [P, NH, P]) for i in range(2)]
    E = [st.sb(f"E{i}", [P, NH, P]) for i in range(2)]
    cbm = [st.sb(f"cbm{i}", [P, P]) for i in range(2)]
    rows = [st.sb(f"rows{i}", [P, 3 * P]) for i in range(2)]
    xdt = [st.sb(f"xdt{i}", [P, NH, HP]) for i in range(2)]
    xdd = [st.sb(f"xdd{i}", [P, NH, HP]) for i in range(2)]
    yrow = st.sb("yrow", [P, NT, DI])
    state = [st.sb(f"state{i}", [P, NH, HP]) for i in range(2)]
    skip = st.sb("skip", [P, NH])
    ssq, rms = st.sb("ssq", [P, NT]), st.sb("rms", [P, NT])
    sqb = [st.sb(f"sqb{i}", [P, DI]) for i in range(2)]
    yT = st.sb("yT", [P, 2, S])
    ow, nw = st.sb("ow", [P, 2, P]), st.sb("nw", [P, 2])
    psB = [st.ps(f"psB{i}") for i in range(2)]
    psX = [st.ps(f"psX{i}") for i in range(2)]
    psG = [st.ps(f"psG{i}") for i in range(2)]
    psY = [st.ps(f"psY{i}") for i in range(2)]
    loaded, r_ready, pre_done, seg_done, cbm_ready, rows_ready, e_ready, m_ready, x_ready, y_done, s_done, s_step, y_step = [
        st.sem(n) for n in ("loaded", "r_ready", "pre_done", "seg_done", "cbm_ready", "rows_ready", "e_ready", "m_ready",
                            "x_ready", "y_done", "s_done", "s_step", "y_step")]
    YS = 5
    with st.block() as block:
        @block.sync
        def _(sp):
            sp.dma_start(skip[:], bcast_row(a["L3_attn_D"], NH)).then_inc(loaded, 16)
            sp.dma_start(ow[:], a["L3_attn_out_proj_wT"].rearrange("(k p) d -> p k d", p=P)).then_inc(loaded, 16)
            sp.dma_start(nw[:], a["L3_attn_norm_w"].rearrange("(k p) -> p k", p=P), allow_slow_non_contiguous=True).then_inc(loaded, 16)

        @block.gpsimd
        def _(pool):
            def ramp(c):
                if c >= 2:
                    pool.wait_ge(seg_done, c - 1)
                nc.gpsimd.tensor_tensor(R[c % 2][:], incl[:].unsqueeze(1).broadcast_to([P, NH, P]),
                                        ac[:, c, :].unsqueeze(2).broadcast_to([P, NH, P]), ALU.mult).then_inc(r_ready, 1)
            ramp(0)
            for c in range(NT):
                if c + 1 < NT:
                    ramp(c + 1)
                pool.wait_ge(e_ready, c + 1)
                pool.wait_ge(cbm_ready, c + 1)
                nc.gpsimd.tensor_tensor(E[c % 2][:], E[c % 2][:], cbm[c % 2][:].unsqueeze(1).broadcast_to([P, NH, P]),
                                        ALU.mult).then_inc(m_ready, 1)

        @block.tensor
        def _(pe):
            mm = nc.tensor.matmul

            def pre(c):
                b, cs = c % 2, slice(c * P, (c + 1) * P)
                if c >= 2:
                    pe.wait_ge(cbm_ready, c - 1)
                    pe.wait_ge(rows_ready, c - 1)
                    pe.wait_ge(s_step, 2 * c - 1)
                mm(psB[b][:, 0:P], F[:, 2, cs], F[:, 3, cs], start=True, stop=True)
                for k in range(3):
                    ins = nc.tensor.transpose(psX[b][:, k * P:(k + 1) * P], F[:, k, cs], g.ident[:])
                ins.then_inc(pre_done, 1)
                pe.wait_ge(r_ready, c + 1)
                if c >= 2:
                    pe.wait_ge(e_ready, c - 1)
                mm(psG[b][:], strict[:], R[b][:].rearrange("p h l -> p (h l)"), start=True, stop=True).then_inc(seg_done, 1)

            def post(c):
                b, cs = c % 2, slice(c * P, (c + 1) * P)
                pe.wait_ge(x_ready, 2 * c + 2)
                pe.wait_ge(rows_ready, c + 1)
                pe.wait_ge(cbm_ready, c + 1)
                mm(psB[b][:, P:P + DI], rows[b][:, 2 * P:3 * P], xdd[b][:].rearrange("p h d -> p (h d)"),
                   start=True, stop=True, skip_group_check=True).then_inc(s_done, 1)
                pe.wait_ge(m_ready, c + 1)
                if c >= 2:
                    pe.wait_ge(y_step, YS * (c - 1))
                for h in range(NH):
                    mm(psY[b][:, h * HP:(h + 1) * HP], E[b][:, h, :], xdt[b][:, h, :], start=True, stop=True,
                       skip_group_check=True)
                pe.wait_ge(s_step, 2 * c + 1)
                mm(psY[b][:, DI:2 * DI], F[:, 3, cs], state[b][:].rearrange("p h d -> p (h d)"),
                   start=True, stop=True, skip_group_check=True).then_inc(y_done, 1)

            pre(0)
            for c in range(NT):
                if c + 1 < NT:
                    pre(c + 1)
                post(c)

        @block.scalar
        def _(act):
            def rows_out(c):
                b = c % 2
                act.wait_ge(pre_done, c + 1)
                if c >= 2:
                    act.wait_ge(y_step, YS * (c - 1))
                    act.wait_ge(s_done, c - 1)
                nc.scalar.activation(rows[b][:], psX[b][:, 0:3 * P], ACT.Copy).then_inc(rows_ready, 1)
                act.wait_ge(seg_done, c + 1)
                if c >= 2:
                    act.wait_ge(y_done, c - 1)
                nc.scalar.activation(E[b][:].rearrange("p h l -> p (h l)"), psG[b][:], ACT.Exp).then_inc(e_ready, 1)
            for c in range(NT):
                rows_out(c)

        @block.vector
        def _(dve):
            tt, ts = nc.vector.tensor_tensor, nc.vector.tensor_scalar
            nc.vector.memset(state[0][:], 0.0).then_inc(s_step, 1)

            def wide(x, c):
                return x[:, c, :].unsqueeze(2).broadcast_to([P, NH, HP])

            def before(c):
                b = c % 2
                dve.wait_ge(pre_done, c + 1)
                if c >= 2:
                    dve.wait_ge(m_ready, c - 1)
                tt(cbm[b][:], psB[b][:, 0:P], incl[:], ALU.mult).then_inc(cbm_ready, 1)
                dve.wait_ge(rows_ready, c + 1)
                if c >= 2:
                    dve.wait_ge(y_done, c - 1)
                    dve.wait_ge(s_done, c - 1)
                x = rows[b][:, 0:DI].rearrange("p (h d) -> p h d", h=NH)
                tt(xdt[b][:], x, wide(dt, c), ALU.mult).then_inc(x_ready, 1)
                dve.wait_ge(x_ready, 2 * c + 1)
                tt(xdd[b][:], xdt[b][:], wide(decay, c), ALU.mult).then_inc(x_ready, 1)

            def after(c):
                b = c % 2
                dve.wait_ge(s_done, c + 1)
                dve.wait_ge(s_step, 2 * c + 1)
                if c:
                    dve.wait_ge(y_done, c)
                nxt = state[1 - b][:]
                tt(nxt, state[b][:], wide(tot, c), ALU.mult).then_inc(s_step, 1)
                dve.wait_ge(s_step, 2 * c + 2)
                tt(nxt, nxt, psB[b][:, P:P + DI].rearrange("p (h d) -> p h d", h=NH), ALU.add).then_inc(s_step, 1)
                dve.wait_ge(y_done, c + 1)
                y = yrow[:, c, :].rearrange("p (h d) -> p h d", h=NH)
                x = rows[b][:, 0:DI].rearrange("p (h d) -> p h d", h=NH)
                pw = psY[b][:, 0:DI].rearrange("p (h d) -> p h d", h=NH)
                pt = psY[b][:, DI:2 * DI].rearrange("p (h d) -> p h d", h=NH)
                if c == 0:
                    dve.wait_ge(loaded, 48)
                tt(y, pt, wide(acs, c), ALU.mult).then_inc(y_step, 1)
                dve.wait_ge(y_step, YS * c + 1)
                tt(y, y, pw, ALU.add).then_inc(y_step, 1)
                tt(x, x, skip[:].unsqueeze(2).broadcast_to([P, NH, HP]), ALU.mult).then_inc(y_step, 1)
                dve.wait_ge(y_step, YS * c + 3)
                tt(y, y, x, ALU.add).then_inc(y_step, 1)
                dve.wait_ge(y_step, YS * c + 4)
                tt(y, y, zs[:, c, :].rearrange("p (h d) -> p h d", h=NH), ALU.mult).then_inc(y_step, 1)

            before(0)
            for c in range(NT):
                if c + 1 < NT:
                    before(c + 1)
                after(c)
    st2 = Stage(nc, "l3o")
    scaled, squared, rms_step, t_done, t_ready, o_done, o_added = [
        st2.sem(n) for n in ("scaled", "squared", "rms_step", "t_done", "t_ready", "o_done", "o_added")]
    with st2.block() as block:
        @block.vector
        def _(dve):
            for k in range(2):
                nc.vector.tensor_scalar(ow[:, k, :], ow[:, k, :], nw[:, k:k + 1], None, ALU.mult).then_inc(scaled, 1)
            dve.wait_ge(rms_step, 1)
            nc.vector.reciprocal(rms[:], rms[:]).then_inc(rms_step, 1)
            dve.wait_ge(rms_step, 2)
            for t in range(NT):
                dve.wait_ge(o_done, t // 4 * 4 + 4)
                nc.vector.scalar_tensor_tensor(out=g.X[:, t, :], in0=psG[t // 4 % 2][:, t % 4 * P:(t % 4 + 1) * P],
                                               scalar=rms[:, t:t + 1], in1=g.X[:, t, :], op0=ALU.mult,
                                               op1=ALU.add).then_inc(o_added, 1)

        @block.tensor
        def _(pe):
            for n in range(2 * NC):
                k, c = n // NC, n % NC
                if n >= 4:
                    pe.wait_ge(t_ready, n - 3)
                for t in range(4 * c, 4 * c + 4):
                    ins = nc.tensor.transpose((psB + psX)[n % 4][:, t % 4 * P:(t % 4 + 1) * P], yrow[:, t, k * P:(k + 1) * P],
                                              g.ident[:])
                ins.then_inc(t_done, 1)
            pe.wait_ge(scaled, 2)
            for t in range(NT):
                pe.wait_ge(t_ready, NC + t // 4 + 1)
                if t % 4 == 0 and t >= 8:
                    pe.wait_ge(o_added, 4 * (t // 4 - 1))
                for k in range(2):
                    ins = nc.tensor.matmul(psG[t // 4 % 2][:, t % 4 * P:(t % 4 + 1) * P], yT[:, k, t * P:(t + 1) * P],
                                           ow[:, k, :], start=k == 0, stop=k == 1, skip_group_check=True)
                ins.then_inc(o_done, 1)

        @block.scalar
        def _(act):
            for t in range(NT):
                if t >= 2:
                    act.wait_ge(squared, t - 1)
                nc.scalar.activation(sqb[t % 2][:], yrow[:, t, :], ACT.Square, accum_out=ssq[:, t:t + 1]).then_inc(squared, 1)
            act.wait_ge(squared, NT)
            nc.scalar.activation(rms[:], ssq[:], ACT.Sqrt, bias=1e-5, scale=1.0 / DI).then_inc(rms_step, 1)
            for n in range(2 * NC):
                k, c = n // NC, n % NC
                act.wait_ge(t_done, n + 1)
                nc.scalar.activation(yT[:, k, c * CH:(c + 1) * CH], (psB + psX)[n % 4][:], ACT.Copy).then_inc(t_ready, 1)
    st2.close()
    st.close()
    big.close()


BH, BD = 8, 64
BI = BH * BD
BW = 64
FH = 341
F_CHUNKS = ((0, P), (P, P), (2 * P, FH - 2 * P))
MAGNIFY = 8.0


def rotary_tables():
    half = np.arange(0, BD, 2, dtype=np.float32)
    inv = (np.float32(1.0) / np.float32(10000.0) ** (half / np.float32(BD))).astype(np.float32)
    t = np.arange(S, dtype=np.float32)
    freqs = np.concatenate([t[:, None] * inv[None, :]] * 2, -1).astype(np.float32)
    base = ((half + np.float32(0.4 * BD)) / np.float32(1.4 * BD)).astype(np.float32)
    power = ((t - S // 2) / np.float32(BW // 2)).astype(np.float32)
    scale = np.concatenate([(base[None, :] ** power[:, None]).astype(np.float32)] * 2, -1)
    cos, sin = np.cos(freqs), np.sin(freqs)
    sign = np.concatenate([-np.ones(BD // 2), np.ones(BD // 2)]).astype(np.float32)
    out = np.stack([np.stack([cos * scale, sin * scale * sign], 1), np.stack([cos / scale, sin / scale * sign], 1)], 1)
    return np.ascontiguousarray(out.astype(np.float32).reshape(S, 4 * BD))


def shift_rows(nc, g, name, R, Hs):
    st = Stage(nc, name)
    zeroed, shifted, copied = st.sem("zeroed"), st.sem("shifted"), st.sem("copied")
    lo = P // 2
    with st.block() as block:
        @block.sync
        def _(sp):
            sp.dma_start(Hs[1:P, :, lo:P], R[0:P - 1, :, lo:P]).then_inc(shifted, 16)
            sp.dma_start(Hs[0:1, 1:NT, lo:P], R[P - 1:P, 0:NT - 1, lo:P]).then_inc(shifted, 16)
            sp.wait_ge(shifted, 32)

        @block.vector
        def _(dve):
            nc.vector.memset(Hs[0:1, 0, lo:P], 0.0).then_inc(zeroed, 1)
            nc.vector.tensor_copy(Hs[:, :, 0:lo], R[:, :, 0:lo]).then_inc(copied, 1)
    st.close()


def local_qkv(nc, g, name, w_dram, qs, ks, rot, qz, kT, V):
    st = Stage(nc, name)
    w = st.sb("w", [P, 3 * BI])
    tab = [st.sb(f"tab{i}", [P, 2, 2, BD]) for i in range(2)]
    gain = st.sb("gain", [P, 2, 2, BD])
    sq = st.sb("sq", [P, 2 * BH, BD])
    nrm = [st.sb(f"nrm{i}", [P, 2 * BH]) for i in range(2)]
    swp = [st.sb("swp", [P, 2 * BI])] * 2
    two = g.CT[:].rearrange("p (b n) -> p b n", b=2)
    tmp = g.V[:].rearrange("p t d -> p (t d)").rearrange("p (b n) -> p b n", b=2)
    psP = [st.ps(f"psP{i}", 3 * CH) for i in range(2)]
    psT = [st.ps(f"psT{i}") for i in range(2)]
    loaded, tab_loaded, tab_ready, q_zeroed = st.sem("loaded"), [st.sem("tab_loaded0"), st.sem("tab_loaded1")], st.sem("tab_ready"), st.sem("q_zeroed")
    projected, v_ready, qk_ready, squared, norm2_ready, norm_ready, norm_step, same_ready, rot_step, turned, q_out, k_out = [
        st.sem(n) for n in ("projected", "v_ready", "qk_ready", "squared", "norm2_ready", "norm_ready", "norm_step",
                            "same_ready", "rot_step", "turned", "q_out", "k_out")]

    def heads(x, b):
        return x[:, b, :].rearrange("p (h d) -> p h d", d=BD)

    with st.block() as block:
        @block.sync
        def _(sp):
            sp.dma_start(w[:], w_dram).then_inc(loaded, 16)
            for i, s in enumerate((qs, ks)):
                sp.dma_start(gain[:, i, 0, :], bcast_row(s, BD)).then_inc(loaded, 16)
                for lo in (0, BD // 2):
                    hi = BD // 2 - lo
                    sp.dma_start(gain[:, i, 1, lo:lo + BD // 2], bcast_row(s[hi:hi + BD // 2], BD // 2)).then_inc(loaded, 16)
            for t in range(NT):
                if t >= 2:
                    sp.wait_ge(rot_step, 4 * (t - 1))
                    sp.wait_ge(same_ready, t - 1)
                sp.dma_start(tab[t % 2][:].rearrange("p a b d -> p (a b d)"), rot[t * P:(t + 1) * P, :]).then_inc(tab_loaded[t % 2], 16)

        @block.tensor
        def _(pe):
            def project(t):
                if t >= 2:
                    pe.wait_ge(v_ready, t - 1)
                    pe.wait_ge(qk_ready, t - 1)
                    pe.wait_ge(squared, t - 1)
                for j in range(3):
                    ins = nc.tensor.matmul(psP[t % 2][:, j * BI:(j + 1) * BI], g.XnT[:, t * P:(t + 1) * P],
                                           w[:, j * BI:(j + 1) * BI], start=True, stop=True)
                ins.then_inc(projected, 1)

            def turn(t):
                pe.wait_ge(rot_step, 4 * (t + 1))
                for i in range(2):
                    if t:
                        pe.wait_ge((q_out, k_out)[i], (2 * t, t)[i])
                    for j in range(4):
                        ins = nc.tensor.transpose(psT[i][:, j * P:(j + 1) * P], tmp[:, t % 2, (4 * i + j) * P:(4 * i + j + 1) * P],
                                                  g.ident[:])
                    ins.then_inc(turned, 1)

            pe.wait_ge(loaded, 16 * 7)
            project(0)
            for t in range(NT):
                if t + 1 < NT:
                    project(t + 1)
                turn(t)

        @block.scalar
        def _(act):
            def outs(t):
                act.wait_ge(q_zeroed, 2)
                act.wait_ge(turned, 2 * t + 1)
                for half in range(2):
                    rows = slice(64 * half, 64 * half + 64)
                    nc.scalar.activation(qz[rows, half, :, t * P:(t + 1) * P],
                                         psT[0][rows, :].rearrange("p (j n) -> p j n", j=4), ACT.Copy).then_inc(q_out, 1)
                act.wait_ge(turned, 2 * t + 2)
                nc.scalar.activation(kT[:, :, t * P:(t + 1) * P], psT[1][:].rearrange("p (j n) -> p j n", j=4),
                                     ACT.Copy).then_inc(k_out, 1)

            for t in range(NT):
                act.wait_ge(projected, t + 1)
                if t >= 2:
                    act.wait_ge(rot_step, 4 * (t - 1))
                nc.scalar.activation(two[:, t % 2, :], psP[t % 2][:, 0:2 * BI], ACT.Copy).then_inc(qk_ready, 1)
                if t:
                    act.wait_ge(norm2_ready, t)
                nc.scalar.activation(sq[:].rearrange("p h d -> p (h d)"), psP[t % 2][:, 0:2 * BI], ACT.Square).then_inc(squared, 1)
                nc.scalar.activation(V[:, t, :], psP[t % 2][:, 2 * BI:3 * BI], ACT.Copy).then_inc(v_ready, 1)
                act.wait_ge(norm2_ready, t + 1)
                nc.scalar.activation(nrm[t % 2][:], nrm[t % 2][:], ACT.Sqrt).then_inc(norm_ready, 1)
                if t:
                    outs(t - 1)
            outs(NT - 1)

        @block.gpsimd
        def _(pool):
            nc.gpsimd.memset(qz[64:P, 0, :, :], 0.0).then_inc(q_zeroed, 1)
            pool.wait_ge(q_zeroed, 1)
            nc.gpsimd.memset(qz[0:64, 1, :, :], 0.0).then_inc(q_zeroed, 1)
            pool.wait_ge(q_zeroed, 2)
            pool.wait_ge(loaded, 16 * 7)
            for t in range(NT):
                b = t % 2
                pool.wait_ge(tab_loaded[b], 16 * (t // 2 + 1))
                nc.gpsimd.tensor_tensor(tab[b][:], tab[b][:], gain[:], ALU.mult).then_inc(tab_ready, 1)
                pool.wait_ge(tab_ready, t + 1)
                pool.wait_ge(norm_step, 3 * (t + 1))
                if t >= 2:
                    pool.wait_ge(turned, 2 * (t - 1))
                src = two[:, b, :].rearrange("p (a h d) -> p a h d", a=2, d=BD)
                dst = tmp[:, b, :].rearrange("p (a h d) -> p a h d", a=2, d=BD)
                nc.gpsimd.tensor_tensor(dst, src, tab[b][:, :, 0, :].unsqueeze(2).broadcast_to([P, 2, BH, BD]),
                                        ALU.mult).then_inc(same_ready, 1)

        @block.vector
        def _(dve):
            tt, ts = nc.vector.tensor_tensor, nc.vector.tensor_scalar
            for t in range(NT):
                b = t % 2
                n = nrm[b]
                dve.wait_ge(squared, t + 1)
                if t >= 2:
                    dve.wait_ge(norm_step, 3 * (t - 1))
                nc.vector.tensor_reduce(n[:], sq[:], AX.X, ALU.add).then_inc(norm2_ready, 1)
                dve.wait_ge(norm_ready, t + 1)
                ts(n[:], n[:], 1e-12, None, ALU.max).then_inc(norm_step, 1)
                dve.wait_ge(norm_step, 3 * t + 1)
                nc.vector.reciprocal(n[:], n[:]).then_inc(norm_step, 1)
                dve.wait_ge(norm_step, 3 * t + 2)
                dve.wait_ge(qk_ready, t + 1)
                tt(heads(two, b), heads(two, b), n[:].unsqueeze(2).broadcast_to([P, 2 * BH, BD]), ALU.mult).then_inc(norm_step, 1)
                dve.wait_ge(norm_step, 3 * t + 3)
                if t:
                    dve.wait_ge(rot_step, 4 * t)
                dve.wait_ge(tab_ready, t + 1)
                for half in range(2):
                    lo, hi = half * BD // 2, (1 - half) * BD // 2
                    for i in range(2):
                        src = two[:, b, i * BI:(i + 1) * BI].rearrange("p (h d) -> p h d", d=BD)[:, :, hi:hi + BD // 2]
                        dst = swp[b][:, i * BI:(i + 1) * BI].rearrange("p (h d) -> p h d", d=BD)[:, :, lo:lo + BD // 2]
                        ins = tt(dst, src, tab[b][:, i, 1, lo:lo + BD // 2].unsqueeze(1).broadcast_to([P, BH, BD // 2]), ALU.mult)
                    ins.then_inc(rot_step, 1)
                dve.wait_ge(rot_step, 4 * t + 2)
                dve.wait_ge(same_ready, t + 1)
                for i in range(2):
                    cols = slice(i * BI, (i + 1) * BI)
                    tt(tmp[:, b, cols], tmp[:, b, cols], swp[b][:, cols], ALU.add).then_inc(rot_step, 1)
    st.close()


def local_attention(nc, g, name, wo_dram, qz, kT, V, R):
    st = Stage(nc, name)
    wo = st.sb("wo", [P, 4, P])
    mask = [st.sb(f"mask{i}", [P, 2, 2 * P], BF16) for i in range(2)]
    nmx, den = [st.sb(f"nmx{i}", [P, 4]) for i in range(2)], [st.sb(f"den{i}", [P, BH]) for i in range(2)]
    raw = [st.sb(f"raw{i}", [P, 4]) for i in range(2)]
    prob = [g.CT[:, i * 2 * CH:(i + 1) * 2 * CH] for i in range(2)]
    gv = g.V[:].rearrange("p t d -> p (t d)")
    probT = [gv[:, i * 2 * CH:(i + 1) * 2 * CH] for i in range(2)]
    orow, oT = [st.sb(f"orow{i}", [P, BH, BD]) for i in range(2)], [st.sb(f"oT{i}", [P, BI]) for i in range(2)]
    psS = [st.ps(f"psS{i}", 2 * CH) for i in range(2)]
    psP = [st.ps(f"psP{i}") for i in range(2)]
    psO, psW = st.ps("psO"), st.ps("psW")
    loaded, built, scored, max_step, exped, p_turned, p_ready, pv_done, den_ready, o_ready, o_turned, oT_ready, w_done, added = [
        st.sem(n) for n in ("loaded", "built", "scored", "max_step", "exped", "p_turned", "p_ready", "pv_done", "den_ready",
                            "o_ready", "o_turned", "oT_ready", "w_done", "added")]
    NU = 2 * NT
    with st.block() as block:
        @block.sync
        def _(sp):
            sp.dma_start(wo[:], wo_dram.rearrange("(j p) d -> p j d", p=P)).then_inc(loaded, 16)

        @block.gpsimd
        def _(pool):
            n = [0]

            def chain(ins):
                ins.then_inc(built, 1)
                n[0] += 1
                pool.wait_ge(built, n[0])
            for i in range(2):
                chain(nc.gpsimd.memset(mask[i][:], 0.0))
                for h in range(2):
                    prev, cur = mask[i][:, h, 0:P], mask[i][:, h, P:2 * P]
                    if i == 0:
                        chain(nc.gpsimd.memset(prev, NEG))
                    else:
                        chain(nc.gpsimd.affine_select(out=prev, in_=prev, compare_op=ALU.is_ge, fill=NEG, base=-BW,
                                                      pattern=[[1, P]], channel_multiplier=-1))
                    chain(nc.gpsimd.affine_select(out=cur, in_=cur, compare_op=ALU.is_ge, fill=NEG, base=0,
                                                  pattern=[[-1, P]], channel_multiplier=1))
                    chain(nc.gpsimd.affine_select(out=cur, in_=cur, compare_op=ALU.is_ge, fill=NEG, base=BW,
                                                  pattern=[[1, P]], channel_multiplier=-1))

        def kb_range(t):
            return (0, 1) if t else (1,)

        @block.tensor
        def _(pe):
            mm = nc.tensor.matmul

            def score(n):
                t, half, ps = n // 2, n % 2, psS[n % 2]
                if n >= 2:
                    pe.wait_ge(exped, 4 * (n - 1))
                for j in range(2):
                    mm(ps[:, j * CH:(j + 1) * CH], g.identb[:], mask[min(t, 1)][:].rearrange("p a b -> p (a b)"),
                       start=True, stop=False, skip_group_check=True)
                    for i in range(2):
                        h = 4 * half + 2 * j + i
                        lo = 0 if t else P
                        ins = mm(ps[:, (2 * j + i) * 2 * P + lo:(2 * j + i + 1) * 2 * P], qz[:, h % 2, h // 2, t * P:(t + 1) * P],
                                 kT[:, h // 2, (t - 1) * P + lo:(t + 1) * P], start=False, stop=True, skip_group_check=True)
                ins.then_inc(scored, 1)

            def turn_p(n):
                t = n // 2
                pe.wait_ge(exped, 4 * (n + 1))
                for j in range(2):
                    if n:
                        pe.wait_ge(p_ready, 2 * n + j - 1)
                    for i in range(2):
                        for kb in range(2):
                            at = ((2 * j + i) * 2 + kb) * P
                            ins = nc.tensor.transpose(psP[j][:, (2 * i + kb) * P:(2 * i + kb + 1) * P], prob[n % 2][:, at:at + P], g.ident[:])
                    ins.then_inc(p_turned, 1)

            def pv(n):
                t, half = n // 2, n % 2
                if half == 0 and t:
                    pe.wait_ge(o_ready, t)
                pe.wait_ge(p_ready, 2 * (n + 1))
                for i in range(4):
                    h = 4 * half + i
                    kbs = kb_range(t)
                    for kb in kbs:
                        ins = mm(psO[:, h * BD:(h + 1) * BD], probT[n % 2][:, (2 * i + kb) * P:(2 * i + kb + 1) * P],
                                 V[:, t - 1 + kb, h * BD:(h + 1) * BD], start=kb == kbs[0], stop=kb == 1, skip_group_check=True)
                ins.then_inc(pv_done, 1)

            def turn_o(t):
                pe.wait_ge(o_ready, t + 1)
                if t:
                    pe.wait_ge(added, t)
                for j in range(4):
                    ins = nc.tensor.transpose(psW[:, j * P:(j + 1) * P],
                                              orow[t % 2][:, 2 * j:2 * j + 2, :].rearrange("p h d -> p (h d)"), g.ident[:])
                ins.then_inc(o_turned, 1)

            def project(t):
                pe.wait_ge(oT_ready, t + 1)
                for j in range(4):
                    ins = mm(psW[:, 0:P], oT[t % 2][:, j * P:(j + 1) * P], wo[:, j, :], start=j == 0, stop=j == 3)
                ins.then_inc(w_done, 1)

            pe.wait_ge(built, 14)
            pe.wait_ge(loaded, 16)
            score(0)
            for n in range(NU):
                t, half = n // 2, n % 2
                if n + 1 < NU:
                    score(n + 1)
                turn_p(n)
                if half == 0 and t:
                    turn_o(t - 1)
                pv(n)
                if half == 1 and t:
                    project(t - 1)
            turn_o(NT - 1)
            project(NT - 1)

        @block.scalar
        def _(act):
            def o_out(t):
                act.wait_ge(o_turned, t + 1)
                if t >= 2:
                    act.wait_ge(w_done, t - 1)
                nc.scalar.activation(oT[t % 2][:], psW[:], ACT.Copy).then_inc(oT_ready, 1)

            for n in range(NU):
                t, half = n // 2, n % 2
                act.wait_ge(max_step, 2 * (n + 1))
                if n >= 2:
                    act.wait_ge(p_turned, 2 * (n - 1))
                if half == 0 and t >= 2:
                    act.wait_ge(o_ready, t - 1)
                for i in range(4):
                    h = 4 * half + i
                    nc.scalar.activation(prob[n % 2][:, i * 2 * P:(i + 1) * 2 * P], psS[n % 2][:, i * 2 * P:(i + 1) * 2 * P],
                                         ACT.Exp, scale=MAGNIFY, bias=nmx[n % 2][:, i:i + 1],
                                         accum_out=den[t % 2][:, h:h + 1]).then_inc(exped, 1)
                if half == 1 and t:
                    o_out(t - 1)
            o_out(NT - 1)

        @block.vector
        def _(dve):
            def maxima(n):
                b = n % 2
                dve.wait_ge(scored, n + 1)
                if n >= 2:
                    dve.wait_ge(exped, 4 * (n - 1))
                nc.vector.tensor_reduce(raw[b][:], psS[b][:].rearrange("p (h k) -> p h k", h=4), AX.X, ALU.max).then_inc(max_step, 1)
                dve.wait_ge(max_step, 2 * n + 1)
                nc.vector.tensor_scalar(nmx[b][:], raw[b][:], -MAGNIFY, None, ALU.mult).then_inc(max_step, 1)

            def add_row(t):
                dve.wait_ge(w_done, t + 1)
                nc.vector.tensor_tensor(R[:, t, :], R[:, t, :], psW[:, 0:P], ALU.add).then_inc(added, 1)

            maxima(0)
            for n in range(NU):
                t, half = n // 2, n % 2
                if n + 1 < NU:
                    maxima(n + 1)
                for j in range(2):
                    dve.wait_ge(p_turned, 2 * n + j + 1)
                    if n >= 2:
                        dve.wait_ge(pv_done, n - 1)
                    nc.vector.tensor_copy(probT[n % 2][:, j * CH:(j + 1) * CH], psP[j][:]).then_inc(p_ready, 1)
                if half == 1:
                    d = den[t % 2]
                    dve.wait_ge(exped, 4 * (n + 1))
                    nc.vector.reciprocal(d[:], d[:]).then_inc(den_ready, 1)
                    dve.wait_ge(den_ready, t + 1)
                    dve.wait_ge(pv_done, n + 1)
                    if t >= 2:
                        dve.wait_ge(o_turned, t - 1)
                    nc.vector.tensor_tensor(orow[t % 2][:], psO[:].rearrange("p (h d) -> p h d", h=BH),
                                            d[:].unsqueeze(2).broadcast_to([P, BH, BD]), ALU.mult).then_inc(o_ready, 1)
                    if t:
                        add_row(t - 1)
            add_row(NT - 1)
    st.close()


def local_ffn(nc, g, name, w1_dram, b1_dram, w2_dram, b2_dram, R):
    st = Stage(nc, name)
    w1, w2 = st.sb("w1", [P, 2 * FH]), st.sb("w2", [P, 3, P])
    b1, b2 = st.sb("b1", [P, 2, 3]), st.sb("b2", [P, P])
    gl = [st.sb(f"gl{i}", [P, CH]) for i in range(2)]
    h = [st.sb(f"h{i}", [P, 3, CH]) for i in range(2)]
    psA = [st.ps(f"psA{i}") for i in range(2)]
    psG = [st.ps(f"psG{i}") for i in range(2)]
    psO = [st.ps(f"psO{i}") for i in range(2)]
    loaded, in_done, gelu_ready, h_ready, out_done, added = [st.sem(n) for n in (
        "loaded", "in_done", "gelu_ready", "h_ready", "out_done", "added")]
    units = [(c, k) for c in range(NC) for k in range(3)]
    with st.block() as block:
        @block.sync
        def _(sp):
            loads = [(w1[:], w1_dram), (b2[:], bcast_row(b2_dram))]
            for k, (lo, m) in enumerate(F_CHUNKS):
                loads.append((w2[0:m, k, :], w2_dram[lo:lo + m, :]))
                for i in range(2):
                    loads.append((b1[0:m, i, k:k + 1], col(b1_dram[i * FH + lo:i * FH + lo + m])))
            for d, s in loads:
                sp.dma_start(d, s).then_inc(loaded, 16)

        @block.tensor
        def _(pe):
            def inputs(n):
                c, k = units[n]
                lo, m = F_CHUNKS[k]
                if n >= 2:
                    pe.wait_ge(h_ready, n - 1)
                for i, ps in enumerate((psA, psG)):
                    ins = nc.tensor.matmul(ps[n % 2][0:m, :], w1[:, i * FH + lo:i * FH + lo + m], g.XnT[:, c * CH:(c + 1) * CH],
                                           start=True, stop=True)
                ins.then_inc(in_done, 1)

            def down(c):
                pe.wait_ge(h_ready, 3 * (c + 1))
                if c >= 2:
                    pe.wait_ge(added, c)
                for t in range(4):
                    for k, (lo, m) in enumerate(F_CHUNKS):
                        ins = nc.tensor.matmul(psO[c % 2][:, t * P:(t + 1) * P], h[c % 2][0:m, k, t * P:(t + 1) * P], w2[0:m, k, :],
                                               start=k == 0, stop=k == 2, skip_group_check=True)
                ins.then_inc(out_done, 1)

            pe.wait_ge(loaded, 16 * 11)
            for c in range(NC):
                for k in range(3):
                    inputs(3 * c + k)
                    if k == 1 and c:
                        down(c - 1)
            down(NC - 1)

        @block.scalar
        def _(act):
            act.wait_ge(loaded, 16 * 11)
            for n, (c, k) in enumerate(units):
                lo, m = F_CHUNKS[k]
                act.wait_ge(in_done, n + 1)
                if n >= 2:
                    act.wait_ge(h_ready, n - 1)
                nc.scalar.activation(gl[n % 2][0:m, :], psG[n % 2][0:m, :], ACT.Gelu, bias=b1[0:m, 1, k:k + 1]).then_inc(gelu_ready, 1)

        @block.vector
        def _(dve):
            dve.wait_ge(loaded, 16 * 11)
            nc.vector.tensor_tensor(R[:], R[:], b2[:].unsqueeze(1).broadcast_to([P, NT, P]), ALU.add).then_inc(added, 1)

            def add_rows(c):
                dve.wait_ge(out_done, c + 1)
                dve.wait_ge(added, c + 1)
                x = R[:, 4 * c:4 * c + 4, :].rearrange("p t d -> p (t d)")
                nc.vector.tensor_tensor(x, x, psO[c % 2][:], ALU.add).then_inc(added, 1)

            for n, (c, k) in enumerate(units):
                lo, m = F_CHUNKS[k]
                dve.wait_ge(gelu_ready, n + 1)
                if c >= 2:
                    dve.wait_ge(out_done, c - 1)
                nc.vector.scalar_tensor_tensor(out=h[c % 2][0:m, k, :], in0=psA[n % 2][0:m, :], scalar=b1[0:m, 0, k:k + 1],
                                               in1=gl[n % 2][0:m, :], op0=ALU.add, op1=ALU.mult).then_inc(h_ready, 1)
                if k == 2 and c:
                    add_rows(c - 1)
            add_rows(NC - 1)
    st.close()


def l2_ffn(nc, g, a):
    big = Stage(nc, "l2f")
    R = big.sb("R", [P, NT, P])
    layernorm_transpose(nc, g, "l2f_ln", keep_rows=R)
    for l in range(2):
        n = f"l2f{l}_"
        sh = Stage(nc, n + "sh")
        Hs = sh.sb("Hs", [P, NT, P])
        shift_rows(nc, g, n + "shift", R, Hs)
        layernorm_transpose(nc, g, n + "turn", normalise=False, src=Hs)
        sh.close()
        att = Stage(nc, n + "att")
        qz, kT, V = att.sb("qz", [P, 2, 4, S]), att.sb("kT", [P, 4, S]), att.sb("V", [P, NT, BI])
        local_qkv(nc, g, n + "qkv", a["L2_ffn_wqkv"][l], a["L2_ffn_q_scale"][l], a["L2_ffn_k_scale"][l], a["rotary"], qz, kT, V)
        local_attention(nc, g, n + "core", a["L2_ffn_wo"][l], qz, kT, V, R)
        att.close()
        sh = Stage(nc, n + "sh2")
        Hs = sh.sb("Hs", [P, NT, P])
        shift_rows(nc, g, n + "shift2", R, Hs)
        layernorm_transpose(nc, g, n + "norm", src=Hs, affine=(col(a["L2_ffn_ln_g"][l]), col(a["L2_ffn_ln_b"][l])))
        sh.close()
        local_ffn(nc, g, n + "ffn", a["L2_ffn_w1"][l], a["L2_ffn_b1"][l], a["L2_ffn_w2"][l], a["L2_ffn_b2"][l], R)
    added = big.sem("added")
    with big.block() as block:
        @block.vector
        def _(dve):
            nc.vector.tensor_tensor(g.X[:], g.X[:], R[:], ALU.add).then_inc(added, 1)
    big.close()


class Shared:
    pass


def build(nc, a, out, stages):
    g = Shared()
    ctx = ExitStack()
    g.out_stored = nc.alloc_semaphore(name="out_stored")

    def sb(name, shape, dt=F32):
        return ctx.enter_context(nc.sbuf_tensor(name, shape, dt))

    g.X = sb("X", [P, NT, P])
    g.XnT = sb("XnT", [P, S])
    g.V = sb("V", [P, NT, P])
    g.CT = sb("CT", [P, S])
    g.ident, g.identb, g.ones, g.blockdiag = sb("ident", [P, P]), sb("identb", [P, P], BF16), sb("ones", [P, P]), sb("blockdiag", [P, P])
    g.W, g.WT = sb("W", [P, NT, 16]), sb("WT", [16, S])
    g.expand = sb("expand", [H, P])
    g.cur_q, g.cur_k = sb("cur_q", [P, P], BF16), sb("cur_k", [P, P], BF16)
    g.prev_q, g.prev_k = sb("prev_q", [P, P], BF16), sb("prev_k", [P, P], BF16)
    g.caus_q, g.caus_k = sb("caus_q", [P, P], BF16), sb("caus_k", [P, P], BF16)
    g.qparts = nc.dram_tensor("qparts", [3, P, S], BF16, kind="Internal").ap()
    g.kparts = nc.dram_tensor("kparts", [3, P, S], BF16, kind="Internal").ap()
    g.o_dram = nc.dram_tensor("o_dram", [P, S], F32, kind="Internal").ap()
    g.den_dram = nc.dram_tensor("den_dram", [H, S], F32, kind="Internal").ap()
    build_constants(nc, g)
    load_tokens(nc, g, a["L0_attn_x"])
    for s in stages:
        STAGES[s](nc, g, a)
    store_tokens(nc, g, out)
    ctx.close()


STAGES = {"L0A": l0_attn, "L1A": l1_attn, "L2A": l2_attn, "L1F": l1_ffn, "L3F": l3_ffn, "L0F": l0_ffn, "L3A": l3_attn, "L2F": l2_ffn}


def kernel(**inputs):
    import numpy as _np
    import concourse.bacc as _bacc
    from concourse import mybir as _mybir
    from concourse.bass_utils import run_bass_kernel_spmd as _run

    nc = _bacc.Bacc("TRN2", target_bir_lowering=False, num_devices=1)
    arrays, aps = {}, {}
    for name, v in list(inputs.items()) + [("rotary", rotary_tables())]:
        v = _np.asarray(v)
        if name in TRANSPOSED:
            name, v = name + "T", v.T
        v = _np.ascontiguousarray(v)
        arrays[f"in_{name}"] = v
        aps[name] = nc.dram_tensor(f"in_{name}", v.shape, _mybir.dt.from_np(v.dtype), kind="ExternalInput").ap()
    out = nc.dram_tensor("out_0", (1, S, P), _mybir.dt.float32, kind="ExternalOutput").ap()
    build(nc, aps, out, RUN)
    r = _run(nc, [arrays], core_ids=[0])
    return r.results[0]["out_0"]


TRANSPOSED = ("L1_attn_Wq", "L1_attn_Wk", "L1_attn_Wv", "L2_attn_Wq", "L2_attn_Wk", "L2_attn_Wv", "L2_attn_Wo",
              "L3_attn_in_proj_w", "L3_attn_out_proj_w")
RUN = ["L0A", "L0F", "L1A", "L1F", "L2A", "L2F", "L3A", "L3F"]
```

```python
from contextlib import ExitStack

import numpy as np

import concourse.bass as bass
from concourse import mybir

F32 = mybir.dt.float32
BF16 = mybir.dt.bfloat16
ALU = mybir.AluOpType
ACT = mybir.ActivationFunctionType
AX = mybir.AxisListType

P = 128
S = 2048
NT = S // P
CH = 512
NC = S // CH
H = 16
HD = P // H
SEG = S * H // P
NEG = -1.0e30
M_FLOOR = -1.0e29
TERMS = 9
QK_ROWS = TERMS * HD
QKM_ROWS = QK_ROWS + 3


class Stage:

    def __init__(self, nc, name):
        self.nc, self.name, self.ctx, self.sems = nc, name, ExitStack(), []

    def sb(self, name, shape, dt=F32):
        return self.ctx.enter_context(self.nc.sbuf_tensor(f"{self.name}_{name}", shape, dt))

    def ps(self, name, cols=CH, dt=F32):
        return self.ctx.enter_context(self.nc.psum_tensor(f"{self.name}_{name}", [P, cols], dt))

    def sem(self, name):
        s = self.nc.alloc_semaphore(name=f"{self.name}_{name}")
        self.sems.append(s)
        return s

    def block(self):
        return self.nc.Block()

    def close(self):
        self.nc.clear_and_free_semaphores(self.sems)
        self.nc.all_engine_barrier()
        self.ctx.close()


class Head:

    def __init__(self, k, i=None, stride=0):
        self.k, self.i, self.stride = k, i, stride

    def __add__(self, n):
        return Head(self.k + n, self.i, self.stride)

    def __sub__(self, n):
        return self + -n

    def count(self, per_head, more=0):
        fixed = self.k * per_head + more
        return fixed if self.i is None else self.i * (self.stride * per_head) + fixed

    def turn(self, per_head, more=0):
        fixed = self.k // 4 * per_head + more
        return fixed if self.i is None else self.i * per_head + fixed


def wait(eng, sem, value):
    if isinstance(value, int) and value <= 0:
        return
    eng.wait_ge(sem, value)


def held_since(n, bufs, per_head):
    if n >= bufs:
        return n - bufs + 1
    last = max(m for m in range(per_head) if m % bufs == n % bufs)
    return last + 1 - per_head


def build_constants(nc, g):
    st = Stage(nc, "const")
    made = st.sem("made")
    count = [0]
    with st.block() as block:
        @block.gpsimd
        def _(pool):
            def chain(ins):
                ins.then_inc(made, 1)
                count[0] += 1
                pool.wait_ge(made, count[0])

            def fill(t, v):
                chain(nc.gpsimd.memset(t, v))

            def keep(t, op, base, cm, step, value, n=P):
                chain(nc.gpsimd.affine_select(out=t, in_=t, compare_op=op, fill=value, base=base,
                                              pattern=[[step, n]], channel_multiplier=cm))

            fill(g.ident[:], 0.0)
            keep(g.ident[:], ALU.not_equal, 0, 1, -1, 1.0)
            fill(g.identb[:], 0.0)
            keep(g.identb[:], ALU.not_equal, 0, 1, -1, 1.0)
            fill(g.ones[:], 1.0)
            fill(g.spread[:], 0.0)
            chain(nc.gpsimd.affine_select(out=g.spread[:].rearrange("p s (h d) -> p s h d", d=HD),
                                          in_=g.spread[:].rearrange("p s (h d) -> p s h d", d=HD),
                                          compare_op=ALU.not_equal, fill=1.0, base=0,
                                          pattern=[[-1, P // H], [-(P // H), H], [0, HD]], channel_multiplier=1))
            fill(g.blockdiag[:], 1.0)
            v = g.blockdiag[:].rearrange("p (h d) -> p h d", d=HD)
            for base, cm, step in ((0, 1, -HD), (HD - 1, -1, HD)):
                chain(nc.gpsimd.affine_select(out=v, in_=v, compare_op=ALU.is_ge, fill=0.0, base=base,
                                              pattern=[[step, H], [0, HD]], channel_multiplier=cm))
            for t in (g.cur_q, g.cur_k, g.prev_q, g.prev_k, g.caus_q, g.caus_k):
                fill(t[:], 0.0)
            keep(g.cur_q[:], ALU.is_gt, 0, 1, -1, NEG)
            keep(g.cur_k[:], ALU.is_gt, 0, -1, 1, NEG)
            keep(g.prev_q[:], ALU.is_ge, 0, -1, 1, NEG)
            keep(g.prev_q[:], ALU.is_ge, -1, 0, 1, NEG)
            keep(g.prev_k[:], ALU.is_ge, 0, 1, -1, NEG)
            keep(g.prev_k[:], ALU.is_ge, -1, 1, 0, NEG)
            keep(g.caus_q[:], ALU.is_ge, 0, 1, -1, NEG)
            keep(g.caus_k[:], ALU.is_ge, 0, -1, 1, NEG)
    st.close()


def load_tokens(nc, g, x):
    st = Stage(nc, "loadx")
    loaded = st.sem("loaded")
    with st.block() as block:
        @block.sync
        def _(sp):
            sp.dma_start(g.X[:], x[0].rearrange("(t p) d -> p t d", p=P)).then_inc(loaded, 16)
            sp.wait_ge(loaded, 16)
    st.close()


def store_tokens(nc, g, out):
    st = Stage(nc, "storex")
    stored = g.out_stored
    with st.block() as block:
        @block.sync
        def _(sp):
            sp.dma_start(out[0].rearrange("(t p) d -> p t d", p=P), g.X[:]).then_inc(stored, 16)
            sp.wait_ge(stored, 16)
    st.close()


def layernorm_transpose(nc, g, name, keep_rows=None, normalise=True, src=None, affine=None):
    st = Stage(nc, name)
    X = g.X if src is None else src
    stats = st.sb("stats", [P, NT, 6])
    mv = st.sb("mv", [P, NT, 2])
    std = st.sb("std", [P, NT])
    rstd = st.sb("rstd", [P, NT])
    xn = keep_rows if keep_rows is not None else (st.sb("xn", [P, NT, P]) if normalise else X)
    psT = [st.ps(f"psT{i}") for i in range(2)]
    stats_ready, moments_ready, std_ready, rstd_ready = (
        st.sem("stats_ready"), st.sem("moments_ready"), st.sem("std_ready"), st.sem("rstd_ready"))
    xn_ready, transposed, copied = st.sem("xn_ready"), st.sem("transposed"), st.sem("copied")
    gain = st.sb("gain", [P, 2])
    loaded = st.sem("loaded")
    with st.block() as block:
        @block.sync
        def _(sp):
            if affine is not None:
                for i in range(2):
                    sp.dma_start(gain[:, i:i + 1], affine[i]).then_inc(loaded, 16)

        @block.vector
        def _(dve):
            if not normalise:
                return
            for t in range(NT):
                nc.vector.bn_stats(stats[:, t, :], X[:, t, :]).then_inc(stats_ready, 1)
            for t in range(NT):
                dve.wait_ge(stats_ready, t + 1)
                nc.vector.bn_aggr(mv[:, t, :], stats[:, t, :]).then_inc(moments_ready, 1)
            dve.wait_ge(std_ready, 1)
            nc.vector.reciprocal(rstd[:], std[:]).then_inc(rstd_ready, 1)
            dve.wait_ge(rstd_ready, 1)
            for t in range(NT):
                nc.vector.tensor_scalar(xn[:, t, :], X[:, t, :], mv[:, t, 0:1], rstd[:, t:t + 1],
                                        ALU.subtract, ALU.mult).then_inc(xn_ready, 1)

        @block.scalar
        def _(act):
            if normalise:
                act.wait_ge(moments_ready, NT)
                nc.scalar.activation(std[:], mv[:, :, 1], ACT.Sqrt, bias=1e-5).then_inc(std_ready, 1)
            for c in range(NC):
                act.wait_ge(transposed, 4 * (c + 1))
                if affine is None:
                    ins = nc.scalar.activation(g.XnT[:, c * CH:(c + 1) * CH], psT[c % 2][:], ACT.Copy)
                else:
                    act.wait_ge(loaded, 32)
                    ins = nc.scalar.activation(g.XnT[:, c * CH:(c + 1) * CH], psT[c % 2][:], ACT.Identity,
                                               scale=gain[:, 0:1], bias=gain[:, 1:2])
                ins.then_inc(copied, 1)

        @block.tensor
        def _(pe):
            for t in range(NT):
                if normalise:
                    pe.wait_ge(xn_ready, t + 1)
                if t % 4 == 0 and t >= 8:
                    pe.wait_ge(copied, t // 4 - 1)
                nc.tensor.transpose(psT[t // 4 % 2][:, t % 4 * P:(t % 4 + 1) * P], xn[:, t, :],
                                    g.ident[:]).then_inc(transposed, 1)
    st.close()


def score_pieces(blocks, per_bank, same_chunk):
    out = []
    for i, (r, c) in enumerate(blocks):
        if out and i % per_bank and out[-1][0] == r and out[-1][1] + out[-1][2] == c and not (
                same_chunk and c % 4 == 0):
            out[-1][2] += 1
        else:
            out.append([r, c, 1, i])
    return out


def attention_plan(kind):
    def keys(qb):
        return {"full": range(NT), "causal": range(qb + 1), "window": range(max(qb - 1, 0), qb + 1)}[kind]
    by_query = [(qb, kb) for qb in range(NT) for kb in keys(qb)]
    by_key = [(kb, qb) for kb in range(NT) for qb in range(NT) if kb in keys(qb)]
    a = [score_pieces(by_query[i:i + 4], 4, False) for i in range(0, len(by_query), 4)]
    b = [score_pieces(by_key[i:i + 8], 4, True) for i in range(0, len(by_key), 8)]
    return a, b


def attention_core(nc, g, name, kind, scale, ahead, pair_at):
    a_plan, b_plan = attention_plan(kind)
    NA, NB = len(a_plan), len(b_plan)
    LEAD = max(2, round(NA * ahead))
    LEAD = max(2, round(NA * ahead))
    st = Stage(nc, name)
    qh = [st.sb(f"qh{i}", [P, S], BF16) for i in range(4)]
    kh = [st.sb(f"kh{i}", [P, S], BF16) for i in range(4)]
    vh = [st.sb(f"vh{i}", [P, NT, 32]) for i in range(2)]
    prob = [st.sb(f"prob{i}", [P, 2 * CH]) for i in range(4)]
    oh = [st.sb(f"oh{i}", [P, CH]) for i in range(4)]
    npart = 5
    mpart = st.sb("mpart", [P, NT, npart])
    mrow = st.sb("mrow", [P, NT])
    negm = st.sb("negm", [P, NT])
    mrest = st.sb("mrest", [P, NT])
    mb = st.sb("mb", [P, P // NT, NT], BF16)
    mT = st.sb("mT", [3 * NT, P], BF16)
    psA = [st.ps(f"psA{i}") for i in range(3)]
    psB = [st.ps(f"psB{i}", 2 * CH) for i in range(2)]
    psV = st.ps("psV")
    psM = psA[0][:].bitcast(BF16)[:, 0:P]

    preset = st.sem("preset")
    qk_loaded = [st.sem(f"qk_loaded{i}") for i in range(4)]
    vh_ready = st.sem("vh_ready")
    a_scored = st.sem("a_scored")
    a_reduced = st.sem("a_reduced")
    m_step = st.sem("m_step")
    mT_written = st.sem("mT_written")
    mT_ready = st.sem("mT_ready")
    m_loaded = st.sem("m_loaded")
    b_scored = st.sem("b_scored")
    b_exped = st.sem("b_exped")
    pv_done = st.sem("pv_done")
    o_copied = st.sem("o_copied")
    o_stored = [st.sem(f"o_stored{i}") for i in range(4)]

    def mask_of(kb, qb, by_query):
        if kind == "causal" and kb == qb:
            return g.caus_q if by_query else g.caus_k
        if kind == "window":
            if kb == qb:
                return g.cur_q if by_query else g.cur_k
            return g.prev_q if by_query else g.prev_k
        return None

    part = {}
    seen = [0] * NT
    for n, pieces in enumerate(a_plan):
        for qb, kb, nb, at in pieces:
            part[n, at] = seen[qb]
            seen[qb] += 1
    assert max(seen) <= npart
    last_of_chunk = {}
    for u, pieces in enumerate(b_plan):
        for kb, qb, nb, at in pieces:
            last_of_chunk[qb // 4] = (u, at)
    first_of_chunk = {}
    for u, pieces in reversed(list(enumerate(b_plan))):
        for kb, qb, nb, at in reversed(pieces):
            first_of_chunk[qb // 4] = (u, at)

    with st.block() as block:
        @block.sync
        def _(sp):
            def load_qk(h):
                b = h.k % 4
                wait(sp, pv_done, (h - 3).count(NB))
                for i in range(3):
                    lo = 3 * HD * i
                    sp.dma_start(kh[b][lo:lo + 3 * HD, :], g.kparts[:, bass.ds(h.count(HD), HD), :]).then_inc(qk_loaded[b], 16)
                    sp.dma_start(qh[b][lo:lo + 3 * HD, :], g.qparts[i:i + 1, bass.ds(h.count(HD), HD), :]
                                 .broadcast_to([3, HD, S])).then_inc(qk_loaded[b], 16)

            def load_m(h):
                wait(sp, mT_ready, (h + 1).count(1))
                for i in range(3):
                    sp.dma_start(qh[h.k % 4][QK_ROWS + i:QK_ROWS + i + 1, :].rearrange("o (t j) -> o t j", j=P),
                                 mT[i * NT:(i + 1) * NT, :]).then_inc(m_loaded, 16)

            def store_o(h):
                b = h.k % 4
                wait(sp, o_copied, (h + 1).count(1))
                for c in range(NC):
                    sp.dma_start(g.o_dram[bass.ds(h.count(HD), HD), c * CH:(c + 1) * CH],
                                 oh[b][32 * c:32 * c + HD, :]).then_inc(o_stored[b], 16)
                    sp.dma_start(g.den_dram[bass.ds(h.count(1), 1), c * CH:(c + 1) * CH],
                                 oh[b][32 * c + HD:32 * c + HD + 1, :]).then_inc(o_stored[b], 16)

            def step(h, has_m=True, has_qk=True, has_o=True):
                if has_m:
                    load_m(h + 1)
                if has_qk:
                    load_qk(h + 3)
                if has_o:
                    store_o(h - 1)

            sp.wait_ge(preset, 10)
            for h in range(3):
                load_qk(Head(h))
            load_m(Head(0))
            for h in range(4):
                step(Head(h), has_o=h > 0)
            with nc.sync.Fori(0, (H - 8) // 4) as i:
                for k in range(4, 8):
                    step(Head(k, i, 4))
            for h in range(H - 4, H):
                step(Head(h), has_m=h < H - 1, has_qk=h < H - 3)
            store_o(Head(H - 1))
            for b in range(4):
                sp.wait_ge(o_stored[b], 128 * H // 4)

        @block.gpsimd
        def _(pool):
            for b in range(4):
                nc.gpsimd.memset(kh[b][:], 1.0).then_inc(preset, 1)
            for p in range(2):
                nc.gpsimd.memset(vh[p][:], 0.0).then_inc(preset, 1)
            pool.wait_ge(preset, 6)
            for p in range(2):
                nc.gpsimd.memset(vh[p][:, :, HD:HD + 1], 1.0).then_inc(preset, 1)
            nc.gpsimd.memset(mpart[:], -3.0e38).then_inc(preset, 1)
            nc.gpsimd.memset(mb[:], 0.0).then_inc(preset, 1)

            def lay_v(h):
                wait(pool, pv_done, (h - 1).count(NB))
                nc.gpsimd.tensor_copy(vh[h.k % 2][:, :, 0:HD], g.V[:, :, bass.ds(h.count(HD), HD)]).then_inc(vh_ready, 1)

            pool.wait_ge(preset, 10)
            lay_v(Head(0))
            lay_v(Head(1))
            with nc.gpsimd.Fori(0, (H - 2) // 2) as i:
                lay_v(Head(2, i, 2))
                lay_v(Head(3, i, 2))

        @block.tensor
        def _(pe):
            def a_unit(h, n):
                b = h.k % 4
                if n == 0:
                    wait(pe, qk_loaded[b], h.turn(96, 96))
                    wait(pe, mT_ready, h.count(1))
                wait(pe, a_reduced, h.count(NA, held_since(n, 3, NA)))
                for qb, kb, nb, at in a_plan[n]:
                    ins = nc.tensor.matmul(psA[n % 3][:, at * P:(at + nb) * P], qh[b][0:QK_ROWS, qb * P:(qb + 1) * P],
                                           kh[b][0:QK_ROWS, kb * P:(kb + nb) * P], start=True,
                                           stop=not any(mask_of(kb + i, qb, True) for i in range(nb)),
                                           skip_group_check=True)
                    for i in range(nb):
                        m = mask_of(kb + i, qb, True)
                        if m is not None:
                            ins = nc.tensor.matmul(psA[n % 3][:, (at + i) * P:(at + i + 1) * P], g.identb[:], m[:],
                                                   start=False, stop=True, skip_group_check=True)
                ins.then_inc(a_scored, 1)

            def transpose_m(h):
                wait(pe, m_step, (h + 1).count(6))
                nc.tensor.transpose(psM, mb[:].rearrange("p a b -> p (a b)"), g.identb[:]).then_inc(mT_written, 1)

            def b_unit(h, u):
                b = h.k % 4
                if u == 0:
                    wait(pe, m_loaded, (h + 1).count(48))
                wait(pe, b_exped, h.count(NB, held_since(u, 2, NB)))
                for kb, qb, nb, at in b_plan[u]:
                    ins = nc.tensor.matmul(psB[u % 2][:, at * P:(at + nb) * P], kh[b][0:QKM_ROWS, kb * P:(kb + 1) * P],
                                           qh[b][0:QKM_ROWS, qb * P:(qb + nb) * P], start=True,
                                           stop=not any(mask_of(kb, qb + i, False) for i in range(nb)),
                                           skip_group_check=True)
                    for i in range(nb):
                        m = mask_of(kb, qb + i, False)
                        if m is not None:
                            ins = nc.tensor.matmul(psB[u % 2][:, (at + i) * P:(at + i + 1) * P], g.identb[:], m[:],
                                                   start=False, stop=True, skip_group_check=True)
                ins.then_inc(b_scored, 1)

            def pv(h, u):
                p = h.k % 2
                if u == 0:
                    wait(pe, vh_ready, (h + 1).count(1))
                    wait(pe, o_copied, h.count(1))
                wait(pe, b_exped, h.count(NB, u + 1))
                for kb, qb, nb, at in b_plan[u]:
                    c, q = qb // 4, qb % 4
                    ins = nc.tensor.matmul(psV[32 * c:32 * c + 32, q * P:(q + nb) * P], vh[p][:, kb, :],
                                           prob[u % 4][:, at * P:(at + nb) * P], start=(u, at) == first_of_chunk[c],
                                           stop=(u, at) == last_of_chunk[c], skip_group_check=True)
                ins.then_inc(pv_done, 1)

            tail = range((NB - 1) // 2 * 2, NB)

            def step(h, first=False, next_two=2):
                a_units = [(1, n) for n in range(LEAD, NA)] if next_two >= 1 else []
                turn_at = len(a_units)
                a_units += [(2, n) for n in range(LEAD)] if next_two == 2 else []
                total, done, active = max(NA, len(a_units)), 0, 0
                turn_unit = 0 if turn_at == 0 and next_two else None

                def more_maxima():
                    nonlocal done, active
                    active += 1
                    quota = total * active // (2 * NB - 2 * (turn_at > 0))
                    while done < min(quota, len(a_units)):
                        if done == turn_at and turn_unit is None:
                            return
                        a_unit(h + a_units[done][0], a_units[done][1])
                        done += 1

                for u in range(NB):
                    b_unit(h, u)
                    if u != turn_unit:
                        more_maxima()
                    if u == 1 and not first:
                        for v in tail:
                            pv(h - 1, v)
                    if pair_at == "odd" and u % 2 and u > 1:
                        pv(h, u - 3)
                        pv(h, u - 2)
                    elif u % 2 == 0 and u and (pair_at == "even" or u == NB - 1):
                        pv(h, u - 2)
                        pv(h, u - 1)
                    if u == turn_unit:
                        transpose_m(h + 1)
                    if u != turn_unit or turn_at == 0:
                        more_maxima()
                    if turn_unit is None and done >= turn_at and next_two:
                        turn_unit = u + 1
                while done < len(a_units):
                    a_unit(h + a_units[done][0], a_units[done][1])
                    done += 1

            pe.wait_ge(preset, 10)
            for n in range(NA):
                a_unit(Head(0), n)
            transpose_m(Head(0))
            for n in range(LEAD):
                a_unit(Head(1), n)
            step(Head(0), first=True)
            step(Head(1))
            with nc.tensor.Fori(0, (H - 4) // 4) as i:
                for k in range(2, 6):
                    step(Head(k, i, 4))
            step(Head(H - 2), next_two=1)
            step(Head(H - 1), next_two=0)
            for v in tail:
                pv(Head(H - 1), v)

        @block.scalar
        def _(act):
            def copy_o(h):
                b = h.k % 4
                wait(act, pv_done, (h + 1).count(NB))
                wait(act, o_stored[b], h.turn(128))
                nc.scalar.activation(oh[b][:], psV[:], ACT.Copy).then_inc(o_copied, 1)

            def step(h, first=False):
                for u in range(NB):
                    wait(act, b_scored, h.count(NB, u + 1))
                    wait(act, pv_done, h.count(NB, held_since(u, 4, NB)))
                    n = sum(x[2] for x in b_plan[u]) * P
                    nc.scalar.activation(prob[u % 4][:, 0:n], psB[u % 2][:, 0:n], ACT.Exp, scale=scale).then_inc(b_exped, 1)
                    if u == 1 and not first:
                        copy_o(h - 1)

            step(Head(0), first=True)
            for h in range(1, 5):
                step(Head(h))
            with nc.scalar.Fori(0, (H - 8) // 4) as i:
                for k in range(5, 9):
                    step(Head(k, i, 4))
            for h in range(H - 3, H):
                step(Head(h))
            copy_o(Head(H - 1))

        @block.vector
        def _(dve):
            def maxima(h):
                for n in range(NA):
                    wait(dve, a_scored, h.count(NA, n + 1))
                    for qb, kb, nb, at in a_plan[n]:
                        k = part[n, at]
                        ins = nc.vector.tensor_reduce(mpart[:, qb, k:k + 1], psA[n % 3][:, at * P:(at + nb) * P],
                                                      AX.X, ALU.max)
                    ins.then_inc(a_reduced, 1)
                wait(dve, a_reduced, (h + 1).count(NA))
                step = [0]

                def chain(ins):
                    ins.then_inc(m_step, 1)
                    step[0] += 1
                    wait(dve, m_step, h.count(6, step[0]))

                chain(nc.vector.tensor_reduce(mrow[:], mpart[:], AX.X, ALU.max))
                chain(nc.vector.tensor_scalar(negm[:], mrow[:], -1.0, -M_FLOOR, ALU.mult, ALU.min))
                wait(dve, mT_written, h.count(1))
                chain(nc.vector.tensor_copy(mb[:, 0, :], negm[:]))
                chain(nc.vector.tensor_tensor(mrest[:], negm[:], mb[:, 0, :], ALU.subtract))
                chain(nc.vector.tensor_copy(mb[:, 1, :], mrest[:]))
                chain(nc.vector.tensor_tensor(mb[:, 2, :], mrest[:], mb[:, 1, :], ALU.subtract))
                wait(dve, mT_written, (h + 1).count(1))
                wait(dve, m_loaded, h.count(48))
                nc.vector.tensor_copy(mT[:], psM[0:3 * NT, :]).then_inc(mT_ready, 1)

            dve.wait_ge(preset, 10)
            maxima(Head(0))
            with nc.vector.Fori(0, H - 1) as i:
                maxima(Head(1, i, 1))
    st.close()


def attention_front(nc, g, name, wqT, wkT, wvT, bq=None, bk=None, bv=None, func=None, head_scales=None):
    st = Stage(nc, name)
    func = func or ACT.Identity
    w = st.sb("w", [P, 3, P])
    bqk = st.sb("bqk", [P, 2])
    bvr = st.sb("bvr", [P, P])
    qk = [st.sb(n, [P, S]) for n in ("qT", "kT")]
    parts = [[st.sb(f"part{n}{i}", [P, S], BF16) for i in range(3)] for n in ("q", "k")]
    rest = [st.sb(f"rest{n}", [P, S]) for n in ("q", "k")]
    psQ = [st.ps(f"psQ{i}") for i in range(4)]
    w_loaded, projected, qk_ready, v_projected, v_ready = (
        st.sem("w_loaded"), st.sem("projected"), st.sem("qk_ready"), st.sem("v_projected"), st.sem("v_ready"))
    part_step = [st.sem("q_part_step"), st.sem("k_part_step")]
    stored = st.sem("stored")
    zeroed = st.sem("zeroed")
    squared, norm2_ready, norm_ready, factor_step, spread, scaled, scale_step = [st.sem(n) for n in (
        "squared", "norm2_ready", "norm_ready", "factor_step", "spread", "scaled", "scale_step")]
    has_bias = bq is not None
    nload = 3 + (3 if has_bias else 0) + (2 if head_scales else 0)
    if head_scales:
        hs = st.sb("hs", [P, 2])
        nrm, dn = st.sb("nrm", [P, 2, SEG]), st.sb("dn", [P, 2, SEG])
        gather = st.sb("gather", [P, P // H, P])
        psN = st.ps("psN")
        gathered = st.sem("gather_built")

    def split(dve):
        for half in range(2):
            if head_scales:
                dve.wait_ge(scaled, NC * (half + 1))
            else:
                dve.wait_ge(qk_ready, NC * (half + 1))
            cols = slice(half * S // 2, (half + 1) * S // 2)
            for step in range(4):
                for which in range(2):
                    sem, f, r = part_step[which], qk[which][:, cols], rest[which][:, cols]
                    p1, p2, p3 = (x[:, cols] for x in parts[which])
                    if step:
                        dve.wait_ge(sem, 4 * half + step)
                    if step == 0:
                        ins = nc.vector.tensor_copy(p1, f)
                    elif step == 1:
                        ins = nc.vector.tensor_tensor(r, f, p1, ALU.subtract)
                    elif step == 2:
                        ins = nc.vector.tensor_copy(p2, r)
                    else:
                        ins = nc.vector.tensor_tensor(p3, r, p2, ALU.subtract)
                    ins.then_inc(sem, 1)

    with st.block() as block:
        @block.sync
        def _(sp):
            for i, a in enumerate((wqT, wkT, wvT)):
                sp.dma_start(w[:, i, :], a).then_inc(w_loaded, 16)
            if has_bias:
                sp.dma_start(bqk[:, 0:1], bq).then_inc(w_loaded, 16)
                sp.dma_start(bqk[:, 1:2], bk).then_inc(w_loaded, 16)
                sp.dma_start(bvr[:], bv).then_inc(w_loaded, 16)
            if head_scales:
                sp.dma_start(hs[:, 0:1], head_scales[0]).then_inc(w_loaded, 16)
                sp.dma_start(hs[:, 1:2], head_scales[1]).then_inc(w_loaded, 16)
            for half in range(2):
                cols = slice(half * S // 2, (half + 1) * S // 2)
                for i, after in enumerate((1, 3, 4)):
                    for which, dram in ((0, g.qparts), (1, g.kparts)):
                        sp.wait_ge(part_step[which], 4 * half + after)
                        sp.dma_start(dram[i][:, cols], parts[which][i][:, cols]).then_inc(stored, 16)
            sp.wait_ge(stored, 16 * 12)

        @block.tensor
        def _(pe):
            pe.wait_ge(w_loaded, 16 * nload)
            for n in range(2 * NC):
                c, which = n // 2, n % 2
                if n >= 4:
                    pe.wait_ge(qk_ready, n - 3)
                nc.tensor.matmul(psQ[n % 4][:], w[:, which, :], g.XnT[:, c * CH:(c + 1) * CH],
                                 start=True, stop=True).then_inc(projected, 1)
            for t in range(NT):
                if t % 4 == 0:
                    pe.wait_ge(qk_ready, t // 4 + 5)
                nc.tensor.matmul(psQ[t // 4][:, t % 4 * P:(t % 4 + 1) * P], g.XnT[:, t * P:(t + 1) * P], w[:, 2, :],
                                 start=True, stop=True, skip_group_check=True).then_inc(v_projected, 1)
            if head_scales:
                pe.wait_ge(gathered, 5)
                for which in range(2):
                    pe.wait_ge(squared, 2 * NC - 1 + which)
                    for i in range(P // H):
                        ins = nc.tensor.matmul(psN[:, which * SEG:(which + 1) * SEG], gather[:, i, :],
                                               rest[which][:, i * SEG:(i + 1) * SEG], start=i == 0,
                                               stop=i == P // H - 1, skip_group_check=True)
                    ins.then_inc(norm2_ready, 1)
                pe.wait_ge(factor_step, 4)
                for n in range(2 * NC):
                    c, which = n // 2, n % 2
                    if n >= 4:
                        pe.wait_ge(scaled, n - 3)
                    else:
                        pe.wait_ge(v_ready, n + 1)
                    for i in range(CH // SEG):
                        ins = nc.tensor.matmul(psQ[n % 4][:, i * SEG:(i + 1) * SEG], g.spread[:, CH // SEG * c + i, :],
                                               dn[:, which, :], start=True, stop=True, skip_group_check=True)
                    ins.then_inc(spread, 1)

        @block.scalar
        def _(act):
            act.wait_ge(w_loaded, 16 * nload)
            act.wait_ge(zeroed, 1)
            for n in range(2 * NC):
                c, which = n // 2, n % 2
                act.wait_ge(projected, n + 1)
                nc.scalar.activation(qk[which][:, c * CH:(c + 1) * CH], psQ[n % 4][:], func,
                                     bias=bqk[:, which:which + 1]).then_inc(qk_ready, 1)
                if head_scales:
                    act.wait_ge(qk_ready, n + 1)
                    nc.scalar.activation(rest[which][:, c * CH:(c + 1) * CH], qk[which][:, c * CH:(c + 1) * CH],
                                         ACT.Square).then_inc(squared, 1)
            for c in range(NC):
                act.wait_ge(v_projected, 4 * (c + 1))
                nc.scalar.activation(g.V[:, 4 * c:4 * c + 4, :].rearrange("p a b -> p (a b)"), psQ[c][:],
                                     func).then_inc(v_ready, 1)
            if head_scales:
                act.wait_ge(norm2_ready, 2)
                nc.scalar.activation(nrm[:].rearrange("p a j -> p (a j)"), psN[:], ACT.Sqrt).then_inc(norm_ready, 1)

        @block.vector
        def _(dve):
            if not has_bias:
                nc.vector.memset(bqk[:], 0.0).then_inc(zeroed, 1)
            else:
                dve.wait_ge(w_loaded, 16 * nload)
                nc.vector.tensor_copy(bqk[:], bqk[:]).then_inc(zeroed, 1)
            if head_scales:
                dve.wait_ge(norm_ready, 1)
                nc.vector.tensor_scalar(dn[:], nrm[:], 1e-6, None, ALU.add).then_inc(factor_step, 1)
                dve.wait_ge(factor_step, 1)
                nc.vector.reciprocal(dn[:], dn[:]).then_inc(factor_step, 1)
                dve.wait_ge(factor_step, 2)
                for which in range(2):
                    nc.vector.scalar_tensor_tensor(out=dn[:, which, :], in0=nrm[:, which, :], scalar=hs[:, which:which + 1],
                                                   in1=dn[:, which, :], op0=ALU.mult, op1=ALU.mult).then_inc(factor_step, 1)
                for n in range(2 * NC):
                    c, which = n // 2, n % 2
                    f = qk[which][:, c * CH:(c + 1) * CH]
                    dve.wait_ge(spread, n + 1)
                    nc.vector.tensor_tensor(f, f, psQ[n % 4][:], ALU.mult).then_inc(scaled, 1)
            split(dve)

        @block.gpsimd
        def _(pool):
            if head_scales:
                v = gather[:].rearrange("p s (h t) -> p s h t", h=H)
                nc.gpsimd.memset(gather[:], 1.0).then_inc(gathered, 1)
                for n, (base, cm, pattern) in enumerate((
                        (0, 1, [[0, P // H], [-HD, H], [0, P // H]]), (HD - 1, -1, [[0, P // H], [HD, H], [0, P // H]]),
                        (0, 0, [[-1, P // H], [0, H], [1, P // H]]), (0, 0, [[1, P // H], [0, H], [-1, P // H]]))):
                    pool.wait_ge(gathered, n + 1)
                    nc.gpsimd.affine_select(out=v, in_=v, compare_op=ALU.is_ge, fill=0.0, base=base,
                                            pattern=pattern, channel_multiplier=cm).then_inc(gathered, 1)
            if has_bias:
                pool.wait_ge(w_loaded, 16 * nload)
                pool.wait_ge(v_ready, NC)
                nc.gpsimd.tensor_tensor(g.V[:], g.V[:], bvr[:].unsqueeze(1).broadcast_to([P, NT, P]), ALU.add).then_inc(scale_step, 1)
    st.close()


def attention_normalise(nc, g, name):
    st = Stage(nc, name)
    den = st.sb("den", [P, SEG])
    psD = [st.ps(f"psD{i}") for i in range(4)]
    ctx_loaded = st.sem("ctx_loaded")
    loaded, clamped, recip_ready, spread, ctx_ready = (
        st.sem("loaded"), st.sem("clamped"), st.sem("recip_ready"), st.sem("spread"), st.sem("ctx_ready"))
    with st.block() as block:
        @block.sync
        def _(sp):
            sp.dma_start(den[:], g.den_dram.rearrange("h (s j) -> (h s) j", j=SEG)).then_inc(loaded, 16)
            sp.dma_start(g.CT[:], g.o_dram).then_inc(ctx_loaded, 16)

        @block.tensor
        def _(pe):
            pe.wait_ge(recip_ready, 1)
            for c in range(NC):
                for i in range(CH // SEG):
                    ins = nc.tensor.matmul(psD[c][:, i * SEG:(i + 1) * SEG], g.spread[:, CH // SEG * c + i, :], den[:],
                                           start=True, stop=True, skip_group_check=True)
                ins.then_inc(spread, 1)

        @block.vector
        def _(dve):
            dve.wait_ge(loaded, 16)
            nc.vector.tensor_scalar(den[:], den[:], 1e-30, None, ALU.max).then_inc(clamped, 1)
            dve.wait_ge(clamped, 1)
            nc.vector.reciprocal(den[:], den[:]).then_inc(recip_ready, 1)
            dve.wait_ge(ctx_loaded, 16)
            for c in range(NC):
                dve.wait_ge(spread, c + 1)
                nc.vector.tensor_tensor(g.CT[:, c * CH:(c + 1) * CH], g.CT[:, c * CH:(c + 1) * CH], psD[c][:],
                                        ALU.mult).then_inc(ctx_ready, 1)
    st.close()


def project_add(nc, g, name, srcT, wT, bias_row=None, ntiles=1):
    st = Stage(nc, name)
    w = st.sb("w", [P, P])
    b = st.sb("b", [P, P])
    psO = [st.ps(f"psO{i}") for i in range(4)]
    loaded, projected, added, bias_added = st.sem("loaded"), st.sem("projected"), st.sem("added"), st.sem("bias_added")
    nload = (wT is not None) + (bias_row is not None)
    with st.block() as block:
        @block.sync
        def _(sp):
            if wT is not None:
                sp.dma_start(w[:], wT).then_inc(loaded, 16)
            if bias_row is not None:
                sp.dma_start(b[:], bias_row).then_inc(loaded, 16)

        @block.tensor
        def _(pe):
            if nload:
                pe.wait_ge(loaded, 16 * nload)
            for t in range(NT):
                o = psO[t // 4][:, t % 4 * P:(t % 4 + 1) * P]
                if wT is None:
                    ins = nc.tensor.transpose(o, srcT[:, t * P:(t + 1) * P], g.ident[:])
                else:
                    ins = nc.tensor.matmul(o, srcT[:, t * P:(t + 1) * P], w[:], start=True, stop=True,
                                           skip_group_check=True)
                ins.then_inc(projected, 1)

        @block.vector
        def _(dve):
            if bias_row is not None:
                dve.wait_ge(loaded, 16 * nload)
                nc.vector.tensor_tensor(g.X[:], g.X[:], b[:].unsqueeze(1).broadcast_to([P, NT, P]), ALU.add).then_inc(bias_added, 1)
                dve.wait_ge(bias_added, 1)
            for c in range(NC):
                dve.wait_ge(projected, 4 * (c + 1))
                x = g.X[:, 4 * c:4 * c + 4, :].rearrange("p a b -> p (a b)")
                nc.vector.tensor_tensor(x, x, psO[c][:], ALU.add).then_inc(added, 1)
    st.close()


NLAT = 64
LH = 4
LD = LH * HD
LCH = S // NLAT


def latent_mix(nc, g, a):
    st = Stage(nc, "latent")
    rq_w, rkv_w, rout_w = st.sb("rq_w", [P, LD]), st.sb("rkv_w", [P, 2 * LD]), st.sb("rout_w", [LD, P])
    rq_b, rk_b, rv_b, rout_b = st.sb("rq_b", [LD, 1]), st.sb("rk_b", [LD, 1]), st.sb("rv_b", [P, LD]), st.sb("rout_b", [P, 1])
    gcol = st.sb("gcol", [P, 2])
    gmat = st.sb("gmat", [P, 2, P])
    pooled = st.sb("pooled", [P, 2, NLAT])
    rqT = st.sb("rqT", [LD, S])
    rkT = st.sb("rkT", [LD, NLAT])
    rkd = st.sb("rkd", [LD, LH, NLAT])
    rvs = st.sb("rvs", [P, LD])
    rvmask = st.sb("rvmask", [P, 2, LD])
    rvd = st.sb("rvd", [P, 2, LD])
    lmask = st.sb("lmask", [P, 2 * NLAT])
    sc = st.sb("sc", [P, NT, LH, NLAT])
    mx, den = st.sb("mx", [P, NT * LH]), st.sb("den", [P, NT * LH])
    scT = st.sb("scT", [P, 2, S])
    latT = st.sb("latT", [LD, S])
    remT = st.sb("remT", [P, S])
    gate = st.sb("gate", [P, S])
    diff = st.sb("diff", [P, S])
    psA = [st.ps(f"psA{i}") for i in range(4)]
    psB = [st.ps(f"psB{i}") for i in range(4)]
    loaded, masks = st.sem("loaded"), st.sem("masks_built")
    pooled_ready, gmat_ready = st.sem("pooled_ready"), st.sem("gmat_ready")
    kv_projected, kv_ready, rq_projected, rq_ready = (
        st.sem("kv_projected"), st.sem("kv_ready"), st.sem("rq_projected"), st.sem("rq_ready"))
    diag_ready, scored, masked, soft = st.sem("diag_ready"), st.sem("scored"), st.sem("masked"), st.sem("soft_step")
    exped, transposed, t_copied, lat_done, lat_copied = (
        st.sem("exped"), st.sem("transposed"), st.sem("t_copied"), st.sem("lat_done"), st.sem("lat_copied"))
    rem_done, rem_ready, gate_done, gate_ready, mixed = (
        st.sem("rem_done"), st.sem("rem_ready"), st.sem("gate_done"), st.sem("gate_ready"), st.sem("mixed"))
    NL = 10
    with st.block() as block:
        @block.sync
        def _(sp):
            for dst, src in ((rq_w[:], a["L0_attn_rq_w"]), (rkv_w[:], a["L0_attn_rkv_w"]), (rout_w[:], a["L0_attn_rout_w"]),
                             (rq_b[:], a["L0_attn_rq_b"].unsqueeze(1)), (rk_b[:], a["L0_attn_rkv_b"][0:LD].unsqueeze(1)),
                             (rv_b[:], a["L0_attn_rkv_b"][LD:2 * LD].unsqueeze(0).broadcast_to([P, LD])),
                             (rout_b[:], a["L0_attn_rout_b"].unsqueeze(1)),
                             (gcol[:, 0:1], a["L0_attn_gl_w"].unsqueeze(0).broadcast_to([H, HD, 1])),
                             (gcol[:, 1:2], a["L0_attn_gr_w"].unsqueeze(0).broadcast_to([H, HD, 1]))):
                sp.dma_start(dst, src).then_inc(loaded, 16)

        @block.gpsimd
        def _(pool):
            nc.gpsimd.memset(lmask[:], 0.0).then_inc(masks, 1)
            nc.gpsimd.memset(rvmask[:], 0.0).then_inc(masks, 1)
            pool.wait_ge(masks, 2)
            nc.gpsimd.affine_select(out=lmask[:], in_=lmask[:], compare_op=ALU.is_ge, fill=NEG, base=(NLAT - 1) * LCH,
                                    pattern=[[-LCH, 2 * NLAT]], channel_multiplier=1).then_inc(masks, 1)
            for c in range(2):
                for half in range(2):
                    lo = (2 * c + half) * HD
                    pool.wait_ge(masks, 3 + 2 * c + half)
                    nc.gpsimd.memset(rvmask[64 * half:64 * half + 64, c, lo:lo + HD], 1.0).then_inc(masks, 1)

        @block.vector
        def _(dve):
            tt, ts = nc.vector.tensor_tensor, nc.vector.tensor_scalar
            nc.vector.tensor_reduce(diff[:, 0:NLAT], g.XnT[:].rearrange("p (l j) -> p l j", j=LCH), AX.X,
                                    ALU.add).then_inc(pooled_ready, 1)
            dve.wait_ge(pooled_ready, 1)
            for i in range(2):
                ts(pooled[:, i, :], diff[:, 0:NLAT], 1.0 / LCH, None, ALU.mult).then_inc(pooled_ready, 1)
            dve.wait_ge(loaded, 16 * 9)
            for i in range(2):
                ts(gmat[:, i, :], g.blockdiag[:], gcol[:, i:i + 1], None, ALU.mult).then_inc(gmat_ready, 1)
            dve.wait_ge(kv_ready, 1)
            tt(rkd[:], rkT[:].unsqueeze(1).broadcast_to([LD, LH, NLAT]),
               g.blockdiag[0:LD, 0:LD:HD].unsqueeze(2).broadcast_to([LD, LH, NLAT]), ALU.mult).then_inc(diag_ready, 1)
            dve.wait_ge(masks, 7)
            dve.wait_ge(kv_projected, 2)
            tt(rvs[:], psA[1][:, 0:LD], rv_b[:], ALU.add).then_inc(diag_ready, 1)
            dve.wait_ge(diag_ready, 2)
            for c in range(2):
                tt(rvd[:, c, :], rvs[:], rvmask[:, c, :], ALU.mult).then_inc(diag_ready, 1)
            for t in range(NT):
                dve.wait_ge(scored, t + 1)
                nc.vector.scalar_tensor_tensor(
                    out=sc[:, t, :, :], in0=psB[t % 4][:, 0:LH * NLAT].rearrange("p (h l) -> p h l", h=LH),
                    scalar=float(1.0 / np.sqrt(HD)),
                    in1=lmask[:, NLAT - 4 * t:2 * NLAT - 4 * t].unsqueeze(1).broadcast_to([P, LH, NLAT]),
                    op0=ALU.mult, op1=ALU.add).then_inc(masked, 1)
            dve.wait_ge(masked, NT)
            s3 = sc[:].rearrange("p t h l -> p (t h) l")

            def wide(x):
                return x[:].unsqueeze(2).broadcast_to([P, NT * LH, NLAT])
            nc.vector.tensor_reduce(mx[:], s3, AX.X, ALU.max).then_inc(soft, 1)
            dve.wait_ge(soft, 1)
            ts(mx[:], mx[:], M_FLOOR, None, ALU.max).then_inc(soft, 1)
            dve.wait_ge(soft, 2)
            tt(s3, s3, wide(mx), ALU.subtract).then_inc(soft, 1)
            dve.wait_ge(exped, 1)
            nc.vector.tensor_reduce(den[:], s3, AX.X, ALU.add).then_inc(soft, 1)
            dve.wait_ge(soft, 4)
            ts(den[:], den[:], 1e-30, None, ALU.max).then_inc(soft, 1)
            dve.wait_ge(soft, 5)
            nc.vector.reciprocal(den[:], den[:]).then_inc(soft, 1)
            dve.wait_ge(soft, 6)
            tt(s3, s3, wide(den), ALU.mult).then_inc(soft, 1)
            dve.wait_ge(rem_ready, NC)
            tt(diff[:], g.CT[:], remT[:], ALU.subtract).then_inc(mixed, 1)
            dve.wait_ge(mixed, 1)
            dve.wait_ge(gate_ready, NC)
            tt(diff[:], diff[:], gate[:], ALU.mult).then_inc(mixed, 1)
            dve.wait_ge(mixed, 2)
            tt(g.CT[:], diff[:], remT[:], ALU.add).then_inc(mixed, 1)

        @block.scalar
        def _(act):
            act.wait_ge(loaded, 16 * 9)
            act.wait_ge(kv_projected, 1)
            nc.scalar.activation(rkT[:], psA[0][0:LD, 0:NLAT], ACT.Identity, bias=rk_b[:]).then_inc(kv_ready, 1)
            for c in range(NC):
                act.wait_ge(rq_projected, c + 1)
                nc.scalar.activation(rqT[:, c * CH:(c + 1) * CH], psB[c][0:LD, :], ACT.Identity,
                                     bias=rq_b[:]).then_inc(rq_ready, 1)
            act.wait_ge(soft, 3)
            nc.scalar.activation(sc[:], sc[:], ACT.Exp).then_inc(exped, 1)
            for n in range(2 * NC):
                act.wait_ge(transposed, 4 * (n + 1))
                c, half = n // 2, n % 2
                nc.scalar.activation(scT[:, half, c * CH:(c + 1) * CH], psA[n % 4][:], ACT.Copy).then_inc(t_copied, 1)
            for c in range(NC):
                act.wait_ge(lat_done, c + 1)
                nc.scalar.activation(latT[:, c * CH:(c + 1) * CH], psB[c][0:LD, :], ACT.Copy).then_inc(lat_copied, 1)
            for c in range(NC):
                act.wait_ge(rem_done, c + 1)
                nc.scalar.activation(remT[:, c * CH:(c + 1) * CH], psA[c][:], ACT.Identity, bias=rout_b[:]).then_inc(rem_ready, 1)
            for c in range(NC):
                act.wait_ge(gate_done, c + 1)
                nc.scalar.activation(gate[:, c * CH:(c + 1) * CH], psB[c][:], ACT.Sigmoid).then_inc(gate_ready, 1)

        @block.tensor
        def _(pe):
            mm = nc.tensor.matmul
            pe.wait_ge(loaded, 16 * 9)
            pe.wait_ge(pooled_ready, 3)
            mm(psA[0][0:LD, 0:NLAT], rkv_w[:, 0:LD], pooled[:, 0, :], start=True, stop=True).then_inc(kv_projected, 1)
            mm(psA[1][:, 0:LD], pooled[:].rearrange("p a l -> p (a l)"), rkv_w[:, LD:2 * LD], start=True,
               stop=True).then_inc(kv_projected, 1)
            for c in range(NC):
                mm(psB[c][0:LD, :], rq_w[:], g.XnT[:, c * CH:(c + 1) * CH], start=True, stop=True).then_inc(rq_projected, 1)
            pe.wait_ge(diag_ready, 4)
            pe.wait_ge(rq_ready, NC)
            for t in range(NT):
                if t >= 4:
                    pe.wait_ge(masked, t - 3)
                mm(psB[t % 4][:, 0:LH * NLAT], rqT[:, t * P:(t + 1) * P], rkd[:].rearrange("p h l -> p (h l)"),
                   start=True, stop=True).then_inc(scored, 1)
            pe.wait_ge(soft, 7)
            pe.wait_ge(kv_ready, 1)
            for n in range(2 * NC):
                c, half = n // 2, n % 2
                if n >= 4:
                    pe.wait_ge(t_copied, n - 3)
                for i in range(4):
                    src = sc[:, 4 * c + i, 2 * half:2 * half + 2, :].rearrange("p h l -> p (h l)")
                    nc.tensor.transpose(psA[n % 4][:, i * P:(i + 1) * P], src, g.ident[:]).then_inc(transposed, 1)
            for c in range(NC):
                pe.wait_ge(t_copied, 2 * c + 2)
                for half in range(2):
                    ins = mm(psB[c][0:LD, :], rvd[:, half, :], scT[:, half, c * CH:(c + 1) * CH],
                             start=half == 0, stop=half == 1)
                ins.then_inc(lat_done, 1)
            pe.wait_ge(t_copied, 2 * NC)
            for c in range(NC):
                pe.wait_ge(lat_copied, c + 1)
                mm(psA[c][:], rout_w[:], latT[:, c * CH:(c + 1) * CH], start=True, stop=True).then_inc(rem_done, 1)
            pe.wait_ge(gmat_ready, 2)
            pe.wait_ge(lat_copied, NC)
            for c in range(NC):
                pe.wait_ge(rem_ready, c + 1)
                mm(psB[c][:], gmat[:, 0, :], g.CT[:, c * CH:(c + 1) * CH], start=True, stop=False)
                mm(psB[c][:], gmat[:, 1, :], remT[:, c * CH:(c + 1) * CH], start=False, stop=True).then_inc(gate_done, 1)
    st.close()


def col(ap):
    return ap.unsqueeze(1)


def bcast_row(ap, n=P):
    return ap.unsqueeze(0).broadcast_to([P, n])


def l0_attn(nc, g, a):
    layernorm_transpose(nc, g, "l0a_ln")
    w, b = a["L0_attn_qkv_w"], a["L0_attn_qkv_b"]
    attention_front(nc, g, "l0a_front", w[:, 0:P], w[:, P:2 * P], w[:, 2 * P:3 * P],
                    col(b[0:P]), col(b[P:2 * P]), bcast_row(b[2 * P:3 * P]))
    attention_core(nc, g, "l0a_core", "window", float(1.0 / np.sqrt(HD)), 0.5, "even")
    attention_normalise(nc, g, "l0a_norm")
    latent_mix(nc, g, a)
    project_add(nc, g, "l0a_out", g.CT, a["L0_attn_out_w"], bias_row=bcast_row(a["L0_attn_out_b"]))


def l1_attn(nc, g, a):
    layernorm_transpose(nc, g, "l1a_ln")
    attention_front(nc, g, "l1a_front", a["L1_attn_WqT"], a["L1_attn_WkT"], a["L1_attn_WvT"])
    attention_core(nc, g, "l1a_core", "full", float(1.0 / np.sqrt(np.float32(P))), 0.1, "odd")
    attention_normalise(nc, g, "l1a_norm")
    project_add(nc, g, "l1a_out", g.CT, None)


def l2_attn(nc, g, a):
    layernorm_transpose(nc, g, "l2a_ln")
    scales = [a[n].unsqueeze(1).unsqueeze(2).broadcast_to([H, HD, 1]) for n in ("L2_attn_q_scale", "L2_attn_k_scale")]
    attention_front(nc, g, "l2a_front", a["L2_attn_WqT"], a["L2_attn_WkT"], a["L2_attn_WvT"],
                    func=ACT.Silu, head_scales=scales)
    attention_core(nc, g, "l2a_core", "causal", 1.0, 0.8, "odd")
    attention_normalise(nc, g, "l2a_norm")
    project_add(nc, g, "l2a_out", g.CT, a["L2_attn_WoT"])


def router(nc, g, name, E, rw, rb=None, hidden=None):
    st = Stage(nc, name)
    rw_s, rb_s = st.sb("rw", [P, E]), st.sb("rb", [P, E])
    w1, b1 = st.sb("w1", [P, P]), st.sb("b1", [P, 1])
    hT = st.sb("hT", [P, S])
    L = st.sb("L", [P, NT, E])
    gt, eq = st.sb("gt", [P, NT, E, E]), st.sb("eq", [P, NT, E, E])
    tri = st.sb("tri", [P, E, E])
    rank, mx, den = st.sb("rank", [P, NT, E]), st.sb("mx", [P, NT]), st.sb("den", [P, NT])
    psH = [st.ps(f"psH{i}") for i in range(4)]
    psL = st.ps("psL")
    loaded, tri_built, hid_done, hid_ready, scored, step, exped, transposed, copied = (
        st.sem("loaded"), st.sem("tri_built"), st.sem("hid_done"), st.sem("hid_ready"), st.sem("scored"),
        st.sem("step"), st.sem("exped"), st.sem("transposed"), st.sem("copied"))
    loads = [(rw_s[:], rw)]
    if rb is not None:
        loads.append((rb_s[:], rb))
    if hidden is not None:
        loads += [(w1[:], hidden[0]), (b1[:], hidden[1])]
    NL = 16 * len(loads)
    with st.block() as block:
        @block.sync
        def _(sp):
            for d, s in loads:
                sp.dma_start(d, s).then_inc(loaded, 16)

        @block.gpsimd
        def _(pool):
            nc.gpsimd.memset(tri[:], 1.0).then_inc(tri_built, 1)
            pool.wait_ge(tri_built, 1)
            nc.gpsimd.affine_select(out=tri[:], in_=tri[:], compare_op=ALU.is_gt, fill=0.0, base=0,
                                    pattern=[[1, E], [-1, E]], channel_multiplier=0).then_inc(tri_built, 1)

        @block.tensor
        def _(pe):
            pe.wait_ge(loaded, NL)
            if hidden is not None:
                for c in range(NC):
                    nc.tensor.matmul(psH[c][:], w1[:], g.XnT[:, c * CH:(c + 1) * CH], start=True, stop=True).then_inc(hid_done, 1)
            src = hT if hidden is not None else g.XnT
            for t in range(NT):
                if hidden is not None:
                    pe.wait_ge(hid_ready, t // 4 + 1)
                nc.tensor.matmul(psL[:, t * E:(t + 1) * E], src[:, t * P:(t + 1) * P], rw_s[:], start=True, stop=True,
                                 skip_group_check=True).then_inc(scored, 1)
            pe.wait_ge(step, 12)
            if hidden is not None:
                pe.wait_ge(hid_ready, NC)
            for t in range(NT):
                nc.tensor.transpose(psH[t // 4][0:E, t % 4 * P:(t % 4 + 1) * P], g.W[:, t, 0:E], g.ident[:]).then_inc(transposed, 1)

        @block.scalar
        def _(act):
            if hidden is not None:
                act.wait_ge(loaded, NL)
                for c in range(NC):
                    act.wait_ge(hid_done, c + 1)
                    nc.scalar.activation(hT[:, c * CH:(c + 1) * CH], psH[c][:], ACT.Silu, bias=b1[:]).then_inc(hid_ready, 1)
            act.wait_ge(step, 8)
            nc.scalar.activation(L[:], L[:], ACT.Exp).then_inc(exped, 1)
            for c in range(NC):
                act.wait_ge(transposed, 4 * (c + 1))
                nc.scalar.activation(g.WT[0:E, c * CH:(c + 1) * CH], psH[c][0:E, :], ACT.Copy).then_inc(copied, 1)

        @block.vector
        def _(dve):
            n = [0]

            def chain(ins):
                ins.then_inc(step, 1)
                n[0] += 1
                dve.wait_ge(step, n[0])
            tt = nc.vector.tensor_tensor
            dve.wait_ge(scored, NT)
            dve.wait_ge(loaded, NL)
            ps = psL[:, 0:NT * E].rearrange("p (t e) -> p t e", e=E)
            if rb is not None:
                chain(tt(L[:], ps, rb_s[:].unsqueeze(1).broadcast_to([P, NT, E]), ALU.add))
            else:
                chain(nc.vector.tensor_copy(L[:], ps))
            other = L[:].unsqueeze(2).broadcast_to([P, NT, E, E])
            this = L[:].unsqueeze(3).broadcast_to([P, NT, E, E])
            dve.wait_ge(tri_built, 2)
            chain(tt(gt[:], other, this, ALU.is_gt))
            chain(tt(eq[:], other, this, ALU.is_equal))
            chain(tt(eq[:], eq[:], tri[:].unsqueeze(1).broadcast_to([P, NT, E, E]), ALU.mult))
            chain(tt(gt[:], gt[:], eq[:], ALU.add))
            chain(nc.vector.tensor_reduce(rank[:], gt[:], AX.X, ALU.add))
            chain(nc.vector.tensor_reduce(mx[:], L[:], AX.X, ALU.max))
            chain(tt(L[:], L[:], mx[:].unsqueeze(2).broadcast_to([P, NT, E]), ALU.subtract))
            dve.wait_ge(exped, 1)
            chain(nc.vector.scalar_tensor_tensor(out=g.W[:, :, 0:E], in0=rank[:], scalar=1.5, in1=L[:],
                                                 op0=ALU.is_lt, op1=ALU.mult))
            chain(nc.vector.tensor_reduce(den[:], g.W[:, :, 0:E], AX.X, ALU.add))
            chain(nc.vector.reciprocal(den[:], den[:]))
            chain(tt(g.W[:, :, 0:E], g.W[:, :, 0:E], den[:].unsqueeze(2).broadcast_to([P, NT, E]), ALU.mult))
    st.close()


def l1_experts(nc, g, a):
    E, HID = 8, 512
    J = HID // P
    st = Stage(nc, "l1e")
    w1, w2 = st.sb("w1", [P, E, HID]), st.sb("w2", [P, E, J, P])
    b1, b2 = st.sb("b1", [P, E, J]), st.sb("b2", [E, P])
    h = [st.sb(f"h{i}", [P, J, CH]) for i in range(2)]
    wc = st.sb("wc", [P, 4, E])
    psH = [st.ps(f"psH{i}") for i in range(4)]
    psO = [st.ps(f"psO{i}") for i in range(2)]
    loaded, hid_done, hid_ready, out_done, out_added, wc_ready = (
        st.sem("loaded"), st.sem("hid_done"), st.sem("hid_ready"), st.sem("out_done"), st.sem("out_added"), st.sem("wc_ready"))
    UH, UO = E * J, E + 1

    with st.block() as block:
        @block.sync
        def _(sp):
            for d, s in ((w1[:], a["L1_ffn_we1"].rearrange("e d h -> d e h")),
                         (w2[:], a["L1_ffn_we2"].rearrange("e (j p) d -> p e j d", p=P)),
                         (b1[:], a["L1_ffn_be1"].rearrange("e (j p) -> p e j", p=P)),
                         (b2[:], a["L1_ffn_be2"])):
                sp.dma_start(d, s, allow_slow_non_contiguous=True).then_inc(loaded, 16)

        @block.tensor
        def _(pe):
            def hid(c, e, xs):
                for j in range(J):
                    n = e * J + j
                    wait(pe, hid_ready, c.count(UH, n - 3))
                    nc.tensor.matmul(psH[j][:], w1[:, e, j * P:(j + 1) * P], xs, start=True, stop=True).then_inc(hid_done, 1)

            def outp(c, e):
                wait(pe, hid_ready, c.count(UH, e * J + J))
                wait(pe, out_added, c.count(UO, e - 1))
                for t in range(4):
                    for j in range(J):
                        ins = nc.tensor.matmul(psO[e % 2][:, t * P:(t + 1) * P], h[e % 2][:, j, t * P:(t + 1) * P],
                                               w2[:, e, j, :], start=j == 0, stop=j == J - 1, skip_group_check=True)
                ins.then_inc(out_done, 1)

            def chunk(c, xs, c_static):
                hid(c, 0, xs)
                for e in range(E):
                    if e + 1 < E:
                        hid(c, e + 1, xs)
                    outp(c, e)

            pe.wait_ge(loaded, 64)
            for c in range(NC):
                chunk(Head(c), g.XnT[:, c * CH:(c + 1) * CH], c)
                wait(pe, out_added, c * UO + E - 1)
                for t in range(4):
                    q = c * 4 + t
                    ins = nc.tensor.matmul(psO[0][:, t * P:(t + 1) * P], g.WT[0:E, q * P:(q + 1) * P], b2[:],
                                           start=True, stop=True, skip_group_check=True)
                ins.then_inc(out_done, 1)
                wait(pe, out_added, (c + 1) * UO)

        @block.scalar
        def _(act):
            act.wait_ge(loaded, 64)
            for c in range(NC):
                for e in range(E):
                    for j in range(J):
                        wait(act, hid_done, c * UH + e * J + j + 1)
                        if j == 0:
                            wait(act, out_done, c * UO + e - 1 if e >= 2 else c * UO)
                        nc.scalar.activation(h[e % 2][:, j, :], psH[j][:], ACT.Silu, bias=b1[:, e, j:j + 1]).then_inc(hid_ready, 1)

        @block.vector
        def _(dve):
            for c in range(NC):
                for e in range(E):
                    wait(dve, out_done, c * UO + e + 1)
                    if e + c:
                        wait(dve, out_added, c * UO + e)
                    for t in range(4):
                        q = 4 * c + t
                        ins = nc.vector.scalar_tensor_tensor(
                            out=g.X[:, q, :], in0=psO[e % 2][:, t * P:(t + 1) * P], scalar=g.W[:, q, e:e + 1],
                            in1=g.X[:, q, :], op0=ALU.mult, op1=ALU.add)
                    ins.then_inc(out_added, 1)
                wait(dve, out_done, (c + 1) * UO)
                wait(dve, out_added, c * UO + E)
                x = g.X[:, 4 * c:4 * c + 4, :].rearrange("p t d -> p (t d)")
                nc.vector.tensor_tensor(x, x, psO[0][:], ALU.add).then_inc(out_added, 1)
    st.close()


def l1_ffn(nc, g, a):
    keep = Stage(nc, "l1f_keep")
    xn = keep.sb("xn", [P, NT, P])
    layernorm_transpose(nc, g, "l1f_ln", keep_rows=xn)
    added = keep.sem("added")
    with keep.block() as block:
        @block.vector
        def _(dve):
            nc.vector.tensor_tensor(g.X[:], g.X[:], xn[:], ALU.add).then_inc(added, 1)
    keep.close()
    router(nc, g, "l1r", 8, a["L1_ffn_rw2"], rb=bcast_row(a["L1_ffn_rb2"], 8),
           hidden=(a["L1_ffn_rw1"], col(a["L1_ffn_rb1"])))
    l1_experts(nc, g, a)


def l3_experts(nc, g, a):
    E, I = 16, 64
    PR = E // 2
    ALPHA, LIMIT = 1.702, 7.0
    st = Stage(nc, "l3e")
    gu, gub = st.sb("gu", [P, E, 2 * I]), st.sb("gub", [P, PR, 2])
    dn, dnb = st.sb("dn", [P, PR, P]), st.sb("dnb", [E, P])
    sel = st.sb("sel", [E, PR, P])
    gate = [st.sb(f"gate{i}", [P, CH]) for i in range(3)]
    up = [st.sb(f"up{i}", [P, CH]) for i in range(3)]
    sg = [st.sb(f"sg{i}", [P, CH]) for i in range(3)]
    hs = [st.sb(f"hs{i}", [P, CH]) for i in range(3)]
    psG = [st.ps(f"psG{i}") for i in range(2)]
    psU = [st.ps(f"psU{i}") for i in range(2)]
    psS = [st.ps(f"psS{i}") for i in range(2)]
    psO = [st.ps(f"psO{i}") for i in range(2)]
    loaded, sel_built, in_done, score_done, gate_ready, up_ready, sig_ready, up1_ready, glu_ready, act_ready, h_ready, down_done, o_ready = (
        [st.sem(n) for n in ("loaded", "sel_built", "in_done", "score_done", "gate_ready", "up_ready", "sig_ready", "up1_ready",
                             "glu_ready", "act_ready", "h_ready", "down_done", "o_ready")])
    units = [(c, r) for c in range(NC) for r in range(PR)]
    with st.block() as block:
        @block.sync
        def _(sp):
            for d, s in ((gu[:], a["L3_ffn_gate_up_proj"].rearrange("e d f -> d e f")),
                         (dn[:], a["L3_ffn_down_proj"].rearrange("(r e) i h -> (e i) r h", e=2)),
                         (dnb[:], a["L3_ffn_down_proj_bias"])):
                sp.dma_start(d, s).then_inc(loaded, 16)
            for r in range(PR):
                sp.dma_start(gub[:, r, :], a["L3_ffn_gate_up_proj_bias"][2 * r:2 * r + 2, :]
                             .rearrange("e (i g) -> (e i) g", g=2), allow_slow_non_contiguous=True).then_inc(loaded, 16)

        @block.gpsimd
        def _(pool):
            nc.gpsimd.memset(sel[:], 1.0).then_inc(sel_built, 1)
            pool.wait_ge(sel_built, 1)
            v = sel[:].rearrange("e r m -> e (r m)")
            nc.gpsimd.affine_select(out=v, in_=v, compare_op=ALU.is_ge, fill=0.0, base=0,
                                    pattern=[[1, PR * P]], channel_multiplier=-I).then_inc(sel_built, 1)
            pool.wait_ge(sel_built, 2)
            nc.gpsimd.affine_select(out=v, in_=v, compare_op=ALU.is_ge, fill=0.0, base=I - 1,
                                    pattern=[[-1, PR * P]], channel_multiplier=I).then_inc(sel_built, 1)
            for n in range(len(units)):
                b = n % 3
                pool.wait_ge(up_ready, n + 1)
                pool.wait_ge(sig_ready, n + 1)
                nc.gpsimd.tensor_tensor(sg[b][:], sg[b][:], gate[b][:], ALU.mult).then_inc(glu_ready, 1)
                pool.wait_ge(glu_ready, n + 1)
                nc.gpsimd.tensor_tensor(sg[b][:], sg[b][:], up[b][:], ALU.mult).then_inc(act_ready, 1)

        @block.tensor
        def _(pe):
            mm = nc.tensor.matmul

            def inputs(n):
                c, r = units[n]
                xs = g.XnT[:, c * CH:(c + 1) * CH]
                w = gu[:, 2 * r:2 * r + 2, :].rearrange("p e f -> p (e f)")
                if n >= 2:
                    pe.wait_ge(gate_ready, n - 1)
                    pe.wait_ge(up_ready, n - 1)
                mm(psG[n % 2][:], w[:, 0::2], xs, start=True, stop=True)
                mm(psU[n % 2][:], w[:, 1::2], xs, start=True, stop=True).then_inc(in_done, 1)

            def scores(n):
                c, r = units[n]
                if n >= 2:
                    pe.wait_ge(h_ready, n - 1)
                mm(psS[n % 2][:], sel[:, r, :], g.WT[:, c * CH:(c + 1) * CH], start=True, stop=True).then_inc(score_done, 1)

            def down(n):
                c, r = units[n]
                if r == 0:
                    if c >= 2:
                        pe.wait_ge(o_ready, c - 1)
                    mm(psO[c % 2][:], dnb[:], g.WT[:, c * CH:(c + 1) * CH], start=True, stop=False)
                pe.wait_ge(h_ready, n + 1)
                mm(psO[c % 2][:], dn[:, r, :], hs[n % 3][:], start=False, stop=r == PR - 1).then_inc(down_done, 1)

            pe.wait_ge(loaded, 16 * (3 + PR))
            pe.wait_ge(sel_built, 3)
            for n in range(len(units) + 3):
                if n < len(units):
                    inputs(n)
                if 1 <= n <= len(units):
                    scores(n - 1)
                if n >= 3:
                    down(n - 3)

        @block.scalar
        def _(act):
            def copy_out(c):
                act.wait_ge(down_done, PR * (c + 1))
                nc.scalar.activation(g.CT[:, c * CH:(c + 1) * CH], psO[c % 2][:], ACT.Copy).then_inc(o_ready, 1)

            for n in range(len(units)):
                c, r = units[n]
                act.wait_ge(gate_ready, n + 1)
                if n >= 3:
                    act.wait_ge(h_ready, n - 2)
                nc.scalar.activation(sg[n % 3][:], gate[n % 3][:], ACT.Sigmoid, scale=ALPHA).then_inc(sig_ready, 1)
                if r == 3 and c:
                    copy_out(c - 1)
            copy_out(NC - 1)

        @block.vector
        def _(dve):
            ts = nc.vector.tensor_scalar
            dve.wait_ge(loaded, 16 * (3 + PR))

            def times_score(n):
                dve.wait_ge(act_ready, n + 1)
                dve.wait_ge(score_done, n + 1)
                if n >= 3:
                    dve.wait_ge(down_done, n - 2)
                nc.vector.tensor_tensor(hs[n % 3][:], psS[n % 2][:], sg[n % 3][:], ALU.mult).then_inc(h_ready, 1)

            for n in range(len(units)):
                c, r = units[n]
                b = n % 3
                dve.wait_ge(in_done, n + 1)
                if n >= 3:
                    dve.wait_ge(act_ready, n - 2)
                ts(gate[b][:], psG[n % 2][:], gub[:, r, 0:1], LIMIT, ALU.add, ALU.min).then_inc(gate_ready, 1)
                ts(up[b][:], psU[n % 2][:], gub[:, r, 1:2], LIMIT, ALU.add, ALU.min).then_inc(up1_ready, 1)
                dve.wait_ge(up1_ready, n + 1)
                ts(up[b][:], up[b][:], -LIMIT, 1.0, ALU.max, ALU.add).then_inc(up_ready, 1)
                if n >= 2:
                    times_score(n - 2)
            times_score(len(units) - 2)
            times_score(len(units) - 1)
    st.close()


def l3_ffn(nc, g, a):
    layernorm_transpose(nc, g, "l3f_ln")
    router(nc, g, "l3r", 16, a["L3_ffn_router_weight"])
    l3_experts(nc, g, a)
    project_add(nc, g, "l3f_out", g.CT, None)


QB = 16
FF = 352
FB = FF // QB


class Fp4:
    DVE_STEPS = 13

    def __init__(self, st, name, blocks):
        self.n = blocks
        self.mag, self.sgn, self.acc, self.low = (st.sb(name + s, [P, blocks, QB]) for s in ("mag", "sgn", "acc", "low"))
        self.scale, self.inv = st.sb(name + "scale", [P, blocks]), st.sb(name + "inv", [P, blocks])
        self.act_step, self.dve_step = st.sem(name + "act_step"), st.sem(name + "dve_step")
        self.low_step = st.sem(name + "low_step")

    def on_act(self, nc, x):
        nc.scalar.activation(self.mag[:], x, ACT.Abs).then_inc(self.act_step, 1)
        nc.scalar.activation(self.sgn[:], x, ACT.Sign).then_inc(self.act_step, 1)

    def on_pool(self, nc, pool, turn=0):
        pool.wait_ge(self.dve_step, turn * self.DVE_STEPS + 4)
        nc.gpsimd.tensor_scalar(self.low[:], self.mag[:], 1.75, None, ALU.is_gt).then_inc(self.low_step, 1)

    def on_dve(self, nc, dve, x, turn=0):
        count = [turn * self.DVE_STEPS]

        def chain(ins):
            ins.then_inc(self.dve_step, 1)
            count[0] += 1
            dve.wait_ge(self.dve_step, count[0])
        mag, acc = self.mag[:], self.acc[:]
        stt, tt, ts = nc.vector.scalar_tensor_tensor, nc.vector.tensor_tensor, nc.vector.tensor_scalar
        wide = self.scale[:].unsqueeze(2).broadcast_to([P, self.n, QB])
        dve.wait_ge(self.act_step, 2 * turn + 1)
        chain(nc.vector.tensor_reduce(self.scale[:], mag, AX.X, ALU.max))
        chain(ts(self.scale[:], self.scale[:], float(np.float32(1) / np.float32(6)), 1e-12, ALU.mult, ALU.max))
        chain(nc.vector.reciprocal(self.inv[:], self.scale[:]))
        chain(tt(mag, mag, self.inv[:].unsqueeze(2).broadcast_to([P, self.n, QB]), ALU.mult))
        chain(ts(acc, mag, 5.0, 2.0, ALU.is_gt, ALU.mult))
        chain(stt(out=acc, in0=mag, scalar=3.5, in1=acc, op0=ALU.is_gt, op1=ALU.add))
        chain(stt(out=acc, in0=mag, scalar=2.5, in1=acc, op0=ALU.is_gt, op1=ALU.add))
        dve.wait_ge(self.low_step, turn + 1)
        chain(stt(out=acc, in0=acc, scalar=2.0, in1=self.low[:], op0=ALU.mult, op1=ALU.add))
        for mid in (1.25, 0.75, 0.25):
            chain(stt(out=acc, in0=mag, scalar=mid, in1=acc, op0=ALU.is_gt, op1=ALU.add))
        dve.wait_ge(self.act_step, 2 * turn + 2)
        chain(stt(out=acc, in0=acc, scalar=0.5, in1=self.sgn[:], op0=ALU.mult, op1=ALU.mult))
        chain(tt(x, acc, wide, ALU.mult))


def l0_ffn(nc, g, a):
    big = Stage(nc, "l0f")
    KC = ((0, P), (P, P), (2 * P, FF - 2 * P))
    wT = big.sb("wT", [P, 2, FF])
    dT = big.sb("dT", [P, 3, P])
    xn = big.sb("xn", [P, NT, P])
    layernorm_transpose(nc, g, "l0f_ln", keep_rows=xn)

    st = Stage(nc, "l0w")
    nb = 6 * (P // QB) + FB
    wr = st.sb("wr", [P, nb, QB])
    q = Fp4(st, "w", nb)
    qx = Fp4(st, "x", NT * P // QB)
    psT = [st.ps(f"psT{i}") for i in range(5)]
    zeroed, loaded, transposed, copied = st.sem("zeroed"), st.sem("loaded"), st.sem("transposed"), st.sem("copied")
    flat = wr[:].rearrange("p n q -> p (n q)")
    xb = xn[:].rearrange("p t (n q) -> p (t n) q", q=QB)
    with st.block() as block:
        @block.gpsimd
        def _(pool):
            nc.gpsimd.memset(wr[:], 0.0).then_inc(zeroed, 1)
            qx.on_pool(nc, pool)
            q.on_pool(nc, pool)

        @block.sync
        def _(sp):
            sp.wait_ge(zeroed, 1)
            for i, n in enumerate(("L0_ffn_w_gate", "L0_ffn_w_up")):
                for k, (lo, m) in enumerate(KC):
                    sp.dma_start(flat[0:m, (3 * i + k) * P:(3 * i + k + 1) * P], a[n][lo:lo + m, :]).then_inc(loaded, 16)
            sp.dma_start(flat[:, 6 * P:6 * P + FF], a["L0_ffn_w_down"]).then_inc(loaded, 16)

        @block.scalar
        def _(act):
            qx.on_act(nc, xb)
            act.wait_ge(loaded, 16 * 7)
            q.on_act(nc, wr[:])
            for c in range(NC):
                act.wait_ge(transposed, c + 1)
                nc.scalar.activation(g.XnT[:, c * CH:(c + 1) * CH], psT[3 + c % 2][:], ACT.Copy).then_inc(copied, 1)
            for n in range(3):
                act.wait_ge(transposed, NC + n + 1)
                if n < 2:
                    nc.scalar.activation(wT[:, n, :], psT[n][:, 0:FF], ACT.Copy).then_inc(copied, 1)
                else:
                    for k, (lo, m) in enumerate(KC):
                        nc.scalar.activation(dT[0:m, k, :], psT[2][0:m, k * P:(k + 1) * P], ACT.Copy).then_inc(copied, 1)

        @block.vector
        def _(dve):
            qx.on_dve(nc, dve, xb)
            q.on_dve(nc, dve, wr[:])

        @block.tensor
        def _(pe):
            pe.wait_ge(qx.dve_step, qx.DVE_STEPS)
            for c in range(NC):
                if c >= 2:
                    pe.wait_ge(copied, c - 1)
                for t in range(4 * c, 4 * c + 4):
                    ins = nc.tensor.transpose(psT[3 + c % 2][:, t % 4 * P:(t % 4 + 1) * P], xn[:, t, :], g.ident[:])
                ins.then_inc(transposed, 1)
            pe.wait_ge(q.dve_step, q.DVE_STEPS)
            for n in range(2):
                for k, (lo, m) in enumerate(KC):
                    ins = nc.tensor.transpose(psT[n][:, lo:lo + m], flat[0:m, (3 * n + k) * P:(3 * n + k + 1) * P], g.ident[0:m, 0:m])
                ins.then_inc(transposed, 1)
            for k, (lo, m) in enumerate(KC):
                ins = nc.tensor.transpose(psT[2][0:m, k * P:(k + 1) * P], flat[:, 6 * P + lo:6 * P + lo + m], g.ident[:])
            ins.then_inc(transposed, 1)
    st.close()

    st = Stage(nc, "l0h")
    hid = [st.sb(f"hid{i}", [P, 4, FF]) for i in range(3)]
    sg = [st.sb(f"sg{i}", [P, FF]) for i in range(2)]
    qg = [Fp4(st, f"h{i}", 4 * FB) for i in range(2)]
    hT = [st.sb(f"hT{i}", [P, 3, CH]) for i in range(2)]
    psG = [st.ps(f"psG{i}") for i in range(2)]
    psU = [st.ps(f"psU{i}") for i in range(2)]
    psH = [st.ps(f"psH{i}") for i in range(3)]
    psO = st.ps("psO")
    in_done, silu_ready, hid_ready, transposed, copied, out_done, out_added = [st.sem(n) for n in (
        "in_done", "silu_ready", "hid_ready", "transposed", "copied", "out_done", "out_added")]
    with st.block() as block:
        @block.tensor
        def _(pe):
            def inputs(t):
                if t >= 2:
                    pe.wait_ge(hid_ready, t - 1)
                for ps, i in ((psG, 0), (psU, 1)):
                    ins = nc.tensor.matmul(ps[t % 2][:, 0:FF], g.XnT[:, t * P:(t + 1) * P], wT[:, i, :], start=True, stop=True)
                ins.then_inc(in_done, 1)

            def down(c):
                b = c % 2
                pe.wait_ge(qg[b].dve_step, qg[b].DVE_STEPS * (c // 2 + 1))
                for k, (lo, m) in enumerate(KC):
                    pe.wait_ge(copied, 3 * c + k - 2) if 3 * c + k - 2 > 0 else None
                    for t in range(4):
                        ins = nc.tensor.transpose(psH[k][0:m, t * P:(t + 1) * P], hid[c % 3][:, t, lo:lo + m], g.ident[:])
                    ins.then_inc(transposed, 1)
                if c:
                    pe.wait_ge(out_added, c)
                pe.wait_ge(copied, 3 * c + 3)
                for t in range(4):
                    for k, (lo, m) in enumerate(KC):
                        ins = nc.tensor.matmul(psO[:, t * P:(t + 1) * P], hT[b][0:m, k, t * P:(t + 1) * P], dT[0:m, k, :],
                                               start=k == 0, stop=k == 2, skip_group_check=True)
                ins.then_inc(out_done, 1)

            for c in range(NC):
                for t in range(4 * c, 4 * c + 4):
                    inputs(t)
                if c >= 2:
                    down(c - 2)
            down(NC - 2)
            down(NC - 1)

        @block.gpsimd
        def _(pool):
            for c in range(NC):
                qg[c % 2].on_pool(nc, pool, c // 2)

        def evacuate(act, c):
            for k, (lo, m) in enumerate(KC):
                act.wait_ge(transposed, 3 * c + k + 1)
                if c >= 2:
                    act.wait_ge(out_done, c - 1)
                nc.scalar.activation(hT[c % 2][0:m, k, :], psH[k][0:m, :], ACT.Copy).then_inc(copied, 1)

        @block.scalar
        def _(act):
            for c in range(NC):
                b = c % 2
                for t in range(4 * c, 4 * c + 4):
                    act.wait_ge(in_done, t + 1)
                    if t >= 2:
                        act.wait_ge(hid_ready, t - 1)
                    nc.scalar.activation(sg[t % 2][:], psG[t % 2][:, 0:FF], ACT.Silu).then_inc(silu_ready, 1)
                if c >= 2:
                    evacuate(act, c - 2)
                act.wait_ge(hid_ready, 4 * c + 4)
                if c >= 2:
                    act.wait_ge(qg[b].dve_step, qg[b].DVE_STEPS * (c // 2))
                qg[b].on_act(nc, hid[c % 3][:].rearrange("p t (n q) -> p (t n) q", q=QB))
            evacuate(act, NC - 2)
            evacuate(act, NC - 1)

        @block.vector
        def _(dve):

            def add_out(c):
                dve.wait_ge(out_done, c + 1)
                x = g.X[:, 4 * c:4 * c + 4, :].rearrange("p t d -> p (t d)")
                nc.vector.tensor_tensor(x, x, psO[:], ALU.add).then_inc(out_added, 1)

            def hidden(c):
                for t in range(4 * c, 4 * c + 4):
                    dve.wait_ge(silu_ready, t + 1)
                    if c >= 3:
                        dve.wait_ge(transposed, 3 * (c - 2))
                    nc.vector.tensor_tensor(hid[c % 3][:, t % 4, :], sg[t % 2][:], psU[t % 2][:, 0:FF], ALU.mult).then_inc(hid_ready, 1)

            hidden(0)
            for c in range(NC):
                if c + 1 < NC:
                    hidden(c + 1)
                qg[c % 2].on_dve(nc, dve, hid[c % 3][:].rearrange("p t (n q) -> p (t n) q", q=QB), c // 2)
                if c:
                    add_out(c - 1)
            add_out(NC - 1)
    st.close()
    big.close()


def l3_attn(nc, g, a):
    DI, DS, NH, HP, TAPS = 256, 128, 4, 64, 4
    KT = (DI + 2 * DS) // P
    layernorm_transpose(nc, g, "l3a_ln")
    big = Stage(nc, "l3a")
    F = big.sb("F", [P, KT, S])
    zs = big.sb("zs", [P, NT, DI])
    dt = big.sb("dt", [P, NT, NH])
    ac, acs, tot = big.sb("ac", [P, NT, NH]), big.sb("acs", [P, NT, NH]), big.sb("tot", [P, NT, NH])
    decay = big.sb("decay", [P, NT, NH])
    incl, strict = big.sb("incl", [P, P]), big.sb("strict", [P, P])

    st = Stage(nc, "l3p")
    w = st.sb("w", [P, 2 * DI + 2 * DS + NH])
    cw, cb = st.sb("cw", [P, KT, TAPS]), st.sb("cb", [P, KT])
    U = st.sb("U", [P, KT, TAPS - 1 + S])
    acc = [st.sb(f"acc{i}", [P, S]) for i in range(2)]
    dtb, al = st.sb("dtb", [P, NH]), st.sb("al", [P, NH])
    raw, e, u, d, z0 = [st.sb(n, [P, NT, NH]) for n in ("raw", "e", "u", "d", "z0")]
    psC = [st.ps(f"psC{i}") for i in range(4)]
    psZ = [st.ps(f"psZ{i}") for i in range(2)]
    psD = st.ps("psD")
    loaded, u_zeroed, ch_done, u_ready, z_done, z_ready, conv_step, conv_ready, dt_done, sp_step, sp_act, sums_done, built = [
        st.sem(n) for n in ("loaded", "u_zeroed", "ch_done", "u_ready", "z_done", "z_ready", "conv_step", "conv_ready",
                            "dt_done", "sp_step", "sp_act", "sums_done", "built")]
    with st.block() as block:
        @block.sync
        def _(sp):
            for dst, src in ((w[:], a["L3_attn_in_proj_wT"]),
                             (cw[:], a["L3_attn_conv_w"].rearrange("(k p) j -> p k j", p=P)),
                             (cb[:], a["L3_attn_conv_b"].rearrange("(k p) -> p k", p=P)),
                             (dtb[:], bcast_row(a["L3_attn_dt_bias"], NH)), (al[:], bcast_row(a["L3_attn_A_log"], NH))):
                sp.dma_start(dst, src, allow_slow_non_contiguous=True).then_inc(loaded, 16)

        @block.gpsimd
        def _(pool):
            nc.gpsimd.memset(U[:, :, 0:TAPS - 1], 0.0).then_inc(u_zeroed, 1)
            nc.gpsimd.memset(incl[:], 1.0).then_inc(built, 1)
            nc.gpsimd.memset(strict[:], 1.0).then_inc(built, 1)
            pool.wait_ge(built, 2)
            nc.gpsimd.affine_select(out=incl[:], in_=incl[:], compare_op=ALU.is_ge, fill=0.0, base=0,
                                    pattern=[[1, P]], channel_multiplier=-1).then_inc(built, 1)
            nc.gpsimd.affine_select(out=strict[:], in_=strict[:], compare_op=ALU.is_gt, fill=0.0, base=0,
                                    pattern=[[-1, P]], channel_multiplier=1).then_inc(built, 1)

        @block.tensor
        def _(pe):
            pe.wait_ge(loaded, 80)
            for t in range(NT):
                nc.tensor.matmul(psD[:, t * NH:(t + 1) * NH], g.XnT[:, t * P:(t + 1) * P], w[:, 2 * DI + 2 * DS:],
                                 start=True, stop=True, skip_group_check=True).then_inc(dt_done, 1)
            for n in range(KT * NC):
                k, c = n // NC, n % NC
                if n >= 4:
                    pe.wait_ge(u_ready, n - 3)
                nc.tensor.matmul(psC[n % 4][:], w[:, DI + k * P:DI + (k + 1) * P], g.XnT[:, c * CH:(c + 1) * CH],
                                 start=True, stop=True).then_inc(ch_done, 1)
            for t in range(NT):
                if t >= 2:
                    pe.wait_ge(z_ready, t - 1)
                nc.tensor.matmul(psZ[t % 2][:, 0:DI], g.XnT[:, t * P:(t + 1) * P], w[:, 0:DI],
                                 start=True, stop=True).then_inc(z_done, 1)
            pe.wait_ge(sp_step, 12)
            pe.wait_ge(built, 4)
            ac2 = ac[:].rearrange("p t h -> p (t h)")
            nc.tensor.matmul(psC[0][:, 0:NT * NH], incl[:], ac2, start=True, stop=True).then_inc(sums_done, 1)
            nc.tensor.matmul(psC[1][:, 0:NT * NH], g.ones[:], ac2, start=True, stop=True).then_inc(sums_done, 1)

        @block.scalar
        def _(act):
            act.wait_ge(loaded, 80)
            act.wait_ge(sp_step, 2)
            nc.scalar.activation(e[:], d[:], ACT.Exp).then_inc(sp_act, 1)
            nc.scalar.activation(al[:], al[:], ACT.Exp).then_inc(sp_act, 1)
            act.wait_ge(sp_step, 3)
            nc.scalar.activation(z0[:], u[:], ACT.Ln).then_inc(sp_act, 1)
            for n in range(KT * NC):
                k, c = n // NC, n % NC
                act.wait_ge(ch_done, n + 1)
                nc.scalar.activation(U[:, k, TAPS - 1 + c * CH:TAPS - 1 + (c + 1) * CH], psC[n % 4][:],
                                     ACT.Copy).then_inc(u_ready, 1)
            for t in range(NT):
                act.wait_ge(z_done, t + 1)
                nc.scalar.activation(zs[:, t, :], psZ[t % 2][:, 0:DI], ACT.Silu).then_inc(z_ready, 1)
            for k in range(KT):
                act.wait_ge(conv_step, TAPS * (k + 1))
                nc.scalar.activation(F[:, k, :], acc[k % 2][:], ACT.Silu, bias=cb[:, k:k + 1]).then_inc(conv_ready, 1)
            act.wait_ge(sp_step, 15)
            nc.scalar.activation(decay[:], decay[:], ACT.Exp).then_inc(sp_act, 1)
            nc.scalar.activation(acs[:], acs[:], ACT.Exp).then_inc(sp_act, 1)
            nc.scalar.activation(tot[:], tot[:], ACT.Exp).then_inc(sp_act, 1)

        @block.vector
        def _(dve):
            n = [0]

            def chain(ins):
                ins.then_inc(sp_step, 1)
                n[0] += 1
                dve.wait_ge(sp_step, n[0])
            tt, ts, stt = nc.vector.tensor_tensor, nc.vector.tensor_scalar, nc.vector.scalar_tensor_tensor
            dve.wait_ge(dt_done, NT)
            dve.wait_ge(loaded, 80)
            chain(tt(raw[:], psD[:, 0:NT * NH].rearrange("p (t h) -> p t h", h=NH),
                     dtb[:].unsqueeze(1).broadcast_to([P, NT, NH]), ALU.add))
            chain(stt(out=d[:], in0=raw[:], scalar=-1.0, in1=raw[:], op0=ALU.mult, op1=ALU.min))
            dve.wait_ge(sp_act, 1)
            chain(ts(u[:], e[:], 1.0, None, ALU.add))
            chain(ts(d[:], u[:], -1.0, None, ALU.add))
            dve.wait_ge(sp_act, 3)
            chain(ts(u[:], d[:], 0.0, None, ALU.is_equal))
            chain(tt(d[:], d[:], u[:], ALU.add))
            chain(nc.vector.reciprocal(d[:], d[:]))
            chain(tt(d[:], d[:], z0[:], ALU.mult))
            chain(tt(d[:], d[:], u[:], ALU.add))
            chain(tt(d[:], d[:], e[:], ALU.mult))
            chain(stt(out=dt[:], in0=raw[:], scalar=0.0, in1=d[:], op0=ALU.max, op1=ALU.add))
            chain(stt(out=ac[:], in0=dt[:], scalar=-1.0, in1=al[:].unsqueeze(1).broadcast_to([P, NT, NH]),
                      op0=ALU.mult, op1=ALU.mult))
            dve.wait_ge(u_zeroed, 1)
            m = 0
            for k in range(KT):
                dve.wait_ge(u_ready, NC * (k + 1))
                if k >= 2:
                    dve.wait_ge(conv_ready, k - 1)
                for j in range(TAPS):
                    if j == 0:
                        ins = ts(acc[k % 2][:], U[:, k, 0:S], cw[:, k, 0:1], None, ALU.mult)
                    else:
                        ins = stt(out=acc[k % 2][:], in0=U[:, k, j:j + S], scalar=cw[:, k, j:j + 1], in1=acc[k % 2][:],
                                  op0=ALU.mult, op1=ALU.add)
                    ins.then_inc(conv_step, 1)
                    m += 1
                    dve.wait_ge(conv_step, m)
            dve.wait_ge(sums_done, 2)
            chain(nc.vector.tensor_copy(acs[:], psC[0][:, 0:NT * NH].rearrange("p (t h) -> p t h", h=NH)))
            chain(nc.vector.tensor_copy(tot[:], psC[1][:, 0:NT * NH].rearrange("p (t h) -> p t h", h=NH)))
            chain(tt(decay[:], tot[:], acs[:], ALU.subtract))
    st.close()

    st = Stage(nc, "l3c")
    R = [st.sb(f"R{i}", [P, NH, P]) for i in range(2)]
    E = [st.sb(f"E{i}", [P, NH, P]) for i in range(2)]
    cbm = [st.sb(f"cbm{i}", [P, P]) for i in range(2)]
    rows = [st.sb(f"rows{i}", [P, 3 * P]) for i in range(2)]
    xdt = [st.sb(f"xdt{i}", [P, NH, HP]) for i in range(2)]
    xdd = [st.sb(f"xdd{i}", [P, NH, HP]) for i in range(2)]
    yrow = st.sb("yrow", [P, NT, DI])
    state = [st.sb(f"state{i}", [P, NH, HP]) for i in range(2)]
    skip = st.sb("skip", [P, NH])
    ssq, rms = st.sb("ssq", [P, NT]), st.sb("rms", [P, NT])
    sqb = [st.sb(f"sqb{i}", [P, DI]) for i in range(2)]
    yT = st.sb("yT", [P, 2, S])
    ow, nw = st.sb("ow", [P, 2, P]), st.sb("nw", [P, 2])
    psB = [st.ps(f"psB{i}") for i in range(2)]
    psX = [st.ps(f"psX{i}") for i in range(2)]
    psG = [st.ps(f"psG{i}") for i in range(2)]
    psY = [st.ps(f"psY{i}") for i in range(2)]
    loaded, r_ready, pre_done, seg_done, cbm_ready, rows_ready, e_ready, m_ready, x_ready, y_done, s_done, s_step, y_step = [
        st.sem(n) for n in ("loaded", "r_ready", "pre_done", "seg_done", "cbm_ready", "rows_ready", "e_ready", "m_ready",
                            "x_ready", "y_done", "s_done", "s_step", "y_step")]
    YS = 5
    with st.block() as block:
        @block.sync
        def _(sp):
            sp.dma_start(skip[:], bcast_row(a["L3_attn_D"], NH)).then_inc(loaded, 16)
            sp.dma_start(ow[:], a["L3_attn_out_proj_wT"].rearrange("(k p) d -> p k d", p=P)).then_inc(loaded, 16)
            sp.dma_start(nw[:], a["L3_attn_norm_w"].rearrange("(k p) -> p k", p=P), allow_slow_non_contiguous=True).then_inc(loaded, 16)

        @block.gpsimd
        def _(pool):
            def ramp(c):
                if c >= 2:
                    pool.wait_ge(seg_done, c - 1)
                nc.gpsimd.tensor_tensor(R[c % 2][:], incl[:].unsqueeze(1).broadcast_to([P, NH, P]),
                                        ac[:, c, :].unsqueeze(2).broadcast_to([P, NH, P]), ALU.mult).then_inc(r_ready, 1)
            ramp(0)
            for c in range(NT):
                if c + 1 < NT:
                    ramp(c + 1)
                pool.wait_ge(e_ready, c + 1)
                pool.wait_ge(cbm_ready, c + 1)
                nc.gpsimd.tensor_tensor(E[c % 2][:], E[c % 2][:], cbm[c % 2][:].unsqueeze(1).broadcast_to([P, NH, P]),
                                        ALU.mult).then_inc(m_ready, 1)

        @block.tensor
        def _(pe):
            mm = nc.tensor.matmul

            def pre(c):
                b, cs = c % 2, slice(c * P, (c + 1) * P)
                if c >= 2:
                    pe.wait_ge(cbm_ready, c - 1)
                    pe.wait_ge(rows_ready, c - 1)
                    pe.wait_ge(s_step, 2 * c - 1)
                mm(psB[b][:, 0:P], F[:, 2, cs], F[:, 3, cs], start=True, stop=True)
                for k in range(3):
                    ins = nc.tensor.transpose(psX[b][:, k * P:(k + 1) * P], F[:, k, cs], g.ident[:])
                ins.then_inc(pre_done, 1)
                pe.wait_ge(r_ready, c + 1)
                if c >= 2:
                    pe.wait_ge(e_ready, c - 1)
                mm(psG[b][:], strict[:], R[b][:].rearrange("p h l -> p (h l)"), start=True, stop=True).then_inc(seg_done, 1)

            def post(c):
                b, cs = c % 2, slice(c * P, (c + 1) * P)
                pe.wait_ge(x_ready, 2 * c + 2)
                pe.wait_ge(rows_ready, c + 1)
                pe.wait_ge(cbm_ready, c + 1)
                mm(psB[b][:, P:P + DI], rows[b][:, 2 * P:3 * P], xdd[b][:].rearrange("p h d -> p (h d)"),
                   start=True, stop=True, skip_group_check=True).then_inc(s_done, 1)
                pe.wait_ge(m_ready, c + 1)
                if c >= 2:
                    pe.wait_ge(y_step, YS * (c - 1))
                for h in range(NH):
                    mm(psY[b][:, h * HP:(h + 1) * HP], E[b][:, h, :], xdt[b][:, h, :], start=True, stop=True,
                       skip_group_check=True)
                pe.wait_ge(s_step, 2 * c + 1)
                mm(psY[b][:, DI:2 * DI], F[:, 3, cs], state[b][:].rearrange("p h d -> p (h d)"),
                   start=True, stop=True, skip_group_check=True).then_inc(y_done, 1)

            pre(0)
            for c in range(NT):
                if c + 1 < NT:
                    pre(c + 1)
                post(c)

        @block.scalar
        def _(act):
            def rows_out(c):
                b = c % 2
                act.wait_ge(pre_done, c + 1)
                if c >= 2:
                    act.wait_ge(y_step, YS * (c - 1))
                    act.wait_ge(s_done, c - 1)
                nc.scalar.activation(rows[b][:], psX[b][:, 0:3 * P], ACT.Copy).then_inc(rows_ready, 1)
                act.wait_ge(seg_done, c + 1)
                if c >= 2:
                    act.wait_ge(y_done, c - 1)
                nc.scalar.activation(E[b][:].rearrange("p h l -> p (h l)"), psG[b][:], ACT.Exp).then_inc(e_ready, 1)
            for c in range(NT):
                rows_out(c)

        @block.vector
        def _(dve):
            tt, ts = nc.vector.tensor_tensor, nc.vector.tensor_scalar
            nc.vector.memset(state[0][:], 0.0).then_inc(s_step, 1)

            def wide(x, c):
                return x[:, c, :].unsqueeze(2).broadcast_to([P, NH, HP])

            def before(c):
                b = c % 2
                dve.wait_ge(pre_done, c + 1)
                if c >= 2:
                    dve.wait_ge(m_ready, c - 1)
                tt(cbm[b][:], psB[b][:, 0:P], incl[:], ALU.mult).then_inc(cbm_ready, 1)
                dve.wait_ge(rows_ready, c + 1)
                if c >= 2:
                    dve.wait_ge(y_done, c - 1)
                    dve.wait_ge(s_done, c - 1)
                x = rows[b][:, 0:DI].rearrange("p (h d) -> p h d", h=NH)
                tt(xdt[b][:], x, wide(dt, c), ALU.mult).then_inc(x_ready, 1)
                dve.wait_ge(x_ready, 2 * c + 1)
                tt(xdd[b][:], xdt[b][:], wide(decay, c), ALU.mult).then_inc(x_ready, 1)

            def after(c):
                b = c % 2
                dve.wait_ge(s_done, c + 1)
                dve.wait_ge(s_step, 2 * c + 1)
                if c:
                    dve.wait_ge(y_done, c)
                nxt = state[1 - b][:]
                tt(nxt, state[b][:], wide(tot, c), ALU.mult).then_inc(s_step, 1)
                dve.wait_ge(s_step, 2 * c + 2)
                tt(nxt, nxt, psB[b][:, P:P + DI].rearrange("p (h d) -> p h d", h=NH), ALU.add).then_inc(s_step, 1)
                dve.wait_ge(y_done, c + 1)
                y = yrow[:, c, :].rearrange("p (h d) -> p h d", h=NH)
                x = rows[b][:, 0:DI].rearrange("p (h d) -> p h d", h=NH)
                pw = psY[b][:, 0:DI].rearrange("p (h d) -> p h d", h=NH)
                pt = psY[b][:, DI:2 * DI].rearrange("p (h d) -> p h d", h=NH)
                if c == 0:
                    dve.wait_ge(loaded, 48)
                tt(y, pt, wide(acs, c), ALU.mult).then_inc(y_step, 1)
                dve.wait_ge(y_step, YS * c + 1)
                tt(y, y, pw, ALU.add).then_inc(y_step, 1)
                tt(x, x, skip[:].unsqueeze(2).broadcast_to([P, NH, HP]), ALU.mult).then_inc(y_step, 1)
                dve.wait_ge(y_step, YS * c + 3)
                tt(y, y, x, ALU.add).then_inc(y_step, 1)
                dve.wait_ge(y_step, YS * c + 4)
                tt(y, y, zs[:, c, :].rearrange("p (h d) -> p h d", h=NH), ALU.mult).then_inc(y_step, 1)

            before(0)
            for c in range(NT):
                if c + 1 < NT:
                    before(c + 1)
                after(c)
    st2 = Stage(nc, "l3o")
    scaled, squared, rms_step, t_done, t_ready, o_done, o_added = [
        st2.sem(n) for n in ("scaled", "squared", "rms_step", "t_done", "t_ready", "o_done", "o_added")]
    with st2.block() as block:
        @block.vector
        def _(dve):
            for k in range(2):
                nc.vector.tensor_scalar(ow[:, k, :], ow[:, k, :], nw[:, k:k + 1], None, ALU.mult).then_inc(scaled, 1)
            dve.wait_ge(rms_step, 1)
            nc.vector.reciprocal(rms[:], rms[:]).then_inc(rms_step, 1)
            dve.wait_ge(rms_step, 2)
            for t in range(NT):
                dve.wait_ge(o_done, t // 4 * 4 + 4)
                nc.vector.scalar_tensor_tensor(out=g.X[:, t, :], in0=psG[t // 4 % 2][:, t % 4 * P:(t % 4 + 1) * P],
                                               scalar=rms[:, t:t + 1], in1=g.X[:, t, :], op0=ALU.mult,
                                               op1=ALU.add).then_inc(o_added, 1)

        @block.tensor
        def _(pe):
            for n in range(2 * NC):
                k, c = n // NC, n % NC
                if n >= 4:
                    pe.wait_ge(t_ready, n - 3)
                for t in range(4 * c, 4 * c + 4):
                    ins = nc.tensor.transpose((psB + psX)[n % 4][:, t % 4 * P:(t % 4 + 1) * P], yrow[:, t, k * P:(k + 1) * P],
                                              g.ident[:])
                ins.then_inc(t_done, 1)
            pe.wait_ge(scaled, 2)
            for t in range(NT):
                pe.wait_ge(t_ready, NC + t // 4 + 1)
                if t % 4 == 0 and t >= 8:
                    pe.wait_ge(o_added, 4 * (t // 4 - 1))
                for k in range(2):
                    ins = nc.tensor.matmul(psG[t // 4 % 2][:, t % 4 * P:(t % 4 + 1) * P], yT[:, k, t * P:(t + 1) * P],
                                           ow[:, k, :], start=k == 0, stop=k == 1, skip_group_check=True)
                ins.then_inc(o_done, 1)

        @block.scalar
        def _(act):
            for t in range(NT):
                if t >= 2:
                    act.wait_ge(squared, t - 1)
                nc.scalar.activation(sqb[t % 2][:], yrow[:, t, :], ACT.Square, accum_out=ssq[:, t:t + 1]).then_inc(squared, 1)
            act.wait_ge(squared, NT)
            nc.scalar.activation(rms[:], ssq[:], ACT.Sqrt, bias=1e-5, scale=1.0 / DI).then_inc(rms_step, 1)
            for n in range(2 * NC):
                k, c = n // NC, n % NC
                act.wait_ge(t_done, n + 1)
                nc.scalar.activation(yT[:, k, c * CH:(c + 1) * CH], (psB + psX)[n % 4][:], ACT.Copy).then_inc(t_ready, 1)
    st2.close()
    st.close()
    big.close()


BH, BD = 8, 64
BI = BH * BD
BW = 64
FH = 341
F_CHUNKS = ((0, P), (P, P), (2 * P, FH - 2 * P))
MAGNIFY = 8.0


def rotary_tables():
    half = np.arange(0, BD, 2, dtype=np.float32)
    inv = (np.float32(1.0) / np.float32(10000.0) ** (half / np.float32(BD))).astype(np.float32)
    t = np.arange(S, dtype=np.float32)
    freqs = np.concatenate([t[:, None] * inv[None, :]] * 2, -1).astype(np.float32)
    base = ((half + np.float32(0.4 * BD)) / np.float32(1.4 * BD)).astype(np.float32)
    power = ((t - S // 2) / np.float32(BW // 2)).astype(np.float32)
    scale = np.concatenate([(base[None, :] ** power[:, None]).astype(np.float32)] * 2, -1)
    cos, sin = np.cos(freqs), np.sin(freqs)
    sign = np.concatenate([-np.ones(BD // 2), np.ones(BD // 2)]).astype(np.float32)
    out = np.stack([np.stack([cos * scale, sin * scale * sign], 1), np.stack([cos / scale, sin / scale * sign], 1)], 1)
    return np.ascontiguousarray(out.astype(np.float32).reshape(S, 4 * BD))


def shift_rows(nc, g, name, R, Hs):
    st = Stage(nc, name)
    zeroed, shifted, copied = st.sem("zeroed"), st.sem("shifted"), st.sem("copied")
    lo = P // 2
    with st.block() as block:
        @block.sync
        def _(sp):
            sp.dma_start(Hs[1:P, :, lo:P], R[0:P - 1, :, lo:P]).then_inc(shifted, 16)
            sp.dma_start(Hs[0:1, 1:NT, lo:P], R[P - 1:P, 0:NT - 1, lo:P]).then_inc(shifted, 16)
            sp.wait_ge(shifted, 32)

        @block.vector
        def _(dve):
            nc.vector.memset(Hs[0:1, 0, lo:P], 0.0).then_inc(zeroed, 1)
            nc.vector.tensor_copy(Hs[:, :, 0:lo], R[:, :, 0:lo]).then_inc(copied, 1)
    st.close()


def local_qkv(nc, g, name, w_dram, qs, ks, rot, qz, kT, V):
    st = Stage(nc, name)
    w = st.sb("w", [P, 3 * BI])
    tab = [st.sb(f"tab{i}", [P, 2, 2, BD]) for i in range(2)]
    gain = st.sb("gain", [P, 2, 2, BD])
    sq = st.sb("sq", [P, 2 * BH, BD])
    nrm = [st.sb(f"nrm{i}", [P, 2 * BH]) for i in range(2)]
    swp = [st.sb("swp", [P, 2 * BI])] * 2
    two = g.CT[:].rearrange("p (b n) -> p b n", b=2)
    tmp = g.V[:].rearrange("p t d -> p (t d)").rearrange("p (b n) -> p b n", b=2)
    psP = [st.ps(f"psP{i}", 3 * CH) for i in range(2)]
    psT = [st.ps(f"psT{i}") for i in range(2)]
    loaded, tab_loaded, tab_ready, q_zeroed = st.sem("loaded"), [st.sem("tab_loaded0"), st.sem("tab_loaded1")], st.sem("tab_ready"), st.sem("q_zeroed")
    projected, v_ready, qk_ready, squared, norm2_ready, norm_ready, norm_step, same_ready, rot_step, turned, q_out, k_out = [
        st.sem(n) for n in ("projected", "v_ready", "qk_ready", "squared", "norm2_ready", "norm_ready", "norm_step",
                            "same_ready", "rot_step", "turned", "q_out", "k_out")]

    def heads(x, b):
        return x[:, b, :].rearrange("p (h d) -> p h d", d=BD)

    with st.block() as block:
        @block.sync
        def _(sp):
            sp.dma_start(w[:], w_dram).then_inc(loaded, 16)
            for i, s in enumerate((qs, ks)):
                sp.dma_start(gain[:, i, 0, :], bcast_row(s, BD)).then_inc(loaded, 16)
                for lo in (0, BD // 2):
                    hi = BD // 2 - lo
                    sp.dma_start(gain[:, i, 1, lo:lo + BD // 2], bcast_row(s[hi:hi + BD // 2], BD // 2)).then_inc(loaded, 16)
            for t in range(NT):
                if t >= 2:
                    sp.wait_ge(rot_step, 4 * (t - 1))
                    sp.wait_ge(same_ready, t - 1)
                sp.dma_start(tab[t % 2][:].rearrange("p a b d -> p (a b d)"), rot[t * P:(t + 1) * P, :]).then_inc(tab_loaded[t % 2], 16)

        @block.tensor
        def _(pe):
            def project(t):
                if t >= 2:
                    pe.wait_ge(v_ready, t - 1)
                    pe.wait_ge(qk_ready, t - 1)
                    pe.wait_ge(squared, t - 1)
                for j in range(3):
                    ins = nc.tensor.matmul(psP[t % 2][:, j * BI:(j + 1) * BI], g.XnT[:, t * P:(t + 1) * P],
                                           w[:, j * BI:(j + 1) * BI], start=True, stop=True)
                ins.then_inc(projected, 1)

            def turn(t):
                pe.wait_ge(rot_step, 4 * (t + 1))
                for i in range(2):
                    if t:
                        pe.wait_ge((q_out, k_out)[i], (2 * t, t)[i])
                    for j in range(4):
                        ins = nc.tensor.transpose(psT[i][:, j * P:(j + 1) * P], tmp[:, t % 2, (4 * i + j) * P:(4 * i + j + 1) * P],
                                                  g.ident[:])
                    ins.then_inc(turned, 1)

            pe.wait_ge(loaded, 16 * 7)
            project(0)
            project(1)
            for t in range(NT):
                if t + 2 < NT:
                    project(t + 2)
                turn(t)

        @block.scalar
        def _(act):
            def outs(t):
                act.wait_ge(q_zeroed, 2)
                act.wait_ge(turned, 2 * t + 1)
                for half in range(2):
                    rows = slice(64 * half, 64 * half + 64)
                    nc.scalar.activation(qz[rows, half, :, t * P:(t + 1) * P],
                                         psT[0][rows, :].rearrange("p (j n) -> p j n", j=4), ACT.Copy).then_inc(q_out, 1)
                act.wait_ge(turned, 2 * t + 2)
                nc.scalar.activation(kT[:, :, t * P:(t + 1) * P], psT[1][:].rearrange("p (j n) -> p j n", j=4),
                                     ACT.Copy).then_inc(k_out, 1)

            for t in range(NT):
                act.wait_ge(projected, t + 1)
                if t:
                    act.wait_ge(norm2_ready, t)
                nc.scalar.activation(sq[:].rearrange("p h d -> p (h d)"), psP[t % 2][:, 0:2 * BI], ACT.Square).then_inc(squared, 1)
                nc.scalar.activation(V[:, t, :], psP[t % 2][:, 2 * BI:3 * BI], ACT.Copy).then_inc(v_ready, 1)
                if t >= 2:
                    act.wait_ge(rot_step, 4 * (t - 1))
                nc.scalar.activation(two[:, t % 2, :], psP[t % 2][:, 0:2 * BI], ACT.Copy).then_inc(qk_ready, 1)
                act.wait_ge(norm2_ready, t + 1)
                nc.scalar.activation(nrm[t % 2][:], nrm[t % 2][:], ACT.Sqrt).then_inc(norm_ready, 1)
                if t >= 2:
                    outs(t - 2)
            outs(NT - 2)
            outs(NT - 1)

        @block.gpsimd
        def _(pool):
            nc.gpsimd.memset(qz[64:P, 0, :, :], 0.0).then_inc(q_zeroed, 1)
            pool.wait_ge(q_zeroed, 1)
            nc.gpsimd.memset(qz[0:64, 1, :, :], 0.0).then_inc(q_zeroed, 1)
            pool.wait_ge(q_zeroed, 2)
            pool.wait_ge(loaded, 16 * 7)
            for t in range(NT):
                b = t % 2
                pool.wait_ge(tab_loaded[b], 16 * (t // 2 + 1))
                nc.gpsimd.tensor_tensor(tab[b][:], tab[b][:], gain[:], ALU.mult).then_inc(tab_ready, 1)
                pool.wait_ge(tab_ready, t + 1)
                pool.wait_ge(norm_step, 3 * (t + 1))
                if t >= 2:
                    pool.wait_ge(turned, 2 * (t - 1))
                src = two[:, b, :].rearrange("p (a h d) -> p a h d", a=2, d=BD)
                dst = tmp[:, b, :].rearrange("p (a h d) -> p a h d", a=2, d=BD)
                nc.gpsimd.tensor_tensor(dst, src, tab[b][:, :, 0, :].unsqueeze(2).broadcast_to([P, 2, BH, BD]),
                                        ALU.mult).then_inc(same_ready, 1)

        @block.vector
        def _(dve):
            tt, ts = nc.vector.tensor_tensor, nc.vector.tensor_scalar

            def squares(t):
                dve.wait_ge(squared, t + 1)
                if t >= 2:
                    dve.wait_ge(norm_step, 3 * (t - 1))
                nc.vector.tensor_reduce(nrm[t % 2][:], sq[:], AX.X, ALU.add).then_inc(norm2_ready, 1)

            def normalise(t):
                n = nrm[t % 2]
                dve.wait_ge(norm_ready, t + 1)
                ts(n[:], n[:], 1e-12, None, ALU.max).then_inc(norm_step, 1)
                dve.wait_ge(norm_step, 3 * t + 1)
                nc.vector.reciprocal(n[:], n[:]).then_inc(norm_step, 1)
                dve.wait_ge(norm_step, 3 * t + 2)
                dve.wait_ge(qk_ready, t + 1)
                x = heads(two, t % 2)
                tt(x, x, n[:].unsqueeze(2).broadcast_to([P, 2 * BH, BD]), ALU.mult).then_inc(norm_step, 1)

            squares(0)
            normalise(0)
            squares(1)
            for t in range(NT):
                b = t % 2
                dve.wait_ge(norm_step, 3 * t + 3)
                if t:
                    dve.wait_ge(rot_step, 4 * t)
                dve.wait_ge(tab_ready, t + 1)
                for half in range(2):
                    lo, hi = half * BD // 2, (1 - half) * BD // 2
                    for i in range(2):
                        src = two[:, b, i * BI:(i + 1) * BI].rearrange("p (h d) -> p h d", d=BD)[:, :, hi:hi + BD // 2]
                        dst = swp[b][:, i * BI:(i + 1) * BI].rearrange("p (h d) -> p h d", d=BD)[:, :, lo:lo + BD // 2]
                        ins = tt(dst, src, tab[b][:, i, 1, lo:lo + BD // 2].unsqueeze(1).broadcast_to([P, BH, BD // 2]), ALU.mult)
                    ins.then_inc(rot_step, 1)
                if t + 1 < NT:
                    normalise(t + 1)
                dve.wait_ge(rot_step, 4 * t + 2)
                dve.wait_ge(same_ready, t + 1)
                for i in range(2):
                    cols = slice(i * BI, (i + 1) * BI)
                    tt(tmp[:, b, cols], tmp[:, b, cols], swp[b][:, cols], ALU.add).then_inc(rot_step, 1)
                if t + 2 < NT:
                    squares(t + 2)
    st.close()


def local_attention(nc, g, name, wo_dram, qz, kT, V, R):
    st = Stage(nc, name)
    KEYS = 2 * P - BW
    wo = st.sb("wo", [P, 4, P])
    mask = [st.sb(f"mask{i}", [P, 2, KEYS], BF16) for i in range(2)]
    nmx, den = [st.sb(f"nmx{i}", [P, 4]) for i in range(2)], [st.sb(f"den{i}", [P, BH]) for i in range(2)]
    raw = [st.sb(f"raw{i}", [P, 4]) for i in range(2)]
    prob = [g.CT[:, i * 2 * CH:(i + 1) * 2 * CH] for i in range(2)]
    gv = g.V[:].rearrange("p t d -> p (t d)")
    probT = [gv[:, i * 2 * CH:(i + 1) * 2 * CH] for i in range(2)]
    orow, oT = [st.sb(f"orow{i}", [P, BH, BD]) for i in range(2)], [st.sb(f"oT{i}", [P, BI]) for i in range(2)]
    psS = [st.ps(f"psS{i}", 2 * CH) for i in range(2)]
    psP = [st.ps(f"psP{i}") for i in range(2)]
    psO, psW = st.ps("psO"), st.ps("psW")
    loaded, built, scored, max_step, exped, p_turned, p_ready, pv_done, den_ready, o_ready, o_turned, oT_ready, w_done, added = [
        st.sem(n) for n in ("loaded", "built", "scored", "max_step", "exped", "p_turned", "p_ready", "pv_done", "den_ready",
                            "o_ready", "o_turned", "oT_ready", "w_done", "added")]
    padded = st.sem("padded")
    NU = 2 * NT

    def seen(x, heads):
        return x.rearrange("p (h k) -> p h k", h=heads)[:, :, BW:2 * P]

    with st.block() as block:
        @block.sync
        def _(sp):
            sp.dma_start(wo[:], wo_dram.rearrange("(j p) d -> p j d", p=P)).then_inc(loaded, 16)

        @block.gpsimd
        def _(pool):
            n = [0]
            for i in range(2):
                nc.gpsimd.memset(prob[i].rearrange("p (h k) -> p h k", h=4)[:, :, 0:BW], 0.0).then_inc(padded, 1)

            def chain(ins):
                ins.then_inc(built, 1)
                n[0] += 1
                pool.wait_ge(built, n[0])
            for i in range(2):
                chain(nc.gpsimd.memset(mask[i][:], 0.0))
                for h in range(2):
                    prev, cur = mask[i][:, h, 0:P - BW], mask[i][:, h, P - BW:KEYS]
                    if i == 0:
                        chain(nc.gpsimd.memset(prev, NEG))
                    else:
                        chain(nc.gpsimd.affine_select(out=prev, in_=prev, compare_op=ALU.is_ge, fill=NEG, base=0,
                                                      pattern=[[1, P - BW]], channel_multiplier=-1))
                    chain(nc.gpsimd.affine_select(out=cur, in_=cur, compare_op=ALU.is_ge, fill=NEG, base=0,
                                                  pattern=[[-1, P]], channel_multiplier=1))
                    chain(nc.gpsimd.affine_select(out=cur, in_=cur, compare_op=ALU.is_ge, fill=NEG, base=BW,
                                                  pattern=[[1, P]], channel_multiplier=-1))

        def kb_range(t):
            return (0, 1) if t else (1,)

        @block.tensor
        def _(pe):
            mm = nc.tensor.matmul

            def score(n):
                t, half, ps = n // 2, n % 2, psS[n % 2]
                if n >= 2:
                    pe.wait_ge(exped, 4 * (n - 1))
                for j in range(2):
                    mm(seen(ps[:, j * CH:(j + 1) * CH], 2), g.identb[:], mask[min(t, 1)][:],
                       start=True, stop=False, skip_group_check=True)
                    for i in range(2):
                        h = 4 * half + 2 * j + i
                        lo = BW if t else P
                        ins = mm(ps[:, (2 * j + i) * 2 * P + lo:(2 * j + i + 1) * 2 * P], qz[:, h % 2, h // 2, t * P:(t + 1) * P],
                                 kT[:, h // 2, (t - 1) * P + lo:(t + 1) * P], start=False, stop=True, skip_group_check=True)
                ins.then_inc(scored, 1)

            def turn_p(n):
                t = n // 2
                pe.wait_ge(exped, 4 * (n + 1))
                for j in range(2):
                    if n:
                        pe.wait_ge(p_ready, 2 * n + j - 1)
                    for i in range(2):
                        for kb in range(2):
                            at = ((2 * j + i) * 2 + kb) * P
                            ins = nc.tensor.transpose(psP[j][:, (2 * i + kb) * P:(2 * i + kb + 1) * P], prob[n % 2][:, at:at + P], g.ident[:])
                    ins.then_inc(p_turned, 1)

            def pv(n):
                t, half = n // 2, n % 2
                if half == 0 and t:
                    pe.wait_ge(o_ready, t)
                pe.wait_ge(p_ready, 2 * (n + 1))
                for i in range(4):
                    h = 4 * half + i
                    kbs = kb_range(t)
                    for kb in kbs:
                        ins = mm(psO[:, h * BD:(h + 1) * BD], probT[n % 2][:, (2 * i + kb) * P:(2 * i + kb + 1) * P],
                                 V[:, t - 1 + kb, h * BD:(h + 1) * BD], start=kb == kbs[0], stop=kb == 1, skip_group_check=True)
                ins.then_inc(pv_done, 1)

            def turn_o(t):
                pe.wait_ge(o_ready, t + 1)
                if t:
                    pe.wait_ge(added, t)
                for j in range(4):
                    ins = nc.tensor.transpose(psW[:, j * P:(j + 1) * P],
                                              orow[t % 2][:, 2 * j:2 * j + 2, :].rearrange("p h d -> p (h d)"), g.ident[:])
                ins.then_inc(o_turned, 1)

            def project(t):
                pe.wait_ge(oT_ready, t + 1)
                for j in range(4):
                    ins = mm(psW[:, 0:P], oT[t % 2][:, j * P:(j + 1) * P], wo[:, j, :], start=j == 0, stop=j == 3)
                ins.then_inc(w_done, 1)

            pe.wait_ge(built, 14)
            pe.wait_ge(padded, 2)
            pe.wait_ge(loaded, 16)
            score(0)
            for n in range(NU):
                t, half = n // 2, n % 2
                if n + 1 < NU:
                    score(n + 1)
                if n:
                    pv(n - 1)
                if half == 1 and t:
                    turn_o(t - 1)
                turn_p(n)
                if half == 0 and t >= 2:
                    project(t - 2)
            pv(NU - 1)
            project(NT - 2)
            turn_o(NT - 1)
            project(NT - 1)

        @block.scalar
        def _(act):
            def o_out(t):
                act.wait_ge(o_turned, t + 1)
                if t >= 2:
                    act.wait_ge(w_done, t - 1)
                nc.scalar.activation(oT[t % 2][:], psW[:], ACT.Copy).then_inc(oT_ready, 1)

            for n in range(NU):
                t, half = n // 2, n % 2
                act.wait_ge(max_step, 2 * (n + 1))
                if n >= 2:
                    act.wait_ge(p_turned, 2 * (n - 1))
                if half == 0 and t >= 2:
                    act.wait_ge(o_ready, t - 1)
                for i in range(4):
                    h = 4 * half + i
                    cols = slice(i * 2 * P + BW, (i + 1) * 2 * P)
                    nc.scalar.activation(prob[n % 2][:, cols], psS[n % 2][:, cols],
                                         ACT.Exp, scale=MAGNIFY, bias=nmx[n % 2][:, i:i + 1],
                                         accum_out=den[t % 2][:, h:h + 1]).then_inc(exped, 1)
                if half == 0 and t >= 2:
                    o_out(t - 2)
            o_out(NT - 2)
            o_out(NT - 1)

        @block.vector
        def _(dve):
            def maxima(n):
                b = n % 2
                dve.wait_ge(scored, n + 1)
                if n >= 2:
                    dve.wait_ge(exped, 4 * (n - 1))
                nc.vector.tensor_reduce(raw[b][:], seen(psS[b][:], 4), AX.X, ALU.max).then_inc(max_step, 1)
                dve.wait_ge(max_step, 2 * n + 1)
                nc.vector.tensor_scalar(nmx[b][:], raw[b][:], -MAGNIFY, None, ALU.mult).then_inc(max_step, 1)

            def add_row(t):
                dve.wait_ge(w_done, t + 1)
                nc.vector.tensor_tensor(R[:, t, :], R[:, t, :], psW[:, 0:P], ALU.add).then_inc(added, 1)

            def divide(t):
                d = den[t % 2]
                dve.wait_ge(exped, 8 * (t + 1))
                nc.vector.reciprocal(d[:], d[:]).then_inc(den_ready, 1)
                dve.wait_ge(den_ready, t + 1)
                dve.wait_ge(pv_done, 2 * (t + 1))
                if t >= 2:
                    dve.wait_ge(o_turned, t - 1)
                nc.vector.tensor_tensor(orow[t % 2][:], psO[:].rearrange("p (h d) -> p h d", h=BH),
                                        d[:].unsqueeze(2).broadcast_to([P, BH, BD]), ALU.mult).then_inc(o_ready, 1)

            maxima(0)
            for n in range(NU):
                t, half = n // 2, n % 2
                if n + 1 < NU:
                    maxima(n + 1)
                if half == 0 and t:
                    divide(t - 1)
                for j in range(2):
                    dve.wait_ge(p_turned, 2 * n + j + 1)
                    if n >= 2:
                        dve.wait_ge(pv_done, n - 1)
                    nc.vector.tensor_copy(probT[n % 2][:, j * CH:(j + 1) * CH], psP[j][:]).then_inc(p_ready, 1)
                if half == 0 and t >= 2:
                    add_row(t - 2)
            divide(NT - 1)
            add_row(NT - 2)
            add_row(NT - 1)
    st.close()


def local_ffn(nc, g, name, w1_dram, b1_dram, w2_dram, b2_dram, R):
    st = Stage(nc, name)
    w1, w2 = st.sb("w1", [P, 2 * FH]), st.sb("w2", [P, 3, P])
    b1, b2 = st.sb("b1", [P, 2, 3]), st.sb("b2", [P, P])
    gl = [st.sb(f"gl{i}", [P, CH]) for i in range(2)]
    h = [st.sb(f"h{i}", [P, 3, CH]) for i in range(2)]
    psA = [st.ps(f"psA{i}") for i in range(2)]
    psG = [st.ps(f"psG{i}") for i in range(2)]
    psO = [st.ps(f"psO{i}") for i in range(2)]
    loaded, in_done, gelu_ready, h_ready, out_done, added = [st.sem(n) for n in (
        "loaded", "in_done", "gelu_ready", "h_ready", "out_done", "added")]
    units = [(c, k) for c in range(NC) for k in range(3)]
    with st.block() as block:
        @block.sync
        def _(sp):
            loads = [(w1[:], w1_dram), (b2[:], bcast_row(b2_dram))]
            for k, (lo, m) in enumerate(F_CHUNKS):
                loads.append((w2[0:m, k, :], w2_dram[lo:lo + m, :]))
                for i in range(2):
                    loads.append((b1[0:m, i, k:k + 1], col(b1_dram[i * FH + lo:i * FH + lo + m])))
            for d, s in loads:
                sp.dma_start(d, s).then_inc(loaded, 16)

        @block.tensor
        def _(pe):
            def inputs(n):
                c, k = units[n]
                lo, m = F_CHUNKS[k]
                if n >= 2:
                    pe.wait_ge(h_ready, n - 1)
                for i, ps in enumerate((psA, psG)):
                    ins = nc.tensor.matmul(ps[n % 2][0:m, :], w1[:, i * FH + lo:i * FH + lo + m], g.XnT[:, c * CH:(c + 1) * CH],
                                           start=True, stop=True)
                ins.then_inc(in_done, 1)

            def down(c):
                pe.wait_ge(h_ready, 3 * (c + 1))
                if c >= 2:
                    pe.wait_ge(added, c)
                for t in range(4):
                    for k, (lo, m) in enumerate(F_CHUNKS):
                        ins = nc.tensor.matmul(psO[c % 2][:, t * P:(t + 1) * P], h[c % 2][0:m, k, t * P:(t + 1) * P], w2[0:m, k, :],
                                               start=k == 0, stop=k == 2, skip_group_check=True)
                ins.then_inc(out_done, 1)

            pe.wait_ge(loaded, 16 * 11)
            for c in range(NC):
                for k in range(3):
                    inputs(3 * c + k)
                    if k == 1 and c:
                        down(c - 1)
            down(NC - 1)

        @block.scalar
        def _(act):
            act.wait_ge(loaded, 16 * 11)
            for n, (c, k) in enumerate(units):
                lo, m = F_CHUNKS[k]
                act.wait_ge(in_done, n + 1)
                if n >= 2:
                    act.wait_ge(h_ready, n - 1)
                nc.scalar.activation(gl[n % 2][0:m, :], psG[n % 2][0:m, :], ACT.Gelu, bias=b1[0:m, 1, k:k + 1]).then_inc(gelu_ready, 1)

        @block.vector
        def _(dve):
            dve.wait_ge(loaded, 16 * 11)
            nc.vector.tensor_tensor(R[:], R[:], b2[:].unsqueeze(1).broadcast_to([P, NT, P]), ALU.add).then_inc(added, 1)

            def add_rows(c):
                dve.wait_ge(out_done, c + 1)
                dve.wait_ge(added, c + 1)
                x = R[:, 4 * c:4 * c + 4, :].rearrange("p t d -> p (t d)")
                nc.vector.tensor_tensor(x, x, psO[c % 2][:], ALU.add).then_inc(added, 1)

            for n, (c, k) in enumerate(units):
                lo, m = F_CHUNKS[k]
                dve.wait_ge(gelu_ready, n + 1)
                if c >= 2:
                    dve.wait_ge(out_done, c - 1)
                nc.vector.scalar_tensor_tensor(out=h[c % 2][0:m, k, :], in0=psA[n % 2][0:m, :], scalar=b1[0:m, 0, k:k + 1],
                                               in1=gl[n % 2][0:m, :], op0=ALU.add, op1=ALU.mult).then_inc(h_ready, 1)
                if k == 2 and c:
                    add_rows(c - 1)
            add_rows(NC - 1)
    st.close()


def l2_ffn(nc, g, a):
    big = Stage(nc, "l2f")
    R = big.sb("R", [P, NT, P])
    layernorm_transpose(nc, g, "l2f_ln", keep_rows=R)
    for l in range(2):
        n = f"l2f{l}_"
        sh = Stage(nc, n + "sh")
        Hs = sh.sb("Hs", [P, NT, P])
        shift_rows(nc, g, n + "shift", R, Hs)
        layernorm_transpose(nc, g, n + "turn", normalise=False, src=Hs)
        sh.close()
        att = Stage(nc, n + "att")
        qz, kT, V = att.sb("qz", [P, 2, 4, S]), att.sb("kT", [P, 4, S]), att.sb("V", [P, NT, BI])
        local_qkv(nc, g, n + "qkv", a["L2_ffn_wqkv"][l], a["L2_ffn_q_scale"][l], a["L2_ffn_k_scale"][l], a["rotary"], qz, kT, V)
        local_attention(nc, g, n + "core", a["L2_ffn_wo"][l], qz, kT, V, R)
        att.close()
        sh = Stage(nc, n + "sh2")
        Hs = sh.sb("Hs", [P, NT, P])
        shift_rows(nc, g, n + "shift2", R, Hs)
        layernorm_transpose(nc, g, n + "norm", src=Hs, affine=(col(a["L2_ffn_ln_g"][l]), col(a["L2_ffn_ln_b"][l])))
        sh.close()
        local_ffn(nc, g, n + "ffn", a["L2_ffn_w1"][l], a["L2_ffn_b1"][l], a["L2_ffn_w2"][l], a["L2_ffn_b2"][l], R)
    added = big.sem("added")
    with big.block() as block:
        @block.vector
        def _(dve):
            nc.vector.tensor_tensor(g.X[:], g.X[:], R[:], ALU.add).then_inc(added, 1)
    big.close()


class Shared:
    pass


def build(nc, a, out, stages):
    g = Shared()
    ctx = ExitStack()
    g.out_stored = nc.alloc_semaphore(name="out_stored")

    def sb(name, shape, dt=F32):
        return ctx.enter_context(nc.sbuf_tensor(name, shape, dt))

    g.X = sb("X", [P, NT, P])
    g.XnT = sb("XnT", [P, S])
    g.V = sb("V", [P, NT, P])
    g.CT = sb("CT", [P, S])
    g.ident, g.identb, g.ones, g.blockdiag = sb("ident", [P, P]), sb("identb", [P, P], BF16), sb("ones", [P, P]), sb("blockdiag", [P, P])
    g.W, g.WT = sb("W", [P, NT, 16]), sb("WT", [16, S])
    g.spread = sb("spread", [P, P // H, P])
    g.cur_q, g.cur_k = sb("cur_q", [P, P], BF16), sb("cur_k", [P, P], BF16)
    g.prev_q, g.prev_k = sb("prev_q", [P, P], BF16), sb("prev_k", [P, P], BF16)
    g.caus_q, g.caus_k = sb("caus_q", [P, P], BF16), sb("caus_k", [P, P], BF16)
    g.qparts = nc.dram_tensor("qparts", [3, P, S], BF16, kind="Internal").ap()
    g.kparts = nc.dram_tensor("kparts", [3, P, S], BF16, kind="Internal").ap()
    g.o_dram = nc.dram_tensor("o_dram", [P, S], F32, kind="Internal").ap()
    g.den_dram = nc.dram_tensor("den_dram", [H, S], F32, kind="Internal").ap()
    build_constants(nc, g)
    load_tokens(nc, g, a["L0_attn_x"])
    for s in stages:
        STAGES[s](nc, g, a)
    store_tokens(nc, g, out)
    ctx.close()


STAGES = {"L0A": l0_attn, "L1A": l1_attn, "L2A": l2_attn, "L1F": l1_ffn, "L3F": l3_ffn, "L0F": l0_ffn, "L3A": l3_attn, "L2F": l2_ffn}


def kernel(**inputs):
    import numpy as _np
    import concourse.bacc as _bacc
    from concourse import mybir as _mybir
    from concourse.bass_utils import run_bass_kernel_spmd as _run

    nc = _bacc.Bacc("TRN2", target_bir_lowering=False, num_devices=1)
    arrays, aps = {}, {}
    for name, v in list(inputs.items()) + [("rotary", rotary_tables())]:
        v = _np.asarray(v)
        if name in TRANSPOSED:
            name, v = name + "T", v.T
        v = _np.ascontiguousarray(v)
        arrays[f"in_{name}"] = v
        aps[name] = nc.dram_tensor(f"in_{name}", v.shape, _mybir.dt.from_np(v.dtype), kind="ExternalInput").ap()
    out = nc.dram_tensor("out_0", (1, S, P), _mybir.dt.float32, kind="ExternalOutput").ap()
    build(nc, aps, out, RUN)
    r = _run(nc, [arrays], core_ids=[0])
    return r.results[0]["out_0"]


TRANSPOSED = ("L1_attn_Wq", "L1_attn_Wk", "L1_attn_Wv", "L2_attn_Wq", "L2_attn_Wk", "L2_attn_Wv", "L2_attn_Wo",
              "L3_attn_in_proj_w", "L3_attn_out_proj_w")
RUN = ["L0A", "L0F", "L1A", "L1F", "L2A", "L2F", "L3A", "L3F"]
```
